# Optimizing a Trainium2 kernel written in Bass

```python
import numpy as np
import jax
import jax.numpy as jnp

def _softmax(x, axis=-1):
    return jax.nn.softmax(x, axis=axis)

def _gelu(x):
    return jax.nn.gelu(x, approximate=True)

def _silu(x):
    return jax.nn.silu(x)

def _sigmoid(x):
    return jax.nn.sigmoid(x)

def _layernorm(x, axis=-1, eps=1e-05):
    m = jnp.mean(x, axis=axis, keepdims=True)
    v = jnp.var(x, axis=axis, keepdims=True)
    return (x - m) / jnp.sqrt(v + eps)

def _scatter_add(tgt, idx, src, axis=0):
    return tgt.at[idx].add(src)

def _segment_sum(src, seg, n):
    return jax.ops.segment_sum(src, seg, n)
kernel_name = 'mk_seq_postln_d1_jaxref_r8_450ac1'

def setup_inputs(seed: int=0):
    np.random.seed(seed)
    _w = jnp.asarray

    def _L0_attn_setup():
        import jax, jax.numpy as jnp
        import numpy as np
        B, T, HID = (1, 128, 256)
        H, DK, DV, M, KW = (16, 128, 128, 128, 4)
        SCALE = DK ** (-0.5)
        EPS = 1e-05

        def short_conv(x, w):
            K = w.shape[1]
            xp = jnp.pad(x, ((0, 0), (K - 1, 0), (0, 0)))
            t = x.shape[1]
            y = sum((xp[:, i:i + t] * w[:, i] for i in range(K)))
            return jax.nn.silu(y)

        def l2norm(x):
            return x * jax.lax.rsqrt(jnp.sum(x * x, axis=-1, keepdims=True) + 1e-06)

        def gsa2_scan(q, k, v, w, g, beta):
            b = q.shape[0]
            tm = lambda x: jnp.moveaxis(x, 1, 0)
            Sk0 = jnp.zeros((b, H, DK, M), q.dtype)
            Sv0 = jnp.zeros((b, H, M, DV), q.dtype)

            def step(carry, xs):
                Sk, Sv = carry
                q_t, k_t, v_t, w_t, g_t, b_t = xs
                gt = jnp.exp(g_t)
                bw = b_t[:, :, None] * w_t
                Sk = Sk * gt[:, :, None, :] + k_t[..., :, None] * bw[:, :, None, :]
                Sv = Sv * gt[..., None] + bw[..., None] * v_t[:, :, None, :]
                s = jnp.einsum('bhd,bhdm->bhm', q_t, Sk) * SCALE
                a = jax.nn.softmax(s, axis=-1)
                o_t = jnp.einsum('bhm,bhmd->bhd', a, Sv)
                return ((Sk, Sv), o_t)
            (_, _), o = jax.lax.scan(step, (Sk0, Sv0), (tm(q), tm(k), tm(v), tm(w), tm(g), tm(beta)))
            return jnp.moveaxis(o, 0, 1)
        key = jax.random.key(seed)
        ks = jax.random.split(key, 16)
        s = 0.02
        return {'hidden_states': jax.random.normal(ks[0], (B, T, HID), jnp.float32), 'Wq': jax.random.normal(ks[1], (HID, H * DK), jnp.float32) * s, 'Wk': jax.random.normal(ks[2], (HID, H * DK), jnp.float32) * s, 'Wv': jax.random.normal(ks[3], (HID, H * DV), jnp.float32) * s, 'Ww': jax.random.normal(ks[4], (HID, H * M), jnp.float32) * s, 'cq': jax.random.normal(ks[5], (H * DK, KW), jnp.float32) * 0.2, 'ck': jax.random.normal(ks[6], (H * DK, KW), jnp.float32) * 0.2, 'cv': jax.random.normal(ks[7], (H * DV, KW), jnp.float32) * 0.2, 'Wf1': jax.random.normal(ks[8], (HID, DV), jnp.float32) * s, 'Wf2': jax.random.normal(ks[9], (DV, H * M), jnp.float32) * s, 'Wb': jax.random.normal(ks[10], (HID, H), jnp.float32) * s, 'Wg1': jax.random.normal(ks[11], (HID, DV), jnp.float32) * s, 'Wg2': jax.random.normal(ks[12], (DV, H * DV), jnp.float32) * s, 'bg2': jnp.zeros((H * DV,), jnp.float32), 'norm_w': jnp.ones((DV,), jnp.float32), 'Wo': jax.random.normal(ks[13], (H * DV, HID), jnp.float32) * s}
    _L0_attn_in = _L0_attn_setup()

    def _L0_ffn_setup():
        import jax, jax.numpy as jnp
        import numpy as np
        HIDDEN = 256
        INTER = 1024
        B, S = (4, 128)

        def _qmatmul(x, w_int8, scale):
            y = jnp.einsum('bsh,ho->bso', x, w_int8.astype(x.dtype))
            return y * scale
        key = jax.random.key(seed)
        ks = jax.random.split(key, 7)
        x = jax.random.normal(ks[0], (B, S, HIDDEN), dtype=jnp.float32)
        w_gate = jax.random.randint(ks[1], (HIDDEN, INTER), -128, 128, dtype=jnp.int32).astype(jnp.int8)
        w_up = jax.random.randint(ks[2], (HIDDEN, INTER), -128, 128, dtype=jnp.int32).astype(jnp.int8)
        w_down = jax.random.randint(ks[3], (INTER, HIDDEN), -128, 128, dtype=jnp.int32).astype(jnp.int8)
        s_gate = jax.random.uniform(ks[4], (INTER,), dtype=jnp.float32) * 0.02 + 0.001
        s_up = jax.random.uniform(ks[5], (INTER,), dtype=jnp.float32) * 0.02 + 0.001
        s_down = jax.random.uniform(ks[6], (HIDDEN,), dtype=jnp.float32) * 0.02 + 0.001
        return {'x': x, 'w_gate': w_gate, 'w_up': w_up, 'w_down': w_down, 's_gate': s_gate, 's_up': s_up, 's_down': s_down}
    _L0_ffn_in = _L0_ffn_setup()
    _d = {'L0_attn_hidden_states': _L0_attn_in['hidden_states'], 'L0_attn_Wq': _L0_attn_in['Wq'], 'L0_attn_Wk': _L0_attn_in['Wk'], 'L0_attn_Wv': _L0_attn_in['Wv'], 'L0_attn_Ww': _L0_attn_in['Ww'], 'L0_attn_cq': _L0_attn_in['cq'], 'L0_attn_ck': _L0_attn_in['ck'], 'L0_attn_cv': _L0_attn_in['cv'], 'L0_attn_Wf1': _L0_attn_in['Wf1'], 'L0_attn_Wf2': _L0_attn_in['Wf2'], 'L0_attn_Wb': _L0_attn_in['Wb'], 'L0_attn_Wg1': _L0_attn_in['Wg1'], 'L0_attn_Wg2': _L0_attn_in['Wg2'], 'L0_attn_bg2': _L0_attn_in['bg2'], 'L0_attn_norm_w': _L0_attn_in['norm_w'], 'L0_attn_Wo': _L0_attn_in['Wo'], 'L0_ffn_w_gate': _L0_ffn_in['w_gate'], 'L0_ffn_w_up': _L0_ffn_in['w_up'], 'L0_ffn_w_down': _L0_ffn_in['w_down'], 'L0_ffn_s_gate': _L0_ffn_in['s_gate'], 'L0_ffn_s_up': _L0_ffn_in['s_up'], 'L0_ffn_s_down': _L0_ffn_in['s_down']}
    _x0 = _d['L0_attn_hidden_states']
    _d['L0_attn_hidden_states'] = jax.random.normal(jax.random.fold_in(jax.random.key(seed), 1), (4, 512, 256), dtype=_x0.dtype)
    del _x0
    return _d

def reference(L0_attn_hidden_states, L0_attn_Wq, L0_attn_Wk, L0_attn_Wv, L0_attn_Ww, L0_attn_cq, L0_attn_ck, L0_attn_cv, L0_attn_Wf1, L0_attn_Wf2, L0_attn_Wb, L0_attn_Wg1, L0_attn_Wg2, L0_attn_bg2, L0_attn_norm_w, L0_attn_Wo, L0_ffn_w_gate, L0_ffn_w_up, L0_ffn_w_down, L0_ffn_s_gate, L0_ffn_s_up, L0_ffn_s_down):

    def _L0_attn_ref(hidden_states, Wq, Wk, Wv, Ww, cq, ck, cv, Wf1, Wf2, Wb, Wg1, Wg2, bg2, norm_w, Wo):
        import jax, jax.numpy as jnp
        import numpy as np
        B, T, HID = (1, 128, 256)
        H, DK, DV, M, KW = (16, 128, 128, 128, 4)
        SCALE = DK ** (-0.5)
        EPS = 1e-05

        def short_conv(x, w):
            K = w.shape[1]
            xp = jnp.pad(x, ((0, 0), (K - 1, 0), (0, 0)))
            t = x.shape[1]
            y = sum((xp[:, i:i + t] * w[:, i] for i in range(K)))
            return jax.nn.silu(y)

        def l2norm(x):
            return x * jax.lax.rsqrt(jnp.sum(x * x, axis=-1, keepdims=True) + 1e-06)

        def gsa2_scan(q, k, v, w, g, beta):
            b = q.shape[0]
            tm = lambda x: jnp.moveaxis(x, 1, 0)
            Sk0 = jnp.zeros((b, H, DK, M), q.dtype)
            Sv0 = jnp.zeros((b, H, M, DV), q.dtype)

            def step(carry, xs):
                Sk, Sv = carry
                q_t, k_t, v_t, w_t, g_t, b_t = xs
                gt = jnp.exp(g_t)
                bw = b_t[:, :, None] * w_t
                Sk = Sk * gt[:, :, None, :] + k_t[..., :, None] * bw[:, :, None, :]
                Sv = Sv * gt[..., None] + bw[..., None] * v_t[:, :, None, :]
                s = jnp.einsum('bhd,bhdm->bhm', q_t, Sk) * SCALE
                a = jax.nn.softmax(s, axis=-1)
                o_t = jnp.einsum('bhm,bhmd->bhd', a, Sv)
                return ((Sk, Sv), o_t)
            (_, _), o = jax.lax.scan(step, (Sk0, Sv0), (tm(q), tm(k), tm(v), tm(w), tm(g), tm(beta)))
            return jnp.moveaxis(o, 0, 1)
        h = hidden_states
        q = short_conv(h @ Wq, cq)
        k = short_conv(h @ Wk, ck)
        v = short_conv(h @ Wv, cv)
        w = short_conv(h @ Ww, cv)
        g = jax.nn.log_sigmoid(h @ Wf1 @ Wf2)
        beta = jax.nn.sigmoid(h @ Wb)
        rs = lambda x, d: x.reshape(x.shape[0], x.shape[1], -1, d)
        q, k = (rs(q, DK), rs(k, DK))
        v = rs(v, DV)
        w = l2norm(rs(w, M))
        g = rs(g, M)
        o = gsa2_scan(q, k, v, w, g, beta)
        gate = rs(h @ Wg1 @ Wg2 + bg2, DV)
        o = o * jax.lax.rsqrt(jnp.mean(o * o, axis=-1, keepdims=True) + EPS)
        o = o * norm_w * jax.nn.sigmoid(gate)
        o = o.reshape(o.shape[0], o.shape[1], -1)
        return o @ Wo

    def _L0_ffn_ref(x, w_gate, w_up, w_down, s_gate, s_up, s_down):
        import jax, jax.numpy as jnp
        import numpy as np
        HIDDEN = 256
        INTER = 1024
        B, S = (4, 128)

        def _qmatmul(x, w_int8, scale):
            y = jnp.einsum('bsh,ho->bso', x, w_int8.astype(x.dtype))
            return y * scale
        gate = jax.nn.silu(_qmatmul(x, w_gate, s_gate))
        up = _qmatmul(x, w_up, s_up)
        fuse = gate * up
        return _qmatmul(fuse, w_down, s_down)
    x = L0_attn_hidden_states
    x = _layernorm(x + _L0_attn_ref(x, L0_attn_Wq, L0_attn_Wk, L0_attn_Wv, L0_attn_Ww, L0_attn_cq, L0_attn_ck, L0_attn_cv, L0_attn_Wf1, L0_attn_Wf2, L0_attn_Wb, L0_attn_Wg1, L0_attn_Wg2, L0_attn_bg2, L0_attn_norm_w, L0_attn_Wo), axis=-1)
    x = _layernorm(x + _L0_ffn_ref(x, L0_ffn_w_gate, L0_ffn_w_up, L0_ffn_w_down, L0_ffn_s_gate, L0_ffn_s_up, L0_ffn_s_down), axis=-1)
    return x

_drawn_inputs = setup_inputs


def setup_inputs(seed=0):
    import zlib

    import numpy as np

    out = dict(_drawn_inputs(seed))
    spreads = {'L0_attn_bg2': (0.0, 0.8), 'L0_attn_norm_w': (1.0, 0.6)}
    factors = {'L0_attn_Wq': 8.0,
     'L0_attn_Wk': 8.0,
     'L0_attn_cq': 8.0,
     'L0_attn_ck': 8.0,
     'L0_attn_Wf1': 8.0,
     'L0_attn_Wf2': 8.0,
     'L0_attn_Wb': 5.134,
     'L0_attn_Wg1': 8.0,
     'L0_attn_Wg2': 8.0}
    for name, (base, spread) in spreads.items():
        noise = np.random.default_rng([zlib.crc32(name.encode()), seed]).standard_normal(out[name].shape)
        drawn = base * np.exp(spread * noise) if base else spread * noise
        out[name] = jnp.asarray(drawn.astype(out[name].dtype))
    for name, factor in factors.items():
        out[name] = (out[name] * factor).astype(out[name].dtype)
    return out
```

```python
from contextlib import ExitStack

import concourse.bass as bass
from concourse import mybir

F32 = mybir.dt.float32
I8 = mybir.dt.int8
I32 = mybir.dt.int32
U32 = mybir.dt.uint32
ALU = mybir.AluOpType
ACT = mybir.ActivationFunctionType
AX_X = mybir.AxisListType.X

P = 128
LEVELS = 9
IN_CHUNK = 7
NORM_EPS = 1e-6
RMS_EPS = 1e-5
LN_EPS = 1e-5


class Unit:

    def __init__(self, head, off):
        self.head, self.off = head, off
        self.par = off % 4
        self.h = off // 4 if head is None else head + off // 4

    def count(self, per, k):
        if self.head is None:
            return per * self.off + k
        return self.head * (4 * per) + (per * self.off + k)


class Slot:

    def __init__(self, head, off, units):
        def unit(lag):
            if head is None and not 0 <= off - lag < units:
                return None
            return Unit(head, off - lag)

        self.u1, self.u2, self.u3, self.u4 = (unit(lag) for lag in range(4))
        self.edge = head is None
        self.n = off
        self.j = off % 4


def slots(eng, heads, seqs):
    units = heads * seqs
    for n in range(seqs):
        yield Slot(None, n, units)
    with eng.Fori(1, heads) as h:
        for j in range(seqs):
            yield Slot(h, j, units)
    for n in range(units, units + 3):
        yield Slot(None, n, units)


def wait(eng, sem, value):
    if not isinstance(value, int) or value > 0:
        eng.wait_ge(sem, value)


def build(nc, x, Wq, Wk, Wv, Ww, cq, ck, cv, Wf1, Wf2, Wb, Wg1, Wg2, bg2, norm_w, Wo,
          w_gate, w_up, w_down, s_gate, s_up, s_down, out):
    B, T, HID = x.shape
    KW = cq.shape[1]
    H = Wb.shape[1]
    D = norm_w.shape[0]
    INTER = s_gate.shape[0]
    KT = HID // P
    C = T // P
    NT = B * T // P
    FT = INTER // P
    SCALE = float(D) ** -0.5
    assert D == P and B == 4 and C == 4 and T == 2 << (LEVELS - 1) and KT == 2 and KW == 4

    with ExitStack() as ctx:
        def sb(name, shape, dt=F32):
            return ctx.enter_context(nc.sbuf_tensor(name, shape, dt))

        def sem(name):
            return ctx.enter_context(nc.semaphore(name))

        proj_ps = ctx.enter_context(nc.psum_tensor("proj_ps", [P, 2, T], F32))
        tr_ps = ctx.enter_context(nc.psum_tensor("tr_ps", [P, T], F32))
        out_ps = ctx.enter_context(nc.psum_tensor("out_ps", [P, T], F32))
        mix_ps = ctx.enter_context(nc.psum_tensor("mix_ps", [P, 2, T], F32))
        work_ps = ctx.enter_context(nc.psum_tensor("work_ps", [P, 2, T], F32))

        acc = sb("acc", [P, NT, HID])
        hT = sb("hT", [P, KT, B * T])
        f1T = sb("f1T", [P, B * T])
        g1T = sb("g1T", [P, B * T])
        wo_sb = sb("wo_sb", [P, H, HID])
        beta = sb("beta", [P, NT, H])
        coefs = sb("coefs", [P, 3, H, KW])
        bg2_sb = sb("bg2_sb", [P, H])
        ident = sb("ident", [P, P])
        masks = sb("masks", [P, IN_CHUNK, P // 2])
        consts = sb("consts", [P, 4, C])
        w_head = sb("w_head", [P, 4, KT, P])
        wf2_head = sb("wf2_head", [P, P])
        wg2_head = sb("wg2_head", [P, P])
        coef = sb("coef", [P, 3, KW])
        gbias = sb("gbias", [P, 1])
        wT = sb("wT", [P, 4, T])
        vN = sb("vN", [P, 4, T])
        gT = sb("gT", [P, 4, T])
        tot = sb("tot", [P, 4, T])
        qk = sb("qk", [P, 2, 2, T])
        wN = sb("wN", [P, 2, T])
        fac = sb("fac", [P, 4, C])
        ssq = sb("ssq", [P, 2, C])
        conv = sb("conv", [P, 2, T])
        th = sb("th", [P, 2, T])
        fexp = sb("fexp", [P, T])
        U = sb("U", [P, 2, LEVELS - 1, T])
        A = sb("A", [P, C, T])
        A_lev = sb("A_lev", [P, IN_CHUNK, C, P // 2])
        A_diag = sb("A_diag", [P, C, P])
        UT = sb("UT", [P, 2, T])
        V = sb("V", [P, T])
        sT = sb("sT", [P, T])
        mx = sb("mx", [P, 2, C])
        aN = sb("aN", [P, T])
        aT = sb("aT", [P, T])
        Z = sb("Z", [P, 4, C])
        W = sb("W", [P, T])
        A2 = sb("A2", [P, C, T])
        oN = sb("oN", [P, T])
        ssqo = sb("ssqo", [P, 2, C])
        rms = sb("rms", [P, 2, C])
        tg = sb("tg", [P, T])
        ogT = sb("ogT", [P, T])

        Uflat = U[:, :, :, :].rearrange("p a l t -> p (a l t)")
        setup_w = Uflat[:, 0:2 * KT * P].rearrange("p (i k n) -> p i k n", i=2, k=KT)
        wb_sb = Uflat[:, 2 * KT * P:2 * KT * P + KT * H].rearrange("p (k n) -> p k n", k=KT)

        names = ("x_in w_in wo_in small_in head_w head_f head_g head_q head_k head_v const_ready mask_ready xT_ps xT_sb "
                 "first_ps first_sb wo_scaled coef_set gbias_set "
                 "proj_ps_ready gate_ps_ready wT_ps_ready vT_ps_ready A_ps_ready UT_ps_ready out_ps_ready s_ps_ready "
                 "aT_ps_ready mix_ps_ready o_ps_ready onT_ps_ready y_ps_ready "
                 "conv_step silu_done decay_step U_step V_step max_step mix_done vN_done og_done acc_done "
                 "tap_done tanh_done fexp_done wN_step A_done UT_done a_done aT_done oN_done osq_done on_done tg_done "
                 "fac_step Alev_done sT_done W_step rms_step").split()
        S = {n: sem(n) for n in names}
        (x_in, w_in, wo_in, small_in, head_w, head_f, head_g, head_q, head_k, head_v, const_ready, mask_ready, xT_ps,
         xT_sb, first_ps, first_sb, wo_scaled, coef_set, gbias_set,
         proj_ps_ready, gate_ps_ready, wT_ps_ready, vT_ps_ready, A_ps_ready, UT_ps_ready, out_ps_ready, s_ps_ready,
         aT_ps_ready, mix_ps_ready, o_ps_ready, onT_ps_ready, y_ps_ready,
         conv_step, silu_done, decay_step, U_step, V_step, max_step, mix_done, vN_done, og_done, acc_done,
         tap_done, tanh_done, fexp_done, wN_step, A_done, UT_done, a_done, aT_done, oN_done, osq_done, on_done, tg_done,
         fac_step, Alev_done, sT_done, W_step, rms_step) = (S[n] for n in names)
        ffn = {n: sem("ffn_" + n) for n in (
            "q_in scale_in cast scales stats var_eps rstd norm yT_ps yT_sb up_ps tanh mid fused down_ps scaled res stats2 "
            "var_eps2 rstd2 done store").split()}

        def pairs(ap, lev):
            return ap.rearrange("p (n e l) -> p n e l", e=2, l=1 << lev)

        def block_tot(par, lev, odd):
            if lev == 0:
                t = gT[:, par, :]
                n = T
            else:
                n = T >> lev
                t = tot[:, par, T - 2 * n:T - n]
            t = t.rearrange("p (n e) -> p n e", e=2)[:, :, odd:odd + 1]
            return t.to_broadcast([P, n // 2, 1 << lev])

        def chunk_sel(buf, lev):
            flat = buf[:, :, :].rearrange("p c t -> p (c t)")
            n = P >> (lev + 1)
            cols = [flat[:, c * (T + P):c * (T + P) + P] for c in range(C)]
            one = cols[0].rearrange("p (n e l) -> p n e l", e=2, l=1 << lev)[:, :, 1, :]
            lead, rest = one.ap[0], list(one.ap[1:])
            return bass.AP(one.tensor, one.offset, [list(lead), [T + P, C]] + [list(r) for r in rest])

        def diag_blocks(buf, c0, nc_):
            flat = buf[:, :, :].rearrange("p c t -> p (c t)")[:, c0 * (T + P):c0 * (T + P) + P]
            return bass.AP(flat.tensor, flat.offset, [list(flat.ap[0]), [T + P, nc_], [1, P]])

        def unused(buf, i):
            return buf[:, 3, i * P:(i + 1) * P] if i < 3 else buf[:, 2, 0:P]

        def mask_sel(lev, dt=F32):
            m = masks[:, lev, :].bitcast(dt) if dt != F32 else masks[:, lev, :]
            one = m.rearrange("p (n l) -> p n l", l=1 << lev)
            return bass.AP(one.tensor, one.offset, [list(one.ap[0]), [0, C]] + [list(r) for r in one.ap[1:]])

        def mix_cols(half, lev):
            return mix_ps[:, half, 0:T // 2].rearrange("p (c n l) -> p c n l", c=C, l=1 << lev)

        def Ulev(u, lev):
            return wT[:, u.par, :] if lev == 0 else U[:, u.par % 2, lev - 1, :]


        wg32 = Uflat[:, 2048:4096].rearrange("p (k n) -> p k n", k=KT)
        wu32 = Uflat[:, 4096:6144].rearrange("p (k n) -> p k n", k=KT)
        wd32 = Uflat[:, 6144:8192].rearrange("p (k n) -> p k n", k=FT)
        sg_sb = sb("sg_sb", [P, FT])
        su_sb = sb("su_sb", [P, FT])
        sgu = sb("sgu", [P, FT])
        sd_sb = sb("sd_sb", [P, HID])
        y = A[:, 0:2, :].rearrange("p a (i n) -> p (a i) n", n=HID)
        yT = A[:, 2:4, :]
        fusedT = [gT, tot]
        bn = sb("bn", [P, C, 6])
        tick = sb("tick", [P, 1])
        mv = sb("mv", [P, C, 2])
        rs = sb("rs", [P, C])

        def fused_tile(f):
            return fusedT[f // 4][:, f % 4, :]

        def grow_W(pool, u3, lev):
            w = pairs(W[:, :], lev)[:, :, 1, :]
            pool.wait_ge(W_step, u3.count(9, 1 + lev))
            pool.wait_ge(mix_ps_ready, u3.count(12, 3 + lev))
            nc.gpsimd.tensor_tensor(w, w, block_tot(u3.par, lev, 0), ALU.mult).then_inc(W_step, 1)

        def ffn_gate_ps(f):
            return proj_ps[:, f % 2, :]

        def ffn_up_ps(f):
            return mix_ps[:, f % 2, :]

        CONV_BANK = (1, 1, 0, 1)
        PROJ_AT = (1, 3, 4, 5)
        COEF_OF = (0, 1, 2, 0)

        def tap(act, s, i):
            u1 = s.u1
            if i == 0:
                act.wait_ge(coef_set, u1.h + 1)
            act.wait_ge(proj_ps_ready, u1.count(5, PROJ_AT[i]))
            wait(act, silu_done, u1.count(4, i - 1))
            if i == 1:
                wait(act, vT_ps_ready, u1.count(1, 0))
            nc.scalar.activation(conv[:, i % 2, :], proj_ps[:, CONV_BANK[i], :], ACT.Copy,
                                 scale=coef[:, COEF_OF[i], KW - 1:KW]).then_inc(tap_done, 1)

        def tanh(act, u1, i):
            act.wait_ge(conv_step, u1.count(12, 3 * i + 3))
            nc.scalar.activation(th[:, i % 2, :], conv[:, i % 2, :], ACT.Tanh, scale=0.5).then_inc(tanh_done, 1)

        def evac_UT(act, u2, i):
            act.wait_ge(UT_ps_ready, u2.count(8, i + 1))
            wait(act, out_ps_ready, u2.count(9, i - 1))
            nc.scalar.activation(UT[:, i % 2, :], tr_ps[:, :], ACT.Copy).then_inc(UT_done, 1)

        def down_ps(c):
            return (work_ps[:, 0, 0:HID], work_ps[:, 1, 0:HID], tr_ps[:, 0:HID], out_ps[:, 0:HID])[c]

        def layer_norm(dve, b, before, stats, var_eps, rstd, done, dst):
            def src(c):
                return acc[:, bass.ds(b * C + c, 1), :].rearrange("p o n -> p (o n)")
            if before:
                dve.wait_ge(ffn[before], b * C + C)
            nc.vector.memset(tick[:, :], 0.0)
            for c in range(C):
                nc.vector.bn_stats(bn[:, c, :], src(c)).then_inc(ffn[stats], 1)
            dve.wait_ge(ffn[stats], b * 2 * C + C)
            nc.vector.memset(tick[:, :], 0.0)
            for c in range(C):
                nc.vector.bn_aggr(mv[:, c, :], bn[:, c, :]).then_inc(ffn[stats], 1)
            dve.wait_ge(ffn[stats], b * 2 * C + 2 * C)
            nc.vector.tensor_scalar(rs[:, :].unsqueeze(2), mv[:, :, 1:2], LN_EPS, None, ALU.add)\
                .then_inc(ffn[var_eps], 1)
            dve.wait_ge(ffn[rstd], b * 1 + 1)
            for c in range(C):
                nc.vector.tensor_scalar(dst(c), src(c), mv[:, c, 0:1], rs[:, c:c + 1], ALU.subtract, ALU.mult)\
                    .then_inc(ffn[done], 1)

        def grow_U(dve, u2, lev):
            src, dst = pairs(Ulev(u2, lev), lev), pairs(Ulev(u2, lev + 1), lev)
            if lev == 0:
                dve.wait_ge(silu_done, u2.count(4, 1))
                dve.wait_ge(decay_step, u2.count(9, 9))
                wait(dve, mix_ps_ready, u2.count(12, -12))
            else:
                dve.wait_ge(U_step, u2.count(16, 2 * lev))
            nc.vector.tensor_tensor(dst[:, :, 0, :], src[:, :, 0, :], block_tot(u2.par, lev, 1), ALU.mult)\
                .then_inc(U_step, 1)
            nc.vector.tensor_copy(dst[:, :, 1, :], src[:, :, 1, :]).then_inc(U_step, 1)

        def conv_tap(dve, u1, i, k):
            back = k + 1
            dve.wait_ge(tap_done, u1.count(4, i + 1)) if k == 0 else dve.wait_ge(conv_step, u1.count(12, 3 * i + k))
            y_ = conv[:, i % 2, back:T]
            nc.vector.scalar_tensor_tensor(y_, proj_ps[:, CONV_BANK[i], 0:T - back],
                                           coef[:, COEF_OF[i], KW - 1 - back:KW - back], y_, ALU.mult, ALU.add)\
                .then_inc(conv_step, 1)

        def silu(dve, u1, i):
            dst = (wT[:, u1.par, :], qk[:, u1.par % 2, 0, :], qk[:, u1.par % 2, 1, :],
                   conv[:, 1, :])[i]
            dve.wait_ge(tanh_done, u1.count(4, i + 1))
            nc.vector.scalar_tensor_tensor(dst, th[:, i % 2, :], 1.0, conv[:, i % 2, :], ALU.add, ALU.mult)\
                .then_inc(silu_done, 1)


        def decay(dve, u1, i):
            if i == 0:
                dve.wait_ge(fexp_done, u1.count(1, 1))
                nc.vector.tensor_scalar(fexp[:, :], fexp[:, :], 1.0, None, ALU.add).then_inc(decay_step, 1)
                return
            dve.wait_ge(decay_step, u1.count(9, i))
            if i == 1:
                nc.vector.reciprocal(gT[:, u1.par, :], fexp[:, :]).then_inc(decay_step, 1)
                return
            lev = i - 1
            n = T >> lev
            src = gT[:, u1.par, :] if lev == 1 else tot[:, u1.par, T - 4 * n:T - 2 * n]
            src = src.rearrange("p (n e) -> p n e", e=2)
            nc.vector.tensor_tensor(tot[:, u1.par, T - 2 * n:T - n], src[:, :, 0], src[:, :, 1], ALU.mult)\
                .then_inc(decay_step, 1)

        def descend(dve, u2, r):
            lev = LEVELS - 1 - r
            new = out_ps[:, 0:T // 2]
            if r == 0:
                wait(dve, sT_done, u2.count(1, 0))
                nc.vector.memset(V[:, 0:T // 2], 0.0).then_inc(V_step, 1)
                dve.wait_ge(out_ps_ready, u2.count(9, 1))
                nc.vector.tensor_copy(V[:, T // 2:T], new).then_inc(V_step, 1)
                return
            v = pairs(V[:, :], lev)[:, :, 1, :]
            dve.wait_ge(V_step, u2.count(18, 2 * r))
            nc.vector.tensor_tensor(v, v, block_tot(u2.par, lev, 0), ALU.mult).then_inc(V_step, 1)
            dve.wait_ge(V_step, u2.count(18, 2 * r + 1))
            dve.wait_ge(out_ps_ready, u2.count(9, r + 1))
            nc.vector.tensor_tensor(v, v, new.rearrange("p (n l) -> p n l", l=1 << lev), ALU.add).then_inc(V_step, 1)

        def mixable(dve, s, i):
            if not s.u2:
                wait(dve, mix_done, s.u3.count(12, i))
            dve.wait_ge(mix_ps_ready, s.u3.count(12, i + 1))

        def mix(dve, u3, i):
            half = i % 2
            if i < 2:
                idb = ident[:, :].bitcast(U32).unsqueeze(1).to_broadcast([P, 2, P])
                ins = nc.vector.copy_predicated(diag_blocks(A2, 2 * i, 2), idb,
                                                mix_ps[:, half, 0:T // 2].rearrange("p (c t) -> p c t", c=2))
            elif i < 2 + IN_CHUNK:
                lev = i - 2
                ins = nc.vector.copy_predicated(chunk_sel(A2, lev), mask_sel(lev, U32), mix_cols(half, lev))
            elif i == 9:
                for p_ in range(2):
                    ins = nc.vector.tensor_copy(A2[:, 2 * p_, (2 * p_ + 1) * P:(2 * p_ + 2) * P],
                                                mix_ps[:, half, p_ * P:(p_ + 1) * P])
            else:
                ins = nc.vector.tensor_copy(A2[:, i - 10, T // 2:T], mix_ps[:, half, 0:T // 2])
            ins.then_inc(mix_done, 1)

        def project(pe, s, i):
            u1 = s.u1
            pe.wait_ge((head_w, head_q, head_k, head_v)[i], 16 * (u1.h + 1))
            if i == 0:
                wait(pe, conv_step, u1.count(12, 0))
            elif i == 2:
                pe.wait_ge(fexp_done, u1.count(1, 1))
            else:
                pe.wait_ge(conv_step, u1.count(12, 3 if i == 1 else 6))
            for k in range(KT):
                last = nc.tensor.matmul(proj_ps[:, CONV_BANK[i], :], w_head[:, i, k, :],
                                        hT[:, k, u1.par * T:(u1.par + 1) * T], start=(k == 0), stop=(k == KT - 1))
            last.then_inc(proj_ps_ready, 1)

        def turn_U(pe, u2, i):
            lev = LEVELS - 1 - i
            pe.wait_ge(U_step, u2.count(16, 2 * lev))
            wait(pe, UT_done, u2.count(8, i))
            chunks = (0, 1) if lev == 8 else (0, 2) if lev == 7 else range(C)
            if lev >= 7:
                chunks = range(C)
            for c in chunks:
                last = nc.tensor.transpose(tr_ps[:, c * P:(c + 1) * P], Ulev(u2, lev)[:, c * P:(c + 1) * P],
                                           ident[:, :])
            last.then_inc(UT_ps_ready, 1)

        def level_scores(pe, u2, r):
            lev = LEVELS - 1 - r
            dst = out_ps[:, 0:T // 2]
            wait(pe, V_step, u2.count(18, 2 * r))
            if lev:
                pe.wait_ge(UT_done, u2.count(8, r + 1))
            else:
                pe.wait_ge(wN_step, u2.count(5, 5))
            ut = UT[:, r % 2, :] if lev else wN[:, u2.par % 2, :]
            if lev == 8:
                for c in range(2):
                    last = nc.tensor.matmul(dst, ut[:, c * P:(c + 1) * P], A[:, c, T // 2:T], start=(c == 0), stop=(c == 1))
            elif lev == 7:
                for c in (0, 2):
                    last = nc.tensor.matmul(dst[:, c * P // 2:(c + 2) * P // 2], ut[:, c * P:(c + 1) * P],
                                            A[:, c, (c + 1) * P:(c + 2) * P], start=True, stop=True)
            else:
                pe.wait_ge(Alev_done, u2.count(8, 2 + (IN_CHUNK - 1 - lev)))
                for c in range(C):
                    last = nc.tensor.matmul(dst[:, c * P // 2:(c + 1) * P // 2], ut[:, c * P:(c + 1) * P],
                                            A_lev[:, lev, c, :], start=True, stop=True)
            last.then_inc(out_ps_ready, 1)

        def mix_products(pe, u3, i):
            half = i % 2
            wait(pe, mix_done, u3.count(12, i - 1))
            if i < 2:
                for c in (2 * i, 2 * i + 1):
                    last = nc.tensor.matmul(mix_ps[:, half, (c % 2) * P:(c % 2 + 1) * P], wT[:, u3.par, c * P:(c + 1) * P],
                                            aT[:, c * P:(c + 1) * P], start=True, stop=True)
            else:
                lev = min(i - 2, LEVELS - 1)
                pe.wait_ge(W_step, u3.count(9, 1 + lev))
                ul = Ulev(u3, lev)
                if lev < IN_CHUNK:
                    for c in range(C):
                        t_sel = pairs(W[:, c * P:(c + 1) * P], lev)[:, :, 1, :]
                        last = nc.tensor.matmul(mix_ps[:, half, c * P // 2:(c + 1) * P // 2], ul[:, c * P:(c + 1) * P],
                                                t_sel, start=True, stop=True)
                elif lev == 7:
                    for c in (0, 2):
                        last = nc.tensor.matmul(mix_ps[:, half, c * P // 2:(c + 2) * P // 2], ul[:, c * P:(c + 1) * P],
                                                W[:, (c + 1) * P:(c + 2) * P], start=True, stop=True)
                else:
                    c = i - 10
                    last = nc.tensor.matmul(mix_ps[:, half, 0:T // 2], ul[:, c * P:(c + 1) * P], W[:, T // 2:T],
                                            start=True, stop=True)
            last.then_inc(mix_ps_ready, 1)


        block = ctx.enter_context(nc.Block())

        @block.sync
        def _(sp):
            nc.sync.dma_start(acc[:, :, :], x.rearrange("b (c p) n -> p (b c) n", p=P)).then_inc(x_in, 16)
            nc.sync.dma_start(setup_w[:, 0], Wf1.rearrange("(k p) n -> p k n", p=P)).then_inc(w_in, 16)
            nc.sync.dma_start(setup_w[:, 1], Wg1.rearrange("(k p) n -> p k n", p=P)).then_inc(w_in, 16)
            nc.sync.dma_start(wb_sb, Wb.rearrange("(k p) n -> p k n", p=P)).then_inc(w_in, 16)
            for i, c in enumerate((cv, cq, ck)):
                nc.sync.dma_start(coefs[:, i], c.rearrange("(h p) w -> p h w", p=P)).then_inc(small_in, 16)
            with nc.allow_non_contiguous_dma(reason="a few hundred words, once"):
                nc.sync.dma_start(bg2_sb[:, :], bg2.rearrange("(h p) -> p h", p=P)).then_inc(small_in, 16)
                nc.sync.dma_start(consts[:, 3, 0:1], norm_w.rearrange("(p o) -> p o", o=1)).then_inc(small_in, 16)
            nc.sync.dma_start(wo_sb[:, :, :], Wo.rearrange("(h p) n -> p h n", p=P)).then_inc(wo_in, 16)

            def head_cols(w, h):
                return w[:, bass.ts(h, P)].rearrange("(k p) n -> p k n", p=P)

            def load_head(h, first):
                before = None if first else Unit(h, -1)
                for i, (w, landed) in enumerate(((Ww, head_w), (None, head_f), (Wq, head_q), (Wk, head_k),
                                                 (Wv, head_v))):
                    if before is not None:
                        sp.wait_ge(proj_ps_ready, before.count(5, i + 1))
                    if w is None:
                        nc.sync.dma_start(wf2_head[:, :], Wf2[:, bass.ts(h, P)]).then_inc(landed, 16)
                    else:
                        slot = i if i == 0 else i - 1
                        nc.sync.dma_start(w_head[:, slot], head_cols(w, h)).then_inc(landed, 16)

            def load_gate(h, first):
                if not first:
                    sp.wait_ge(gate_ps_ready, Unit(h, 0).count(1, 0))
                nc.sync.dma_start(wg2_head[:, :], Wg2[:, bass.ts(h, P)]).then_inc(head_g, 16)

            load_head(0, True)
            load_gate(0, True)
            with sp.Fori(1, H) as h:
                load_head(h, False)
                load_gate(h, False)

            sp.wait_ge(mix_ps_ready, 12 * B * H)
            q8 = [Uflat[:, i * 512:(i + 1) * 512].bitcast(I32) for i in range(3)]
            nc.sync.dma_start(q8[0].rearrange("p (k n) -> p k n", k=KT), w_gate.rearrange("(k p) n -> p k n", p=P)).then_inc(ffn["q_in"], 16)
            nc.sync.dma_start(q8[1].rearrange("p (k n) -> p k n", k=KT), w_up.rearrange("(k p) n -> p k n", p=P)).then_inc(ffn["q_in"], 16)
            nc.sync.dma_start(q8[2].rearrange("p (k n) -> p k n", k=FT), w_down.rearrange("(k p) n -> p k n", p=P)).then_inc(ffn["q_in"], 16)
            with nc.allow_non_contiguous_dma(reason="a few hundred words, once"):
                nc.sync.dma_start(sg_sb[:, :], s_gate.rearrange("(f p) -> p f", p=P)).then_inc(ffn["scale_in"], 16)
                nc.sync.dma_start(su_sb[:, :], s_up.rearrange("(f p) -> p f", p=P)).then_inc(ffn["scale_in"], 16)
            nc.sync.dma_start(sd_sb[:, :], s_down.rearrange("(o n) -> o n", o=1).to_broadcast([P, HID])).then_inc(ffn["scale_in"], 16)

            out_v = out.rearrange("b (c p) n -> p (b c) n", p=P)
            with sp.Fori(0, B) as b:
                sp.wait_ge(ffn["done"], b * C + C)
                nc.sync.dma_start(out_v[:, bass.ts(b, C), :], acc[:, bass.ts(b, C), :]).then_inc(ffn["store"], 16)
            sp.wait_ge(ffn["store"], 16 * B)

        @block.gpsimd
        def _(pool):
            nc.gpsimd.memset(ident[:, :], 0.0).then_inc(mask_ready, 1)
            nc.gpsimd.memset(masks[:, :, :], 1.0).then_inc(mask_ready, 1)
            nc.gpsimd.memset(A2[:, :, :], 0.0).then_inc(const_ready, 1)
            nc.gpsimd.memset(consts[:, 0, :], 4.0 * NORM_EPS).then_inc(const_ready, 1)
            nc.gpsimd.memset(consts[:, 1, :], -0.5).then_inc(const_ready, 1)
            nc.gpsimd.memset(consts[:, 2, :], 4.0 * D * RMS_EPS).then_inc(const_ready, 1)
            pool.wait_ge(mask_ready, 2)
            nc.gpsimd.affine_select(out=ident[:, :], in_=ident[:, :], compare_op=ALU.not_equal, fill=1.0, base=0,
                                    pattern=[[-1, P]], channel_multiplier=1).then_inc(mask_ready, 1)
            for lev in range(IN_CHUNK):
                L = 1 << lev
                m = masks[:, lev, :].rearrange("p (n l) -> p n l", l=L)
                nc.gpsimd.affine_select(out=m, in_=m, compare_op=ALU.is_ge, fill=0.0, base=0,
                                        pattern=[[-2 * L, P // 2 // L], [0, L]], channel_multiplier=1)\
                    .then_inc(mask_ready, 1)
                pool.wait_ge(mask_ready, 4 + 2 * lev)
                nc.gpsimd.affine_select(out=m, in_=m, compare_op=ALU.is_ge, fill=0.0, base=L - 1,
                                        pattern=[[2 * L, P // 2 // L], [0, L]], channel_multiplier=-1)\
                    .then_inc(mask_ready, 1)
            pool.wait_ge(mask_ready, 3 + 2 * IN_CHUNK)
            pool.wait_ge(const_ready, 4)

            for s in slots(pool, H, B):
                u1, u2, u3, u4 = s.u1, s.u2, s.u3, s.u4
                if u4:
                    r = rms[:, u4.par % 2, :]
                    z = Z[:, u4.par, :]
                    wait(pool, on_done, u4.count(4, -4))
                    pool.wait_ge(a_done, u4.count(4, 4))
                    nc.gpsimd.tensor_tensor(r, z, z, ALU.mult).then_inc(rms_step, 1)
                    pool.wait_ge(rms_step, u4.count(4, 1))
                    nc.gpsimd.tensor_tensor(r, r, consts[:, 2, :], ALU.mult).then_inc(rms_step, 1)
                    pool.wait_ge(rms_step, u4.count(4, 2))
                    pool.wait_ge(osq_done, u4.count(4, 4))
                    nc.gpsimd.tensor_tensor(r, r, ssqo[:, u4.par % 2, :], ALU.add).then_inc(rms_step, 1)
                    pool.wait_ge(rms_step, u4.count(4, 3))
                    nc.gpsimd.tensor_tensor(r, r, consts[:, 1, :], ALU.pow).then_inc(rms_step, 1)
                if u3:
                    pool.wait_ge(aT_done, u3.count(1, 1))
                    pool.wait_ge(decay_step, u3.count(9, 9))
                    wait(pool, mix_ps_ready, u3.count(12, 0))
                    nc.gpsimd.tensor_tensor(W[:, :], aT[:, :], gT[:, u3.par, :], ALU.mult).then_inc(W_step, 1)
                if u2:
                    wait(pool, out_ps_ready, u2.count(9, 0))
                    wait(pool, s_ps_ready, u2.count(1, 0))
                    pool.wait_ge(A_done, u2.count(4, 4))
                    idb = ident[:, :].unsqueeze(1).to_broadcast([P, C, P])
                    nc.gpsimd.tensor_tensor(A_diag[:, :, :], diag_blocks(A, 0, C), idb, ALU.mult).then_inc(Alev_done, 1)
                for i in range(IN_CHUNK):
                    lev = IN_CHUNK - 1 - i
                    if u2:
                        dst = A_lev[:, lev].rearrange("p c (n l) -> p c n l", l=1 << lev)
                        nc.gpsimd.tensor_tensor(dst, chunk_sel(A, lev), mask_sel(lev), ALU.mult)\
                            .then_inc(Alev_done, 1)
                    if u3:
                        grow_W(pool, u3, i)
                if u3:
                    grow_W(pool, u3, IN_CHUNK)
                if u1:
                    f = fac[:, u1.par, :]
                    pool.wait_ge(wN_step, u1.count(5, 4))
                    nc.gpsimd.tensor_tensor(f, ssq[:, u1.par % 2, :], consts[:, 0, :], ALU.add).then_inc(fac_step, 1)
                    pool.wait_ge(fac_step, u1.count(3, 1))
                    nc.gpsimd.tensor_tensor(f, f, consts[:, 1, :], ALU.pow).then_inc(fac_step, 1)
                    pool.wait_ge(fac_step, u1.count(3, 2))
                    if s.n == 0 and s.edge:
                        pool.wait_ge(first_sb, 2 * B + NT)
                    bt = beta[:, u1.par * C:(u1.par + 1) * C, bass.ds(u1.h, 1)].rearrange("p c o -> p (c o)")
                    nc.gpsimd.tensor_tensor(f, f, bt, ALU.mult).then_inc(fac_step, 1)
                if u2:
                    pool.wait_ge(V_step, u2.count(18, 18))
                    wait(pool, s_ps_ready, u2.count(1, 0))
                    nc.gpsimd.tensor_tensor(sT[:, :], V[:, :], gT[:, u2.par, :], ALU.mult).then_inc(sT_done, 1)

            with pool.Fori(0, B) as b:
                pool.wait_ge(ffn["var_eps"], b * 1 + 1)
                nc.gpsimd.tensor_tensor(rs[:, :], rs[:, :], consts[:, 1, :], ALU.pow).then_inc(ffn["rstd"], 1)
                pool.wait_ge(ffn["var_eps2"], b * 1 + 1)
                nc.gpsimd.tensor_tensor(rs[:, :], rs[:, :], consts[:, 1, :], ALU.pow).then_inc(ffn["rstd2"], 1)

        @block.scalar
        def _(act):
            for g in range(NT * KT // 4):
                act.wait_ge(xT_ps, g + 1)
                k, t0 = g // (NT // 4), (g % (NT // 4)) * T
                nc.scalar.activation(hT[:, k, t0:t0 + T], work_ps[:, g % 2, :], ACT.Copy).then_inc(xT_sb, 1)
            for b in range(B):
                for i, dst in enumerate((f1T, g1T)):
                    act.wait_ge(first_ps, 2 * b + i + 1)
                    nc.scalar.activation(dst[:, b * T:(b + 1) * T], proj_ps[:, i, :], ACT.Copy).then_inc(first_sb, 1)
            act.wait_ge(first_ps, 2 * B + 1)
            nc.scalar.activation(beta[:, :, :].rearrange("p t h -> p (t h)"), work_ps[:, 0, 0:NT * H], ACT.Exp,
                                 scale=-1.0).then_inc(first_sb, 1)
            act.wait_ge(small_in, 16 * 5)
            nc.scalar.activation(bg2_sb[:, :], bg2_sb[:, :], ACT.Copy, scale=0.5).then_inc(gbias_set, 1)

            for s in slots(act, H, B):
                u1, u2, u3, u4 = s.u1, s.u2, s.u3, s.u4
                if u3:
                    act.wait_ge(max_step, u3.count(2, 2))
                    for c in range(C):
                        nc.scalar.activation(aN[:, c * P:(c + 1) * P], work_ps[:, 1, c * P:(c + 1) * P], ACT.Exp,
                                             bias=mx[:, 1, c:c + 1], scale=SCALE / 4,
                                             accum_out=Z[:, u3.par, c:c + 1]).then_inc(a_done, 1)
                if u4:
                    act.wait_ge(oN_done, u4.count(1, 1))
                    for c in range(C):
                        nc.scalar.activation(unused(A2, c), oN[:, c * P:(c + 1) * P], ACT.Square,
                                             accum_out=ssqo[:, u4.par % 2, c:c + 1]).then_inc(osq_done, 1)
                if u3:
                    act.wait_ge(aT_ps_ready, u3.count(1, 1))
                    wait(act, W_step, u3.count(9, -8))
                    wait(act, mix_ps_ready, u3.count(12, -10))
                    nc.scalar.activation(aT[:, :], work_ps[:, 0, :], ACT.Copy).then_inc(aT_done, 1)
                if u2:
                    wait(act, out_ps_ready, u2.count(9, 0))
                    act.wait_ge(fac_step, u2.count(3, 3))
                    for c in range(C):
                        act.wait_ge(A_ps_ready, u2.count(4, c + 1))
                        nc.scalar.activation(A[:, c, c * P:T], work_ps[:, (c + 1) % 2, c * P:T], ACT.Copy,
                                             scale=fac[:, u2.par, c:c + 1]).then_inc(A_done, 1)
                if u4:
                    if u4.par == 0:
                        nc.scalar.activation(gbias[:, :], bg2_sb[:, bass.ds(u4.h, 1)], ACT.Copy).then_inc(gbias_set, 1)
                    act.wait_ge(gbias_set, 2 + u4.h)
                    act.wait_ge(gate_ps_ready, u4.count(1, 1))
                    wait(act, og_done, u4.count(1, 0))
                    nc.scalar.activation(tg[:, :], proj_ps[:, 0, :], ACT.Tanh, bias=gbias[:, 0:1], scale=0.5)\
                        .then_inc(tg_done, 1)
                    act.wait_ge(rms_step, u4.count(4, 4))
                    for c in range(C):
                        nc.scalar.activation(oN[:, c * P:(c + 1) * P], oN[:, c * P:(c + 1) * P], ACT.Copy,
                                             scale=rms[:, u4.par % 2, c:c + 1]).then_inc(on_done, 1)
                if u1:
                    tap(act, s, 0)
                    act.wait_ge(proj_ps_ready, u1.count(5, 2))
                    wait(act, decay_step, u1.count(9, -7))
                    nc.scalar.activation(fexp[:, :], proj_ps[:, 0, :], ACT.Exp, scale=-1.0).then_inc(fexp_done, 1)
                    tanh(act, u1, 0)
                if u2:
                    evac_UT(act, u2, 0)
                if u1:
                    tap(act, s, 1)
                if u2:
                    evac_UT(act, u2, 1)
                if u1:
                    tanh(act, u1, 1)
                if u2:
                    evac_UT(act, u2, 2)
                    evac_UT(act, u2, 3)
                if u1:
                    act.wait_ge(wT_ps_ready, u1.count(1, 1))
                    for c in range(C):
                        nc.scalar.activation(unused(A, c), work_ps[:, 0, c * P:(c + 1) * P], ACT.Square,
                                             accum_out=ssq[:, u1.par % 2, c:c + 1]).then_inc(wN_step, 1)
                    nc.scalar.activation(wN[:, u1.par % 2, :], work_ps[:, 0, :], ACT.Copy).then_inc(wN_step, 1)
                if u2:
                    evac_UT(act, u2, 4)
                if u1:
                    tap(act, s, 2)
                if u2:
                    evac_UT(act, u2, 5)
                    evac_UT(act, u2, 6)
                    evac_UT(act, u2, 7)
                if u1:
                    tanh(act, u1, 2)
                    tap(act, s, 3)
                    tanh(act, u1, 3)
                if u3:
                    act.wait_ge(o_ps_ready, u3.count(1, 1))
                    if u4:
                        act.wait_ge(onT_ps_ready, u4.count(1, 1))
                    nc.scalar.activation(oN[:, :], work_ps[:, 0, :], ACT.Copy).then_inc(oN_done, 1)

            act.wait_ge(ffn["q_in"], 48)
            for i, dst in enumerate((wg32, wu32, wd32)):
                nc.scalar.activation(dst.rearrange("p k n -> p (k n)"), Uflat[:, i * 512:(i + 1) * 512].bitcast(I8),
                                     ACT.Copy).then_inc(ffn["cast"], 1)
            act.wait_ge(ffn["scales"], 2)
            with act.Fori(0, B) as b:
                for k in range(KT):
                    act.wait_ge(ffn["yT_ps"], b * KT + (k + 1))
                    nc.scalar.activation(yT[:, k, :], work_ps[:, k, :], ACT.Copy).then_inc(ffn["yT_sb"], 1)
                for f in range(FT):
                    act.wait_ge(ffn["up_ps"], b * 2 * FT + (2 * f + 1))
                    if f >= 2:
                        act.wait_ge(ffn["mid"], b * FT + (f - 1))
                    nc.scalar.activation(th[:, f % 2, :], ffn_gate_ps(f), ACT.Tanh, scale=sg_sb[:, f:f + 1])\
                        .then_inc(ffn["tanh"], 1)

        @block.vector
        def _(dve):
            dve.wait_ge(first_sb, 2 * B + 1)
            bflat = beta[:, :, :].rearrange("p t h -> p (t h)")
            nc.vector.tensor_scalar(bflat, bflat, 1.0, None, ALU.add).then_inc(wo_scaled, 1)
            dve.wait_ge(wo_scaled, 1)
            for t in range(NT):
                last = nc.vector.reciprocal(beta[:, t, :], beta[:, t, :])
                last.then_inc(first_sb, 1)
            dve.wait_ge(wo_in, 16)
            dve.wait_ge(small_in, 16 * 5)
            nc.vector.tensor_scalar(wo_sb[:, :, :].rearrange("p h n -> p (h n)"),
                                    wo_sb[:, :, :].rearrange("p h n -> p (h n)"),
                                    consts[:, 3, 0:1], 0.5 * float(D) ** 0.5, ALU.mult, ALU.mult).then_inc(wo_scaled, 1)
            dve.wait_ge(mask_ready, 3 + 2 * IN_CHUNK)
            dve.wait_ge(const_ready, 4)

            for s in slots(dve, H, B):
                u1, u2, u3, u4 = s.u1, s.u2, s.u3, s.u4
                if u1 and s.j == 0:
                    dve.wait_ge(tap_done, u1.count(4, 0)) if not s.edge else None
                    nc.vector.tensor_copy(coef[:, :, :], coefs[:, :, bass.ds(u1.h, 1), :].rearrange("p i o w -> p i (o w)"))\
                        .then_inc(coef_set, 1)
                    dve.wait_ge(coef_set, u1.h + 1)
                for lev in range(LEVELS - 1):
                    if u3 and lev in (1, 5, 7):
                        mixable(dve, s, (1, 5, 7).index(lev))
                    if u2:
                        grow_U(dve, u2, lev)
                    if u1 and 2 <= lev < 5:
                        conv_tap(dve, u1, 0, lev - 2)
                    if u1 and lev == 6:
                        decay(dve, u1, 0)
                    if u1 and lev == 7:
                        decay(dve, u1, 1)
                        silu(dve, u1, 0)
                    if u3 and lev in (1, 5, 7):
                        mix(dve, u3, (1, 5, 7).index(lev))
                if u1:
                    for i in range(2, 9):
                        decay(dve, u1, i)
                if u4:
                    dve.wait_ge(tg_done, u4.count(1, 1))
                    dve.wait_ge(onT_ps_ready, u4.count(1, 1))
                    wait(dve, y_ps_ready, u4.count(2, 0))
                    nc.vector.scalar_tensor_tensor(ogT[:, :], tg[:, :], 1.0, work_ps[:, 1, :], ALU.add, ALU.mult)\
                        .then_inc(og_done, 1)
                if u1:
                    for i in range(3):
                        conv_tap(dve, u1, 1, i)
                if u4:
                    for i in range(2):
                        dve.wait_ge(y_ps_ready, u4.count(2, i + 1))
                        a = acc[:, u4.par * C + 2 * i:u4.par * C + 2 * i + 2, :]
                        nc.vector.tensor_tensor(a, a, work_ps[:, i, :].rearrange("p (c n) -> p c n", c=2), ALU.add)\
                            .then_inc(acc_done, 1)
                if u1:
                    silu(dve, u1, 1)
                for r in range(LEVELS):
                    if u3 and r:
                        mixable(dve, s, r + 2)
                    if u2:
                        descend(dve, u2, r)
                    if u3 and r:
                        mix(dve, u3, r + 2)
                    if u1 and r in (4, 5, 6):
                        conv_tap(dve, u1, 2, r - 4)
                    if u1 and r == 7:
                        silu(dve, u1, 2)
                if u3:
                    mixable(dve, s, LEVELS + 2)
                    mix(dve, u3, LEVELS + 2)
                if u1:
                    for i in range(3):
                        conv_tap(dve, u1, 3, i)
                    silu(dve, u1, 3)
                    dve.wait_ge(vT_ps_ready, u1.count(1, 1))
                    dve.wait_ge(fac_step, u1.count(3, 3))
                    fb = fac[:, u1.par, :].unsqueeze(2).to_broadcast([P, C, P])
                    nc.vector.tensor_tensor(vN[:, u1.par, :].rearrange("p (c d) -> p c d", c=C),
                                            work_ps[:, 1, :].rearrange("p (c d) -> p c d", c=C), fb, ALU.mult)\
                        .then_inc(vN_done, 1)
                if u2:
                    dve.wait_ge(s_ps_ready, u2.count(1, 1))
                    wait(dve, a_done, u2.count(4, 0))
                    nc.vector.reduce_max(mx[:, 0, :], work_ps[:, 1, :].rearrange("p (c m) -> p c m", c=C), AX_X)\
                        .then_inc(max_step, 1)
                    dve.wait_ge(max_step, u2.count(2, 1))
                    nc.vector.tensor_scalar(mx[:, 1, :], mx[:, 0, :], -SCALE / 4, None, ALU.mult).then_inc(max_step, 1)

            dve.wait_ge(acc_done, 2 * B * H)
            dve.wait_ge(ffn["scale_in"], 48)
            nc.vector.tensor_tensor(sgu[:, :], sg_sb[:, :], su_sb[:, :], ALU.mult).then_inc(ffn["scales"], 1)
            nc.vector.tensor_scalar(sg_sb[:, :], sg_sb[:, :], 0.5, None, ALU.mult).then_inc(ffn["scales"], 1)
            with dve.Fori(0, B) as b:
                layer_norm(dve, b, None, "stats", "var_eps", "rstd", "norm", lambda c: y[:, c, :])
                for f in range(FT):
                    dve.wait_ge(ffn["tanh"], b * FT + (f + 1))
                    m = conv[:, f % 2, :]
                    nc.vector.scalar_tensor_tensor(m, th[:, f % 2, :], 1.0, ffn_gate_ps(f), ALU.add, ALU.mult)\
                        .then_inc(ffn["mid"], 1)
                    dve.wait_ge(ffn["mid"], b * FT + (f + 1))
                    dve.wait_ge(ffn["up_ps"], b * 2 * FT + (2 * f + 2))
                    nc.vector.scalar_tensor_tensor(fused_tile(f), m, sgu[:, f:f + 1], ffn_up_ps(f), ALU.mult, ALU.mult)\
                        .then_inc(ffn["fused"], 1)
                for c in range(C):
                    dve.wait_ge(ffn["down_ps"], b * C + (c + 1))
                    a = acc[:, bass.ds(b * C + c, 1), :].rearrange("p o n -> p (o n)")
                    nc.vector.scalar_tensor_tensor(a, down_ps(c), 0.5, sd_sb[:, :], ALU.mult, ALU.mult)\
                        .then_inc(ffn["scaled"], 1)
                    dve.wait_ge(ffn["scaled"], b * C + (c + 1))
                    nc.vector.tensor_tensor(a, a, y[:, c, :], ALU.add).then_inc(ffn["res"], 1)
                layer_norm(dve, b, "res", "stats2", "var_eps2", "rstd2", "done",
                           lambda c: acc[:, bass.ds(b * C + c, 1), :].rearrange("p o n -> p (o n)"))

        @block.tensor
        def _(pe):
            mm, tr = nc.tensor.matmul, nc.tensor.transpose
            pe.wait_ge(x_in, 16)
            pe.wait_ge(mask_ready, 3)
            for g in range(NT * KT // 4):
                k, q = g // (NT // 4), g % (NT // 4)
                if g >= 2:
                    pe.wait_ge(xT_sb, g - 1)
                for c in range(4):
                    last = tr(work_ps[:, g % 2, c * P:(c + 1) * P], acc[:, 4 * q + c, k * P:(k + 1) * P], ident[:, :])
                last.then_inc(xT_ps, 1)
            pe.wait_ge(xT_sb, NT * KT // 4)
            pe.wait_ge(w_in, 48)
            for b in range(B):
                for i in range(2):
                    if b:
                        pe.wait_ge(first_sb, 2 * b + i - 1)
                    for k in range(KT):
                        last = mm(proj_ps[:, i, :], setup_w[:, i, k, :], hT[:, k, b * T:(b + 1) * T],
                                  start=(k == 0), stop=(k == KT - 1))
                    last.then_inc(first_ps, 1)
            for t in range(NT):
                for k in range(KT):
                    last = mm(work_ps[:, 0, t * H:(t + 1) * H], hT[:, k, t * P:(t + 1) * P], wb_sb[:, k, :],
                              start=(k == 0), stop=(k == KT - 1))
            last.then_inc(first_ps, 1)
            pe.wait_ge(first_sb, 2 * B + 1)
            pe.wait_ge(wo_scaled, 2)

            for s in slots(pe, H, B):
                u1, u2, u3, u4 = s.u1, s.u2, s.u3, s.u4
                if s.edge:
                    done = [min(max(s.n - lag, 0), B * H) for lag in range(4)]
                    for sem_, per, lag in ((conv_step, 12, 0), (fexp_done, 1, 0), (wN_step, 5, 0), (vN_done, 1, 0),
                                           (A_done, 4, 1), (UT_done, 8, 1), (V_step, 18, 1), (max_step, 2, 1),
                                           (aT_done, 1, 2), (mix_done, 12, 2), (oN_done, 1, 2),
                                           (og_done, 1, 3), (acc_done, 2, 3), (tg_done, 1, 3)):
                        wait(pe, sem_, per * done[lag])
                if u3:
                    pe.wait_ge(a_done, u3.count(4, 4))
                    wait(pe, oN_done, u3.count(1, 0))
                    for c in range(C):
                        last = tr(work_ps[:, 0, c * P:(c + 1) * P], aN[:, c * P:(c + 1) * P], ident[:, :])
                    last.then_inc(aT_ps_ready, 1)
                if u2:
                    pe.wait_ge(silu_done, u2.count(4, 3))
                    if u3:
                        pe.wait_ge(a_done, u3.count(4, 4))
                    for c in range(C):
                        if c == 1 and u3:
                            pe.wait_ge(aT_done, u3.count(1, 1))
                        if c >= 2:
                            pe.wait_ge(A_done, u2.count(4, c - 1))
                        mm(work_ps[:, (c + 1) % 2, c * P:T], qk[:, u2.par % 2, 1, c * P:(c + 1) * P],
                           qk[:, u2.par % 2, 0, c * P:T], start=True, stop=True).then_inc(A_ps_ready, 1)
                if u4:
                    pe.wait_ge(head_g, 16 * (u4.h + 1))
                    if u1 and not s.edge:
                        pe.wait_ge(conv_step, u1.count(12, -3))
                    mm(proj_ps[:, 0, :], wg2_head[:, :], g1T[:, u4.par * T:(u4.par + 1) * T], start=True, stop=True)\
                        .then_inc(gate_ps_ready, 1)
                if u1:
                    project(pe, s, 0)
                    pe.wait_ge(head_f, 16 * (u1.h + 1))
                    if u4:
                        pe.wait_ge(tg_done, u4.count(1, 1))
                    mm(proj_ps[:, 0, :], wf2_head[:, :], f1T[:, u1.par * T:(u1.par + 1) * T], start=True, stop=True)\
                        .then_inc(proj_ps_ready, 1)
                if u4:
                    pe.wait_ge(on_done, u4.count(4, 4))
                    if u2:
                        pe.wait_ge(A_done, u2.count(4, 3))
                    for c in range(C):
                        last = tr(work_ps[:, 1, c * P:(c + 1) * P], oN[:, c * P:(c + 1) * P], ident[:, :])
                    last.then_inc(onT_ps_ready, 1)
                if u3:
                    for i in range(3):
                        mix_products(pe, u3, i)
                if u4:
                    pe.wait_ge(og_done, u4.count(1, 1))
                    if u2:
                        pe.wait_ge(A_done, u2.count(4, 4))
                    for c in range(C):
                        last = mm(work_ps[:, c // 2, (c % 2) * HID:(c % 2 + 1) * HID], ogT[:, c * P:(c + 1) * P],
                                  wo_sb[:, bass.ds(u4.h, 1), :].rearrange("p o n -> p (o n)"), start=True, stop=True)
                        if c % 2:
                            last.then_inc(y_ps_ready, 1)
                if u1:
                    project(pe, s, 1)
                if u2:
                    turn_U(pe, u2, 0)
                    turn_U(pe, u2, 1)
                for r in range(LEVELS):
                    if u2:
                        level_scores(pe, u2, r)
                        if r + 2 < LEVELS - 1:
                            turn_U(pe, u2, r + 2)
                    if u3:
                        mix_products(pe, u3, r + 3)
                    if u1 and r == 2:
                        pe.wait_ge(silu_done, u1.count(4, 1))
                        if u4:
                            pe.wait_ge(acc_done, u4.count(2, 1))
                        for c in range(C):
                            last = tr(work_ps[:, 0, c * P:(c + 1) * P], wT[:, u1.par, c * P:(c + 1) * P], ident[:, :])
                        last.then_inc(wT_ps_ready, 1)
                    if u1 and r == 3:
                        project(pe, s, 2)
                    if u1 and r == 6:
                        project(pe, s, 3)
                if u1:
                    pe.wait_ge(silu_done, u1.count(4, 4))
                    if u4:
                        pe.wait_ge(acc_done, u4.count(2, 2))
                    for c in range(C):
                        last = tr(work_ps[:, 1, c * P:(c + 1) * P], conv[:, 1, c * P:(c + 1) * P], ident[:, :])
                    last.then_inc(vT_ps_ready, 1)
                if u3:
                    pe.wait_ge(mix_done, u3.count(12, 12))
                    pe.wait_ge(vN_done, u3.count(1, 1))
                    if u1:
                        pe.wait_ge(wN_step, u1.count(5, 5))
                    for t in range(C):
                        for c in range(t + 1):
                            last = mm(work_ps[:, 0, t * P:(t + 1) * P], A2[:, c, t * P:(t + 1) * P],
                                      vN[:, u3.par, c * P:(c + 1) * P], start=(c == 0), stop=(c == t))
                    last.then_inc(o_ps_ready, 1)
                if u2:
                    pe.wait_ge(sT_done, u2.count(1, 1))
                    if u1:
                        pe.wait_ge(vN_done, u1.count(1, 1))
                    for c in range(C):
                        mm(work_ps[:, 1, c * P:(c + 1) * P], sT[:, c * P:(c + 1) * P], ident[:, :],
                           start=True, stop=False)
                        last = mm(work_ps[:, 1, c * P:(c + 1) * P], A_diag[:, c, :],
                                  wN[:, u2.par % 2, c * P:(c + 1) * P], start=False, stop=True)
                    last.then_inc(s_ps_ready, 1)

            with pe.Fori(0, B) as b:
                pe.wait_ge(ffn["norm"], b * C + C)
                pe.wait_ge(ffn["cast"], 3)
                for k in range(KT):
                    for c in range(C):
                        last = tr(work_ps[:, k, c * P:(c + 1) * P], y[:, c, k * P:(k + 1) * P], ident[:, :])
                    last.then_inc(ffn["yT_ps"], 1)
                pe.wait_ge(ffn["yT_sb"], b * KT + KT)
                for f in range(FT):
                    if f >= 2:
                        pe.wait_ge(ffn["fused"], b * FT + (f - 1))
                    for w, dst in ((wg32, ffn_gate_ps(f)), (wu32, ffn_up_ps(f))):
                        for k in range(KT):
                            last = mm(dst, w[:, k, f * P:(f + 1) * P], yT[:, k, :], start=(k == 0), stop=(k == KT - 1))
                        last.then_inc(ffn["up_ps"], 1)
                pe.wait_ge(ffn["fused"], b * FT + FT)
                for c in range(C):
                    for f in range(FT):
                        last = mm(down_ps(c), fused_tile(f)[:, c * P:(c + 1) * P], wd32[:, f, :],
                                  start=(f == 0), stop=(f == FT - 1))
                    last.then_inc(ffn["down_ps"], 1)

_INS = ["hidden_states", "Wq", "Wk", "Wv", "Ww", "cq", "ck", "cv", "Wf1", "Wf2", "Wb", "Wg1", "Wg2", "bg2", "norm_w",
        "Wo"]
_FFN = ["w_gate", "w_up", "w_down", "s_gate", "s_up", "s_down"]


def kernel(**inputs):
    import numpy as np
    import concourse.bacc as bacc
    from concourse.bass_utils import run_bass_kernel_spmd

    nc = bacc.Bacc("TRN2", target_bir_lowering=False, num_devices=1)
    arrays, args = {}, []
    for name in ["L0_attn_" + n for n in _INS] + ["L0_ffn_" + n for n in _FFN]:
        a = np.ascontiguousarray(inputs[name])
        if a.dtype == np.int8:
            a = a.view(np.int32)
        arrays["in_" + name] = a
        args.append(nc.dram_tensor("in_" + name, a.shape, mybir.dt.from_np(a.dtype), kind="ExternalInput").ap())
    shape = inputs["L0_attn_hidden_states"].shape
    out = nc.dram_tensor("out_x", shape, F32, kind="ExternalOutput").ap()
    build(nc, *args, out)
    r = run_bass_kernel_spmd(nc, [arrays], core_ids=[0])
    return r.results[0]["out_x"]
```

```python
from contextlib import ExitStack

import concourse.bass as bass
from concourse import mybir

F32 = mybir.dt.float32
F32R = mybir.dt.float32r
I8 = mybir.dt.int8
I32 = mybir.dt.int32
U32 = mybir.dt.uint32
ALU = mybir.AluOpType
ACT = mybir.ActivationFunctionType
AX_X = mybir.AxisListType.X

P = 128
LEVELS = 9
IN_CHUNK = 7
NORM_EPS = 1e-6
RMS_EPS = 1e-5
LN_EPS = 1e-5


class Unit:

    def __init__(self, head, off):
        self.head, self.off = head, off
        self.par = off % 4
        self.h = off // 4 if head is None else head + off // 4

    def count(self, per, k):
        if self.head is None:
            return per * self.off + k
        return self.head * (4 * per) + (per * self.off + k)


class Slot:

    def __init__(self, head, off, units):
        def unit(lag):
            if head is None and not 0 <= off - lag < units:
                return None
            return Unit(head, off - lag)

        self.u1, self.u2, self.u3, self.u4 = (unit(lag) for lag in range(4))
        self.edge = head is None
        self.n = off
        self.j = off % 4


def slots(eng, heads, seqs):
    units = heads * seqs
    for n in range(seqs):
        yield Slot(None, n, units)
    with eng.Fori(1, heads) as h:
        for j in range(seqs):
            yield Slot(h, j, units)
    for n in range(units, units + 3):
        yield Slot(None, n, units)


def wait(eng, sem, value):
    if not isinstance(value, int) or value > 0:
        eng.wait_ge(sem, value)


def build(nc, x, Wq, Wk, Wv, Ww, cq, ck, cv, Wf1, Wf2, Wb, Wg1, Wg2, bg2, norm_w, Wo,
          w_gate, w_up, w_down, s_gate, s_up, s_down, out):
    B, T, HID = x.shape
    KW = cq.shape[1]
    H = Wb.shape[1]
    D = norm_w.shape[0]
    INTER = s_gate.shape[0]
    KT = HID // P
    C = T // P
    NT = B * T // P
    FT = INTER // P
    SCALE = float(D) ** -0.5
    SETUP = 2 * KT * P + KT * H
    assert D == P and B == 4 and C == 4 and T == 2 << (LEVELS - 1) and KT == 2 and KW == 4

    with ExitStack() as ctx:
        def sb(name, shape, dt=F32):
            return stacks[-1].enter_context(nc.sbuf_tensor(name, shape, dt))

        def sem(name):
            return ctx.enter_context(nc.semaphore(name))

        proj_ps = ctx.enter_context(nc.psum_tensor("proj_ps", [P, 2, T], F32))
        tr_ps = ctx.enter_context(nc.psum_tensor("tr_ps", [P, T], F32))
        out_ps = ctx.enter_context(nc.psum_tensor("out_ps", [P, T], F32))
        mix_ps = ctx.enter_context(nc.psum_tensor("mix_ps", [P, 2, T], F32))
        work_ps = ctx.enter_context(nc.psum_tensor("work_ps", [P, 2, T], F32))

        stacks = [ctx]

        acc = sb("acc", [P, NT, HID])
        ident = sb("ident", [P, P])
        masks = sb("masks", [P, IN_CHUNK, P // 2])
        consts = sb("consts", [P, 4, C])

        stacks.append(ExitStack())
        setup_raw = sb("setup_raw", [P, SETUP])
        setup_hi_sb = sb("setup_hi_sb", [P, SETUP], F32R)
        setup_lo_sb = sb("setup_lo_sb", [P, SETUP], F32R)
        stacks.pop().close()

        stacks.append(ExitStack())
        U = sb("U", [P, 2, LEVELS - 1, T])
        hT_hi = sb("hT_hi", [P, KT, B * T], F32R)
        hT_lo = sb("hT_lo", [P, KT, B * T], F32R)
        f1T = sb("f1T", [P, B * T])
        g1T = sb("g1T", [P, B * T])
        beta = sb("beta", [P, NT, H])
        coefs = sb("coefs", [P, 3, H, KW])
        bg2_sb = sb("bg2_sb", [P, H])
        w_raw = sb("w_raw", [P, 4, KT, P])
        w_hi = sb("w_hi", [P, 4, KT, P], F32R)
        w_lo = sb("w_lo", [P, 4, KT, P], F32R)
        wo_head = sb("wo_head", [P, HID])
        wf2_head = sb("wf2_head", [P, P])
        wg2_head = sb("wg2_head", [P, P])
        coef = sb("coef", [P, 3, KW])
        coef_v = sb("coef_v", [P, KW])
        gbias = sb("gbias", [P, 1])
        wT = sb("wT", [P, 4, T])
        vN = sb("vN", [P, 4, T])
        gT = sb("gT", [P, 4, T])
        tot = sb("tot", [P, 4, T])
        qk = sb("qk", [P, 2, T])
        wN = sb("wN", [P, 2, T])
        fac = sb("fac", [P, 4, C])
        ssq = sb("ssq", [P, 2, C])
        conv = sb("conv", [P, 3, T])
        th = sb("th", [P, 2, T])
        fexp = sb("fexp", [P, T])
        A = sb("A", [P, C, T])
        A_lev = sb("A_lev", [P, IN_CHUNK, C, P // 2])
        A_diag = sb("A_diag", [P, C, P])
        UT = sb("UT", [P, 2, T])
        V = sb("V", [P, T])
        mx = sb("mx", [P, 2, C])
        aN = sb("aN", [P, T])
        aT = sb("aT", [P, T])
        Z = sb("Z", [P, 4, C])
        W = sb("W", [P, T])
        A2 = sb("A2", [P, C, T])
        oN = sb("oN", [P, T])
        ssqo = sb("ssqo", [P, 2, C])
        rms = sb("rms", [P, 2, C])
        tg = sb("tg", [P, T])

        heads_output = (aN[:, :], fexp[:, :])

        def setup_weights(buf):
            two = buf[:, 0:2 * KT * P].rearrange("p (i k n) -> p i k n", i=2, k=KT)
            return two[:, 0], two[:, 1], buf[:, 2 * KT * P:SETUP].rearrange("p (k n) -> p k n", k=KT)

        stacks.pop().close()
        stacks.append(ctx)
        q8 = sb("q8", [P, 3, KT * INTER // 4], I32)
        wg_r = sb("wg_r", [P, KT, INTER], F32R)
        wu_r = sb("wu_r", [P, KT, INTER], F32R)
        wd_r = sb("wd_r", [P, FT, HID], F32R)
        sg_sb = sb("sg_sb", [P, FT])
        su_sb = sb("su_sb", [P, FT])
        sgu = sb("sgu", [P, FT])
        sd_sb = sb("sd_sb", [P, HID])
        y = sb("y", [P, NT, HID])
        yT_hi = sb("yT_hi", [P, KT, B * T], F32R)
        yT_lo = sb("yT_lo", [P, KT, B * T], F32R)
        gate_th = sb("gate_th", [P, 2, T])
        gate_mid = sb("gate_mid", [P, 2, T])
        fused = sb("fused", [P, 4, T])
        fused_hi = sb("fused_hi", [P, 4, T], F32R)
        fused_lo = sb("fused_lo", [P, 4, T], F32R)
        tick = sb("tick", [P, 1])
        bn = sb("bn", [P, NT, 6])
        mv = sb("mv", [P, NT, 2])
        rs = sb("rs", [P, NT])

        names = ("x_in w_in small_in head_w head_f head_g head_q head_k head_v head_o const_ready mask_ready xT_ps xT_hi xT_lo "
                 "setup_hi setup_lo first_ps first_sb beta_step norm_set wo_scaled high_done low_done coef_set coef_v_set gbias_set "
                 "proj_ps_ready gate_ps_ready wT_ps_ready vT_ps_ready A_ps_ready UT_ps_ready out_ps_ready s_ps_ready "
                 "aT_ps_ready mix_ps_ready o_ps_ready onT_ps_ready y_ps_ready "
                 "conv_step silu_done decay_step U_step V_step max_step mix_done far_done vN_done og_done y_done acc_done "
                 "tap_done tanh_done fexp_done wN_step A_done UT_done a_done aT_done oN_done osq_done on_done tg_done "
                 "fac_step Alev_done sT_done W_step rms_step").split()
        S = {n: sem(n) for n in names}
        (x_in, w_in, small_in, head_w, head_f, head_g, head_q, head_k, head_v, head_o, const_ready, mask_ready, xT_ps,
         xT_hi, xT_lo, setup_hi, setup_lo, first_ps, first_sb, beta_step, norm_set, wo_scaled, high_done, low_done,
         coef_set, coef_v_set, gbias_set,
         proj_ps_ready, gate_ps_ready, wT_ps_ready, vT_ps_ready, A_ps_ready, UT_ps_ready, out_ps_ready, s_ps_ready,
         aT_ps_ready, mix_ps_ready, o_ps_ready, onT_ps_ready, y_ps_ready,
         conv_step, silu_done, decay_step, U_step, V_step, max_step, mix_done, far_done, vN_done, og_done, y_done, acc_done,
         tap_done, tanh_done, fexp_done, wN_step, A_done, UT_done, a_done, aT_done, oN_done, osq_done, on_done, tg_done,
         fac_step, Alev_done, sT_done, W_step, rms_step) = (S[n] for n in names)
        ffn = {n: sem("ffn_" + n) for n in (
            "q_in scale_in cast scales stats var_eps rstd norm yT_ps yT_hi yT_lo up_ps tanh mid fused fused_hi fused_lo "
            "down_ps scaled res stats2 var_eps2 rstd2 done store").split()}

        def pairs(ap, lev):
            return ap.rearrange("p (n e l) -> p n e l", e=2, l=1 << lev)

        def block_tot(par, lev, odd):
            if lev == 0:
                t = gT[:, par, :]
                n = T
            else:
                n = T >> lev
                t = tot[:, par, T - 2 * n:T - n]
            t = t.rearrange("p (n e) -> p n e", e=2)[:, :, odd:odd + 1]
            return t.to_broadcast([P, n // 2, 1 << lev])

        def chunk_sel(buf, lev):
            flat = buf[:, :, :].rearrange("p c t -> p (c t)")
            n = P >> (lev + 1)
            cols = [flat[:, c * (T + P):c * (T + P) + P] for c in range(C)]
            one = cols[0].rearrange("p (n e l) -> p n e l", e=2, l=1 << lev)[:, :, 1, :]
            lead, rest = one.ap[0], list(one.ap[1:])
            return bass.AP(one.tensor, one.offset, [list(lead), [T + P, C]] + [list(r) for r in rest])

        def diag_blocks(buf, c0, nc_):
            flat = buf[:, :, :].rearrange("p c t -> p (c t)")[:, c0 * (T + P):c0 * (T + P) + P]
            return bass.AP(flat.tensor, flat.offset, [list(flat.ap[0]), [T + P, nc_], [1, P]])

        def unused(buf, i):
            return buf[:, 3, i * P:(i + 1) * P] if i < 3 else buf[:, 2, 0:P]

        def mask_sel(lev, dt=F32):
            m = masks[:, lev, :].bitcast(dt) if dt != F32 else masks[:, lev, :]
            one = m.rearrange("p (n l) -> p n l", l=1 << lev)
            return bass.AP(one.tensor, one.offset, [list(one.ap[0]), [0, C]] + [list(r) for r in one.ap[1:]])

        def mix_cols(half, lev):
            return mix_ps[:, half, 0:T // 2].rearrange("p (c n l) -> p c n l", c=C, l=1 << lev)

        def Ulev(u, lev):
            return wT[:, u.par, :] if lev == 0 else U[:, u.par % 2, lev - 1, :]


        def grow_W(pool, u3, lev):
            w = pairs(W[:, :], lev)[:, :, 1, :]
            pool.wait_ge(W_step, u3.count(9, 1 + lev))
            pool.wait_ge(mix_ps_ready, u3.count(12, 3 + lev))
            nc.gpsimd.tensor_tensor(w, w, block_tot(u3.par, lev, 0), ALU.mult).then_inc(W_step, 1)

        def ffn_gate_ps(f):
            return proj_ps[:, f % 2, :]

        def ffn_up_ps(f):
            return mix_ps[:, f % 2, :]

        CONV_BANK = (0, 0, 1, 1)
        CONV_BUF = (0, 1, 0, 2)
        PROJ_AT = (1, 3, 4, 5)
        COEF_OF = (0, 1, 2, 0)

        def filt(i, k):
            return coef_v[:, k:k + 1] if i == 3 else coef[:, COEF_OF[i], k:k + 1]

        def tap(act, u, i):
            if i == 0:
                act.wait_ge(coef_set, u.h + 1)
                wait(act, silu_done, u.count(4, -1))
            if i == 2:
                act.wait_ge(silu_done, u.count(4, 1))
            if i == 3:
                act.wait_ge(coef_v_set, u.h + 1)
                wait(act, vT_ps_ready, u.count(1, 0))
            act.wait_ge(proj_ps_ready, u.count(5, PROJ_AT[i]))
            nc.scalar.activation(conv[:, CONV_BUF[i], :], proj_ps[:, CONV_BANK[i], :], ACT.Copy,
                                 scale=filt(i, KW - 1)).then_inc(tap_done, 1)

        def tanh(act, u, i):
            act.wait_ge(conv_step, u.count(12, 3 * i + 3))
            nc.scalar.activation(th[:, i % 2, :], conv[:, CONV_BUF[i], :], ACT.Tanh, scale=0.5).then_inc(tanh_done, 1)

        def exp_scores(act, u3):
            act.wait_ge(max_step, u3.count(2, 2))
            wait(act, acc_done, u3.count(2, -2))
            for c in range(C):
                nc.scalar.activation(aN[:, c * P:(c + 1) * P], work_ps[:, 1, c * P:(c + 1) * P], ACT.Exp,
                                     bias=mx[:, 1, c:c + 1], scale=SCALE / 4,
                                     accum_out=Z[:, u3.par, c:c + 1]).then_inc(a_done, 1)

        A_BANK = (0, 0, 1, 0)

        def evac_A(act, u2, c):
            act.wait_ge(A_ps_ready, u2.count(4, c + 1))
            nc.scalar.activation(A[:, c, c * P:T], work_ps[:, A_BANK[c], c * P:T], ACT.Copy,
                                 scale=fac[:, u2.par, c:c + 1]).then_inc(A_done, 1)

        def evac_UT(act, u2, i):
            act.wait_ge(UT_ps_ready, u2.count(8, i + 1))
            wait(act, out_ps_ready, u2.count(9, i - 1))
            dst, src = UT[:, i % 2, :], tr_ps[:, :]
            if i == 0:
                dst, src = dst[:, 0:T // 2], src[:, 0:T // 2]
            if i == 1:
                dst, src = (x_.rearrange("p (n e t) -> p n e t", e=2, t=P)[:, :, 0, :] for x_ in (dst, src))
            nc.scalar.activation(dst, src, ACT.Copy).then_inc(UT_done, 1)

        def down_ps(c):
            return (work_ps[:, 0, 0:HID], work_ps[:, 1, 0:HID], tr_ps[:, 0:HID], out_ps[:, 0:HID])[c]

        def attention_stats(dve, b):
            for t in range(b * C, (b + 1) * C):
                nc.vector.bn_stats(bn[:, t, :], acc[:, t, :]).then_inc(ffn["stats"], 1)
            dve.wait_ge(ffn["stats"], 2 * b * C + C)
            nc.vector.memset(tick[:, :], 0.0)
            for t in range(b * C, (b + 1) * C):
                nc.vector.bn_aggr(mv[:, t, :], bn[:, t, :]).then_inc(ffn["stats"], 1)
            dve.wait_ge(ffn["stats"], 2 * (b + 1) * C)
            nc.vector.tensor_scalar(rs[:, b * C:(b + 1) * C].unsqueeze(2), mv[:, b * C:(b + 1) * C, 1:2], LN_EPS, None,
                                    ALU.add).then_inc(ffn["var_eps"], 1)

        def attention_norm(dve, b):
            dve.wait_ge(ffn["rstd"], b + 1)
            for t in range(b * C, (b + 1) * C):
                nc.vector.tensor_scalar(y[:, t, :], acc[:, t, :], mv[:, t, 0:1], rs[:, t:t + 1], ALU.subtract, ALU.mult)\
                    .then_inc(ffn["norm"], 1)

        def lows(dve, b):
            for k in range(KT):
                dve.wait_ge(ffn["yT_hi"], b * KT + k + 1)
                cols = slice(b * T, (b + 1) * T)
                nc.vector.tensor_tensor(yT_lo[:, k, cols], work_ps[:, k, :], yT_hi[:, k, cols].bitcast(F32), ALU.subtract)\
                    .then_inc(ffn["yT_lo"], 1)

        def layer_norm(dve, b):
            def tile(c):
                return acc[:, bass.ds(b * C + c, 1), :].rearrange("p o n -> p (o n)")
            dve.wait_ge(ffn["res"], b * C + C)
            nc.vector.memset(tick[:, :], 0.0)
            for c in range(C):
                nc.vector.bn_stats(bn[:, c, :], tile(c)).then_inc(ffn["stats2"], 1)
            dve.wait_ge(ffn["stats2"], b * 2 * C + C)
            nc.vector.memset(tick[:, :], 0.0)
            for c in range(C):
                nc.vector.bn_aggr(mv[:, c, :], bn[:, c, :]).then_inc(ffn["stats2"], 1)
            dve.wait_ge(ffn["stats2"], b * 2 * C + 2 * C)
            nc.vector.tensor_scalar(rs[:, 0:C].unsqueeze(2), mv[:, 0:C, 1:2], LN_EPS, None, ALU.add)\
                .then_inc(ffn["var_eps2"], 1)
            dve.wait_ge(ffn["rstd2"], b * 1 + 1)
            for c in range(C):
                nc.vector.tensor_scalar(tile(c), tile(c), mv[:, c, 0:1], rs[:, c:c + 1], ALU.subtract, ALU.mult)\
                    .then_inc(ffn["done"], 1)

        def grow_U(dve, u2, lev):
            src, dst = pairs(Ulev(u2, lev), lev), pairs(Ulev(u2, lev + 1), lev)
            if lev == 0:
                dve.wait_ge(silu_done, u2.count(4, 1))
                dve.wait_ge(decay_step, u2.count(12, 5))
                wait(dve, mix_ps_ready, u2.count(12, -12))
            else:
                dve.wait_ge(U_step, u2.count(16, 2 * lev))
                dve.wait_ge(decay_step, u2.count(12, 5 + lev))
            n = T >> (lev + 1) if lev < IN_CHUNK else 1
            nc.vector.tensor_tensor(dst[:, 0:n, 0, :], src[:, 0:n, 0, :], block_tot(u2.par, lev, 1)[:, 0:n], ALU.mult)\
                .then_inc(U_step, 1)
            nc.vector.tensor_copy(dst[:, 0:n, 1, :], src[:, 0:n, 1, :]).then_inc(U_step, 1)

        def conv_tap(dve, u, i, k):
            back = k + 1
            dve.wait_ge(tap_done, u.count(4, i + 1)) if k == 0 else dve.wait_ge(conv_step, u.count(12, 3 * i + k))
            y_ = conv[:, CONV_BUF[i], back:T]
            nc.vector.scalar_tensor_tensor(y_, proj_ps[:, CONV_BANK[i], 0:T - back], filt(i, KW - 1 - back), y_,
                                           ALU.mult, ALU.add).then_inc(conv_step, 1)

        def silu(dve, u, i):
            dst = (wT[:, u.par, :], qk[:, 0, :], qk[:, 1, :], conv[:, 2, :])[i]
            dve.wait_ge(tanh_done, u.count(4, i + 1))
            nc.vector.scalar_tensor_tensor(dst, th[:, i % 2, :], 1.0, conv[:, CONV_BUF[i], :], ALU.add, ALU.mult)\
                .then_inc(silu_done, 1)

        def gates(dve, u1, i):
            if i == 0:
                dve.wait_ge(fexp_done, u1.count(1, 1))
                nc.vector.tensor_scalar(fexp[:, :], fexp[:, :], 1.0, None, ALU.add).then_inc(decay_step, 1)
                return
            dve.wait_ge(decay_step, u1.count(12, 1))
            cols = slice((i - 1) * P, i * P)
            nc.vector.reciprocal(gT[:, u1.par, cols], fexp[:, cols]).then_inc(decay_step, 1)

        def gate_products(dve, u2, lev):
            dve.wait_ge(decay_step, u2.count(12, 4 + lev))
            n = T >> lev
            src = gT[:, u2.par, :] if lev == 1 else tot[:, u2.par, T - 4 * n:T - 2 * n]
            src = src.rearrange("p (n e) -> p n e", e=2)
            nc.vector.tensor_tensor(tot[:, u2.par, T - 2 * n:T - n], src[:, :, 0], src[:, :, 1], ALU.mult)\
                .then_inc(decay_step, 1)

        def values(dve, u2):
            dve.wait_ge(vT_ps_ready, u2.count(1, 1))
            dve.wait_ge(fac_step, u2.count(3, 3))
            fb = fac[:, u2.par, :].unsqueeze(2).to_broadcast([P, C, P])
            nc.vector.tensor_tensor(vN[:, u2.par, :].rearrange("p (c d) -> p c d", c=C),
                                    work_ps[:, 1, :].rearrange("p (c d) -> p c d", c=C), fb, ALU.mult)\
                .then_inc(vN_done, 1)

        def add_heads_output(pool, u4, i):
            pool.wait_ge(y_done, u4.count(2, i + 1))
            a = acc[:, u4.par * C + 2 * i:u4.par * C + 2 * i + 2, :]
            nc.gpsimd.tensor_tensor(a, a, heads_output[i].rearrange("p (c n) -> p c n", c=2), ALU.add)\
                .then_inc(acc_done, 1)

        def descend(dve, u2, r):
            lev = LEVELS - 1 - r
            new = out_ps[:, 0:T // 2]
            if r == 0:
                wait(dve, s_ps_ready, u2.count(1, 0))
                nc.vector.memset(V[:, 0:T // 2], 0.0).then_inc(V_step, 1)
                dve.wait_ge(out_ps_ready, u2.count(9, 1))
                nc.vector.tensor_copy(V[:, T // 2:T], new).then_inc(V_step, 1)
                return
            v = pairs(V[:, :], lev)[:, :, 1, :]
            dve.wait_ge(V_step, u2.count(18, 2 * r))
            nc.vector.tensor_tensor(v, v, block_tot(u2.par, lev, 0), ALU.mult).then_inc(V_step, 1)
            dve.wait_ge(V_step, u2.count(18, 2 * r + 1))
            dve.wait_ge(out_ps_ready, u2.count(9, r + 1))
            nc.vector.tensor_tensor(v, v, new.rearrange("p (n l) -> p n l", l=1 << lev), ALU.add).then_inc(V_step, 1)

        def mixable(dve, s, i):
            if not s.u2 or i == 2:
                wait(dve, mix_done, s.u3.count(9, i))
            if i == 0:
                wait(dve, o_ps_ready, s.u3.count(1, 0))
            dve.wait_ge(mix_ps_ready, s.u3.count(12, i + 1))

        def mix(dve, u3, i):
            half = i % 2
            if i < 2:
                idb = ident[:, :].bitcast(U32).unsqueeze(1).to_broadcast([P, 2, P])
                ins = nc.vector.copy_predicated(diag_blocks(A2, 2 * i, 2), idb,
                                                mix_ps[:, half, 0:T // 2].rearrange("p (c t) -> p c t", c=2))
            else:
                lev = i - 2
                ins = nc.vector.copy_predicated(chunk_sel(A2, lev), mask_sel(lev, U32), mix_cols(half, lev))
            ins.then_inc(mix_done, 1)

        def mix_far(act, u3, i):
            half = i % 2
            act.wait_ge(mix_ps_ready, u3.count(12, i + 1))
            if i == 9:
                for p_ in range(2):
                    ins = nc.scalar.activation(A2[:, 2 * p_, (2 * p_ + 1) * P:(2 * p_ + 2) * P],
                                               mix_ps[:, half, p_ * P:(p_ + 1) * P], ACT.Copy)
            else:
                ins = nc.scalar.activation(A2[:, i - 10, T // 2:T], mix_ps[:, half, 0:T // 2], ACT.Copy)
            ins.then_inc(far_done, 1)

        def split_product(dst, wh, wl, xh, xl):
            parts = [(wh, xh), (wh, xl), (wl, xh)]
            for k in range(KT):
                for n, (w, x_) in enumerate(parts):
                    last = nc.tensor.matmul(dst, w[:, k, :], x_(k),
                                            start=(k == 0 and n == 0), stop=(k == KT - 1 and n == 2))
            return last

        def project(pe, s, i):
            u1 = s.u1
            pe.wait_ge(low_done, 2 * u1.h + (2 if i == 3 else 1))
            if i == 0:
                if s.u4:
                    pe.wait_ge(tg_done, s.u4.count(1, 1))
            elif i == 1:
                pe.wait_ge(conv_step, u1.count(12, 3))
            elif i == 2:
                pe.wait_ge(fexp_done, u1.count(1, 1))
            else:
                pe.wait_ge(conv_step, u1.count(12, 9))
            cols = slice(u1.par * T, (u1.par + 1) * T)
            last = split_product(proj_ps[:, CONV_BANK[i], :], w_hi[:, i], w_lo[:, i],
                                 lambda k: hT_hi[:, k, cols], lambda k: hT_lo[:, k, cols])
            last.then_inc(proj_ps_ready, 1)

        def even_chunks(lev):
            return (0, 1) if lev == LEVELS - 1 else (0, 2) if lev == IN_CHUNK else range(C)

        def turn_U(pe, u2, i):
            lev = LEVELS - 1 - i
            pe.wait_ge(U_step, u2.count(16, 2 * lev))
            wait(pe, UT_done, u2.count(8, i))
            for c in even_chunks(lev):
                last = nc.tensor.transpose(tr_ps[:, c * P:(c + 1) * P], Ulev(u2, lev)[:, c * P:(c + 1) * P],
                                           ident[:, :])
            last.then_inc(UT_ps_ready, 1)

        def level_scores(pe, u2, r):
            lev = LEVELS - 1 - r
            dst = out_ps[:, 0:T // 2]
            wait(pe, V_step, u2.count(18, 2 * r))
            if lev:
                pe.wait_ge(UT_done, u2.count(8, r + 1))
            else:
                pe.wait_ge(wN_step, u2.count(5, 5))
            ut = UT[:, r % 2, :] if lev else wN[:, u2.par % 2, :]
            if lev == 8:
                for c in range(2):
                    last = nc.tensor.matmul(dst, ut[:, c * P:(c + 1) * P], A[:, c, T // 2:T], start=(c == 0), stop=(c == 1))
            elif lev == 7:
                for c in (0, 2):
                    last = nc.tensor.matmul(dst[:, c * P // 2:(c + 2) * P // 2], ut[:, c * P:(c + 1) * P],
                                            A[:, c, (c + 1) * P:(c + 2) * P], start=True, stop=True)
            else:
                pe.wait_ge(Alev_done, u2.count(8, 1 + (IN_CHUNK - 1 - lev)))
                for c in range(C):
                    last = nc.tensor.matmul(dst[:, c * P // 2:(c + 1) * P // 2], ut[:, c * P:(c + 1) * P],
                                            A_lev[:, lev, c, :], start=True, stop=True)
            last.then_inc(out_ps_ready, 1)

        def mix_products(pe, u3, i):
            half = i % 2
            if i == 0 or i == 1:
                wait(pe, far_done, u3.count(3, i - 1))
            elif i == 11:
                pe.wait_ge(far_done, u3.count(3, 1))
            else:
                pe.wait_ge(mix_done, u3.count(9, i - 1))
            if i < 2:
                for c in (2 * i, 2 * i + 1):
                    last = nc.tensor.matmul(mix_ps[:, half, (c % 2) * P:(c % 2 + 1) * P], wT[:, u3.par, c * P:(c + 1) * P],
                                            aT[:, c * P:(c + 1) * P], start=True, stop=True)
            else:
                lev = min(i - 2, LEVELS - 1)
                pe.wait_ge(W_step, u3.count(9, 1 + lev))
                ul = Ulev(u3, lev)
                if lev < IN_CHUNK:
                    for c in range(C):
                        t_sel = pairs(W[:, c * P:(c + 1) * P], lev)[:, :, 1, :]
                        last = nc.tensor.matmul(mix_ps[:, half, c * P // 2:(c + 1) * P // 2], ul[:, c * P:(c + 1) * P],
                                                t_sel, start=True, stop=True)
                elif lev == 7:
                    for c in (0, 2):
                        last = nc.tensor.matmul(mix_ps[:, half, c * P // 2:(c + 2) * P // 2], ul[:, c * P:(c + 1) * P],
                                                W[:, (c + 1) * P:(c + 2) * P], start=True, stop=True)
                else:
                    c = i - 10
                    last = nc.tensor.matmul(mix_ps[:, half, 0:T // 2], ul[:, c * P:(c + 1) * P], W[:, T // 2:T],
                                            start=True, stop=True)
            last.then_inc(mix_ps_ready, 1)

        def key_query(pe, u2, c):
            nc.tensor.matmul(work_ps[:, A_BANK[c], c * P:T], qk[:, 1, c * P:(c + 1) * P],
                             qk[:, 0, c * P:T], start=True, stop=True).then_inc(A_ps_ready, 1)

        def turn(bank, src):
            for c in range(C):
                last = nc.tensor.transpose(work_ps[:, bank, c * P:(c + 1) * P], src[:, c * P:(c + 1) * P], ident[:, :])
            return last

        block = ctx.enter_context(nc.Block())

        @block.sync
        def _(sp):
            nc.sync.dma_start(acc[:, :, :], x.rearrange("b (c p) n -> p (b c) n", p=P)).then_inc(x_in, 16)
            wf1_raw, wg1_raw, wb_raw = setup_weights(setup_raw)
            nc.sync.dma_start(wf1_raw, Wf1.rearrange("(k p) n -> p k n", p=P)).then_inc(w_in, 16)
            nc.sync.dma_start(wg1_raw, Wg1.rearrange("(k p) n -> p k n", p=P)).then_inc(w_in, 16)
            nc.sync.dma_start(wb_raw, Wb.rearrange("(k p) n -> p k n", p=P)).then_inc(w_in, 16)
            for i, c in enumerate((cv, cq, ck)):
                nc.sync.dma_start(coefs[:, i], c.rearrange("(h p) w -> p h w", p=P)).then_inc(small_in, 16)
            with nc.allow_non_contiguous_dma(reason="a few hundred words, once"):
                nc.sync.dma_start(bg2_sb[:, :], bg2.rearrange("(h p) -> p h", p=P)).then_inc(small_in, 16)
                nc.sync.dma_start(consts[:, 3, 0:1], norm_w.rearrange("(p o) -> p o", o=1)).then_inc(small_in, 16)

            def head_cols(w, h):
                return w[:, bass.ts(h, P)].rearrange("(k p) n -> p k n", p=P)

            def load_head(h, first):
                before = None if first else Unit(h, -1)
                for i, (w, landed) in enumerate(((Ww, head_w), (None, head_f), (Wq, head_q), (Wk, head_k),
                                                 (Wv, head_v))):
                    if before is not None:
                        sp.wait_ge(proj_ps_ready, before.count(5, i + 1))
                    if w is None:
                        nc.sync.dma_start(wf2_head[:, :], Wf2[:, bass.ts(h, P)]).then_inc(landed, 16)
                    else:
                        slot = i if i == 0 else i - 1
                        nc.sync.dma_start(w_raw[:, slot], head_cols(w, h)).then_inc(landed, 16)

            def load_gate(h, first):
                if not first:
                    sp.wait_ge(gate_ps_ready, Unit(h, 0).count(1, 0))
                nc.sync.dma_start(wg2_head[:, :], Wg2[:, bass.ts(h, P)]).then_inc(head_g, 16)

            def load_out(h, first):
                if not first:
                    sp.wait_ge(y_ps_ready, Unit(h, 0).count(2, 0))
                nc.sync.dma_start(wo_head[:, :], Wo[bass.ts(h, P), :]).then_inc(head_o, 16)

            load_head(0, True)
            load_gate(0, True)
            load_out(0, True)
            with sp.Fori(1, H) as h:
                load_head(h, False)
                load_gate(h, False)
                load_out(h, False)

            sp.wait_ge(acc_done, 2 * B * H)
            for i, (w, tiles) in enumerate(((w_gate, KT), (w_up, KT), (w_down, FT))):
                nc.sync.dma_start(q8[:, i, :].rearrange("p (k n) -> p k n", k=tiles), w.rearrange("(k p) n -> p k n", p=P))\
                    .then_inc(ffn["q_in"], 16)
            with nc.allow_non_contiguous_dma(reason="a few hundred words, once"):
                nc.sync.dma_start(sg_sb[:, :], s_gate.rearrange("(f p) -> p f", p=P)).then_inc(ffn["scale_in"], 16)
                nc.sync.dma_start(su_sb[:, :], s_up.rearrange("(f p) -> p f", p=P)).then_inc(ffn["scale_in"], 16)
            nc.sync.dma_start(sd_sb[:, :], s_down.rearrange("(o n) -> o n", o=1).to_broadcast([P, HID])).then_inc(ffn["scale_in"], 16)

            out_v = out.rearrange("b (c p) n -> p (b c) n", p=P)
            with sp.Fori(0, B) as b:
                sp.wait_ge(ffn["done"], b * C + C)
                nc.sync.dma_start(out_v[:, bass.ts(b, C), :], acc[:, bass.ts(b, C), :]).then_inc(ffn["store"], 16)
            sp.wait_ge(ffn["store"], 16 * B)

        @block.gpsimd
        def _(pool):
            nc.gpsimd.memset(ident[:, :], 0.0).then_inc(mask_ready, 1)
            nc.gpsimd.memset(masks[:, :, :], 1.0).then_inc(mask_ready, 1)
            nc.gpsimd.memset(A2[:, :, :], 0.0).then_inc(const_ready, 1)
            nc.gpsimd.memset(consts[:, 0, :], 4.0 * NORM_EPS).then_inc(const_ready, 1)
            nc.gpsimd.memset(consts[:, 1, :], -0.5).then_inc(const_ready, 1)
            nc.gpsimd.memset(consts[:, 2, :], 4.0 * D * RMS_EPS).then_inc(const_ready, 1)
            pool.wait_ge(mask_ready, 2)
            nc.gpsimd.affine_select(out=ident[:, :], in_=ident[:, :], compare_op=ALU.not_equal, fill=1.0, base=0,
                                    pattern=[[-1, P]], channel_multiplier=1).then_inc(mask_ready, 1)
            for lev in range(IN_CHUNK):
                L = 1 << lev
                m = masks[:, lev, :].rearrange("p (n l) -> p n l", l=L)
                nc.gpsimd.affine_select(out=m, in_=m, compare_op=ALU.is_ge, fill=0.0, base=0,
                                        pattern=[[-2 * L, P // 2 // L], [0, L]], channel_multiplier=1)\
                    .then_inc(mask_ready, 1)
                pool.wait_ge(mask_ready, 4 + 2 * lev)
                nc.gpsimd.affine_select(out=m, in_=m, compare_op=ALU.is_ge, fill=0.0, base=L - 1,
                                        pattern=[[2 * L, P // 2 // L], [0, L]], channel_multiplier=-1)\
                    .then_inc(mask_ready, 1)
            pool.wait_ge(mask_ready, 3 + 2 * IN_CHUNK)
            pool.wait_ge(const_ready, 4)

            for s in slots(pool, H, B):
                u1, u2, u3, u4 = s.u1, s.u2, s.u3, s.u4
                if u1 and s.j == 0:
                    pool.wait_ge(high_done, 2 * u1.h + 1)
                    nc.gpsimd.tensor_tensor(w_lo[:, 0:3], w_raw[:, 0:3], w_hi[:, 0:3].bitcast(F32), ALU.subtract)\
                        .then_inc(low_done, 1)
                if u3:
                    pool.wait_ge(aT_done, u3.count(1, 1))
                    pool.wait_ge(decay_step, u3.count(12, 12))
                    wait(pool, mix_ps_ready, u3.count(12, 0))
                    nc.gpsimd.tensor_tensor(W[:, :], aT[:, :], gT[:, u3.par, :], ALU.mult).then_inc(W_step, 1)
                if u2:
                    wait(pool, out_ps_ready, u2.count(9, 0))
                    pool.wait_ge(A_done, u2.count(4, 4))
                for i in range(IN_CHUNK):
                    lev = IN_CHUNK - 1 - i
                    if u2:
                        dst = A_lev[:, lev].rearrange("p c (n l) -> p c n l", l=1 << lev)
                        nc.gpsimd.tensor_tensor(dst, chunk_sel(A, lev), mask_sel(lev), ALU.mult)\
                            .then_inc(Alev_done, 1)
                    if u3:
                        grow_W(pool, u3, i)
                    if u4 and i == 1:
                        r = rms[:, u4.par % 2, :]
                        z = Z[:, u4.par, :]
                        wait(pool, on_done, u4.count(4, -4))
                        pool.wait_ge(a_done, u4.count(4, 4))
                        nc.gpsimd.tensor_tensor(r, z, z, ALU.mult).then_inc(rms_step, 1)
                        pool.wait_ge(rms_step, u4.count(4, 1))
                        nc.gpsimd.tensor_tensor(r, r, consts[:, 2, :], ALU.mult).then_inc(rms_step, 1)
                        pool.wait_ge(rms_step, u4.count(4, 2))
                        pool.wait_ge(osq_done, u4.count(4, 4))
                        nc.gpsimd.tensor_tensor(r, r, ssqo[:, u4.par % 2, :], ALU.add).then_inc(rms_step, 1)
                        pool.wait_ge(rms_step, u4.count(4, 3))
                        nc.gpsimd.tensor_tensor(r, r, consts[:, 1, :], ALU.pow).then_inc(rms_step, 1)
                if u1 and s.j == 0:
                    pool.wait_ge(high_done, 2 * u1.h + 2)
                    nc.gpsimd.tensor_tensor(w_lo[:, 3], w_raw[:, 3], w_hi[:, 3].bitcast(F32), ALU.subtract)\
                        .then_inc(low_done, 1)
                if u1:
                    f = fac[:, u1.par, :]
                    pool.wait_ge(wN_step, u1.count(5, 4))
                    nc.gpsimd.tensor_tensor(f, ssq[:, u1.par % 2, :], consts[:, 0, :], ALU.add).then_inc(fac_step, 1)
                    pool.wait_ge(fac_step, u1.count(3, 1))
                    nc.gpsimd.tensor_tensor(f, f, consts[:, 1, :], ALU.pow).then_inc(fac_step, 1)
                if u3:
                    grow_W(pool, u3, IN_CHUNK)
                if u2:
                    wait(pool, s_ps_ready, u2.count(1, 0))
                    idb = ident[:, :].unsqueeze(1).to_broadcast([P, C, P])
                    nc.gpsimd.tensor_tensor(A_diag[:, :, :], diag_blocks(A, 0, C), idb, ALU.mult).then_inc(Alev_done, 1)
                if u4:
                    add_heads_output(pool, u4, 0)
                    add_heads_output(pool, u4, 1)
                if u1:
                    pool.wait_ge(fac_step, u1.count(3, 2))
                    if s.n == 0 and s.edge:
                        pool.wait_ge(beta_step, 1 + NT)
                    bt = beta[:, u1.par * C:(u1.par + 1) * C, bass.ds(u1.h, 1)].rearrange("p c o -> p (c o)")
                    nc.gpsimd.tensor_tensor(f, f, bt, ALU.mult).then_inc(fac_step, 1)
            for b in range(B):
                pool.wait_ge(ffn["var_eps"], b + 1)
                r = rs[:, b * C:(b + 1) * C]
                nc.gpsimd.tensor_tensor(r, r, consts[:, 1, :], ALU.pow).then_inc(ffn["rstd"], 1)
            with pool.Fori(0, B) as b:
                for f in range(FT):
                    pool.wait_ge(ffn["fused_hi"], b * FT + (f + 1))
                    nc.gpsimd.tensor_tensor(fused_lo[:, f % 4, :], fused[:, f % 4, :], fused_hi[:, f % 4, :].bitcast(F32),
                                            ALU.subtract).then_inc(ffn["fused_lo"], 1)
                pool.wait_ge(ffn["var_eps2"], b * 1 + 1)
                nc.gpsimd.tensor_tensor(rs[:, 0:C], rs[:, 0:C], consts[:, 1, :], ALU.pow).then_inc(ffn["rstd2"], 1)

        @block.scalar
        def _(act):
            for g in range(NT * KT // 4):
                act.wait_ge(xT_ps, g + 1)
                k, t0 = g // (NT // 4), (g % (NT // 4)) * T
                nc.scalar.activation(hT_hi[:, k, t0:t0 + T], work_ps[:, g % 2, :], ACT.Copy).then_inc(xT_hi, 1)
            act.wait_ge(w_in, 48)
            nc.scalar.activation(setup_hi_sb[:, :], setup_raw[:, :], ACT.Copy).then_inc(setup_hi, 1)
            for b in range(B):
                for i, dst in enumerate((f1T, g1T)):
                    act.wait_ge(first_ps, 2 * b + i + 1)
                    nc.scalar.activation(dst[:, b * T:(b + 1) * T], proj_ps[:, i, :], ACT.Copy).then_inc(first_sb, 1)
            act.wait_ge(first_ps, 2 * B + 1)
            nc.scalar.activation(beta[:, :, :].rearrange("p t h -> p (t h)"), work_ps[:, 0, 0:NT * H], ACT.Exp,
                                 scale=-1.0).then_inc(first_sb, 1)
            act.wait_ge(small_in, 16 * 5)
            nc.scalar.activation(bg2_sb[:, :], bg2_sb[:, :], ACT.Copy, scale=0.5).then_inc(gbias_set, 1)

            for s in slots(act, H, B):
                u1, u2, u3, u4 = s.u1, s.u2, s.u3, s.u4
                if u2:
                    tap(act, u2, 3)
                if u1 and s.j == 0:
                    for landed in (head_w, head_q, head_k):
                        act.wait_ge(landed, 16 * (u1.h + 1))
                    nc.scalar.activation(w_hi[:, 0:3], w_raw[:, 0:3], ACT.Copy).then_inc(high_done, 1)
                if u3:
                    exp_scores(act, u3)
                if u4:
                    act.wait_ge(o_ps_ready, u4.count(1, 1))
                    wait(act, onT_ps_ready, u4.count(1, 0))
                    nc.scalar.activation(oN[:, :], work_ps[:, 0, :], ACT.Copy).then_inc(oN_done, 1)
                if u4:
                    if u4.par == 0:
                        nc.scalar.activation(gbias[:, :], bg2_sb[:, bass.ds(u4.h, 1)], ACT.Copy)\
                            .then_inc(gbias_set, 1)
                    act.wait_ge(gbias_set, 2 + u4.h)
                    act.wait_ge(gate_ps_ready, u4.count(1, 1))
                    wait(act, y_ps_ready, u4.count(2, 0))
                    nc.scalar.activation(tg[:, :], proj_ps[:, 0, :], ACT.Tanh, bias=gbias[:, 0:1], scale=0.5)\
                        .then_inc(tg_done, 1)
                if u3:
                    act.wait_ge(aT_ps_ready, u3.count(1, 1))
                    wait(act, W_step, u3.count(9, -8))
                    wait(act, mix_ps_ready, u3.count(12, -10))
                    nc.scalar.activation(aT[:, :], work_ps[:, 1, :], ACT.Copy).then_inc(aT_done, 1)
                if u2:
                    wait(act, out_ps_ready, u2.count(9, 0))
                    wait(act, Alev_done, u2.count(8, 0))
                    act.wait_ge(fac_step, u2.count(3, 3))
                    for c in range(C):
                        evac_A(act, u2, c)
                if u1:
                    tap(act, u1, 0)
                if u2:
                    tanh(act, u2, 3)
                if u2:
                    evac_UT(act, u2, 0)
                if u1:
                    act.wait_ge(proj_ps_ready, u1.count(5, 2))
                    wait(act, decay_step, u1.count(12, -7))
                    wait(act, acc_done, u1.count(2, -6))
                    nc.scalar.activation(fexp[:, :], proj_ps[:, 1, :], ACT.Exp, scale=-1.0).then_inc(fexp_done, 1)
                if u2:
                    evac_UT(act, u2, 1)
                if u4:
                    act.wait_ge(oN_done, u4.count(1, 1))
                    for c in range(C):
                        nc.scalar.activation(unused(A2, c), oN[:, c * P:(c + 1) * P], ACT.Square,
                                             accum_out=ssqo[:, u4.par % 2, c:c + 1]).then_inc(osq_done, 1)
                for r in range(LEVELS):
                    if u1 and r == 2:
                        tap(act, u1, 1)
                    if u1 and r == 4:
                        act.wait_ge(wT_ps_ready, u1.count(1, 1))
                        for c in range(C):
                            nc.scalar.activation(unused(A, c), work_ps[:, 0, c * P:(c + 1) * P], ACT.Square,
                                                 accum_out=ssq[:, u1.par % 2, c:c + 1]).then_inc(wN_step, 1)
                        nc.scalar.activation(wN[:, u1.par % 2, :], work_ps[:, 0, :], ACT.Copy).then_inc(wN_step, 1)
                    if u2 and r + 2 < LEVELS - 1:
                        evac_UT(act, u2, r + 2)
                    if u1 and r == 1:
                        tanh(act, u1, 0)
                    if u4 and r == 2:
                        act.wait_ge(rms_step, u4.count(4, 4))
                        for c in range(C):
                            nc.scalar.activation(oN[:, c * P:(c + 1) * P], oN[:, c * P:(c + 1) * P], ACT.Copy,
                                                 scale=rms[:, u4.par % 2, c:c + 1]).then_inc(on_done, 1)
                    if u1 and s.j == 0 and r == 3:
                        act.wait_ge(head_v, 16 * (u1.h + 1))
                        nc.scalar.activation(w_hi[:, 3], w_raw[:, 3], ACT.Copy).then_inc(high_done, 1)
                    if u4 and u4.par == 0 and r == 3:
                        act.wait_ge(norm_set, 1)
                        act.wait_ge(head_o, 16 * (u4.h + 1))
                        nc.scalar.activation(wo_head[:, :], wo_head[:, :], ACT.Copy, scale=consts[:, 3, 0:1])\
                            .then_inc(wo_scaled, 1)
                    if u1 and r == 4:
                        tanh(act, u1, 1)
                    if u1 and r == 5:
                        tap(act, u1, 2)
                    if u3 and r >= 7:
                        mix_far(act, u3, r + 2)
                    if u4 and r == 8:
                        if u1:
                            act.wait_ge(decay_step, u1.count(12, 5))
                        for i in range(2):
                            act.wait_ge(y_ps_ready, u4.count(2, i + 1))
                            nc.scalar.activation(heads_output[i], work_ps[:, i, :], ACT.Copy).then_inc(y_done, 1)
                    if u1 and r == 8:
                        tanh(act, u1, 2)
                if u3:
                    mix_far(act, u3, LEVELS + 2)
            act.wait_ge(ffn["q_in"], 48)
            for i, dst in enumerate((wg_r, wu_r, wd_r)):
                nc.scalar.activation(dst.rearrange("p k n -> p (k n)"), q8[:, i, :].bitcast(I8),
                                     ACT.Copy).then_inc(ffn["cast"], 1)
            for b in range(B):
                for k in range(KT):
                    act.wait_ge(ffn["yT_ps"], b * KT + (k + 1))
                    nc.scalar.activation(yT_hi[:, k, b * T:(b + 1) * T], work_ps[:, k, :], ACT.Copy)\
                        .then_inc(ffn["yT_hi"], 1)
            act.wait_ge(ffn["scales"], 2)

            def high(b, f):
                act.wait_ge(ffn["fused"], b * FT + (f + 1))
                if f >= 4:
                    act.wait_ge(ffn["down_ps"], b * FT + (f - 3))
                nc.scalar.activation(fused_hi[:, f % 4, :], fused[:, f % 4, :], ACT.Copy).then_inc(ffn["fused_hi"], 1)

            with act.Fori(0, B) as b:
                for f in range(FT):
                    act.wait_ge(ffn["up_ps"], b * 2 * FT + (2 * f + 1))
                    if f >= 2:
                        act.wait_ge(ffn["mid"], b * FT + (f - 1))
                    nc.scalar.activation(gate_th[:, f % 2, :], ffn_gate_ps(f), ACT.Tanh, scale=sg_sb[:, f:f + 1])\
                        .then_inc(ffn["tanh"], 1)
                    if f:
                        high(b, f - 1)
                high(b, FT - 1)

        @block.vector
        def _(dve):
            for g in range(NT * KT // 4):
                k, t0 = g // (NT // 4), (g % (NT // 4)) * T
                dve.wait_ge(xT_hi, g + 1)
                nc.vector.tensor_tensor(hT_lo[:, k, t0:t0 + T], work_ps[:, g % 2, :],
                                        hT_hi[:, k, t0:t0 + T].bitcast(F32),
                                        ALU.subtract).then_inc(xT_lo, 1)
            dve.wait_ge(setup_hi, 1)
            nc.vector.tensor_tensor(setup_lo_sb[:, :], setup_raw[:, :], setup_hi_sb[:, :].bitcast(F32), ALU.subtract).then_inc(setup_lo, 1)
            dve.wait_ge(small_in, 16 * 5)
            nc.vector.tensor_scalar(consts[:, 3, 0:1], consts[:, 3, 0:1], 0.5 * float(D) ** 0.5, None, ALU.mult)\
                .then_inc(norm_set, 1)
            dve.wait_ge(first_sb, 2 * B + 1)
            bflat = beta[:, :, :].rearrange("p t h -> p (t h)")
            nc.vector.tensor_scalar(bflat, bflat, 1.0, None, ALU.add).then_inc(beta_step, 1)
            dve.wait_ge(beta_step, 1)
            for t in range(NT):
                nc.vector.reciprocal(beta[:, t, :], beta[:, t, :]).then_inc(beta_step, 1)
            dve.wait_ge(mask_ready, 3 + 2 * IN_CHUNK)
            dve.wait_ge(const_ready, 4)

            for s in slots(dve, H, B):
                u1, u2, u3, u4 = s.u1, s.u2, s.u3, s.u4
                if u1 and s.j == 0:
                    wait(dve, tap_done, u1.count(4, -1))
                    nc.vector.tensor_copy(coef[:, :, :], coefs[:, :, bass.ds(u1.h, 1), :].rearrange("p i o w -> p i (o w)"))\
                        .then_inc(coef_set, 1)
                if u3:
                    dve.wait_ge(s_ps_ready, u3.count(1, 1))
                    wait(dve, a_done, u3.count(4, 0))
                    nc.vector.reduce_max(mx[:, 0, :], work_ps[:, 1, :].rearrange("p (c m) -> p c m", c=C), AX_X)\
                        .then_inc(max_step, 1)
                    dve.wait_ge(max_step, u3.count(2, 1))
                    nc.vector.tensor_scalar(mx[:, 1, :], mx[:, 0, :], -SCALE / 4, None, ALU.mult).then_inc(max_step, 1)
                if u2:
                    gate_products(dve, u2, 1)
                for lev in range(LEVELS - 1):
                    if u3 and lev >= 6:
                        mixable(dve, s, lev - 6)
                    if u2:
                        grow_U(dve, u2, lev)
                        if lev + 2 < LEVELS - 1:
                            gate_products(dve, u2, lev + 2)
                    if u2 and lev in (1, 3, 7):
                        conv_tap(dve, u2, 3, (1, 3, 7).index(lev))
                    if u3 and lev >= 6:
                        mix(dve, u3, lev - 6)
                if u1 and s.j == 0:
                    dve.wait_ge(coef_set, u1.h + 1)
                if u1:
                    conv_tap(dve, u1, 0, 0)
                if u2:
                    silu(dve, u2, 3)
                if u1:
                    conv_tap(dve, u1, 0, 1)
                    conv_tap(dve, u1, 0, 2)
                if u1 and s.j == 0:
                    nc.vector.tensor_copy(coef_v[:, :], coefs[:, 0, bass.ds(u1.h, 1), :].rearrange("p o w -> p (o w)"))\
                        .then_inc(coef_v_set, 1)
                for r in range(LEVELS):
                    if u3 and r < IN_CHUNK:
                        mixable(dve, s, r + 2)
                    if u2:
                        descend(dve, u2, r)
                    if u3 and r < IN_CHUNK:
                        mix(dve, u3, r + 2)
                    if u1 and r == 0:
                        gates(dve, u1, 0)
                        gates(dve, u1, 1)
                    if u1 and r == 1:
                        gates(dve, u1, 2)
                    if u1 and r == 2:
                        silu(dve, u1, 0)
                    if u2 and r == 2:
                        values(dve, u2)
                    if u1 and r == 2:
                        conv_tap(dve, u1, 1, 0)
                    if u1 and r == 3:
                        conv_tap(dve, u1, 1, 1)
                        conv_tap(dve, u1, 1, 2)
                    if u4 and r == 4:
                        dve.wait_ge(tg_done, u4.count(1, 1))
                        dve.wait_ge(onT_ps_ready, u4.count(1, 1))
                        wait(dve, y_ps_ready, u4.count(2, 0))
                        nc.vector.scalar_tensor_tensor(tg[:, :], tg[:, :], 1.0, work_ps[:, 1, :], ALU.add, ALU.mult)\
                            .then_inc(og_done, 1)
                    if u1 and r == 4:
                        gates(dve, u1, 3)
                    if u1 and r == 5:
                        gates(dve, u1, 4)
                        silu(dve, u1, 1)
                    if u1 and r == 6:
                        conv_tap(dve, u1, 2, 0)
                        conv_tap(dve, u1, 2, 1)
                    if u1 and r == 7:
                        conv_tap(dve, u1, 2, 2)
                if u2:
                    dve.wait_ge(V_step, u2.count(18, 18))
                    nc.vector.tensor_tensor(V[:, :], V[:, :], gT[:, u2.par, :], ALU.mult).then_inc(sT_done, 1)
                if u1:
                    silu(dve, u1, 2)

            dve.wait_ge(acc_done, 2 * B * H)
            dve.wait_ge(ffn["scale_in"], 48)
            nc.vector.tensor_tensor(sgu[:, :], sg_sb[:, :], su_sb[:, :], ALU.mult).then_inc(ffn["scales"], 1)
            nc.vector.tensor_scalar(sg_sb[:, :], sg_sb[:, :], 0.5, None, ALU.mult).then_inc(ffn["scales"], 1)
            nc.vector.memset(tick[:, :], 0.0).then_inc(ffn["scaled"], C)
            for b in range(B + 2):
                if b < B:
                    attention_stats(dve, b)
                if 1 <= b <= B:
                    attention_norm(dve, b - 1)
                if b >= 2:
                    lows(dve, b - 2)
            with dve.Fori(0, B) as b:
                for f in range(FT):
                    dve.wait_ge(ffn["tanh"], b * FT + (f + 1))
                    m = gate_mid[:, f % 2, :]
                    nc.vector.scalar_tensor_tensor(m, gate_th[:, f % 2, :], 1.0, ffn_gate_ps(f), ALU.add, ALU.mult)\
                        .then_inc(ffn["mid"], 1)
                    dve.wait_ge(ffn["mid"], b * FT + (f + 1))
                    dve.wait_ge(ffn["up_ps"], b * 2 * FT + (2 * f + 2))
                    if f >= 4:
                        dve.wait_ge(ffn["fused_lo"], b * FT + (f - 3))
                    nc.vector.scalar_tensor_tensor(fused[:, f % 4, :], m, sgu[:, f:f + 1], ffn_up_ps(f), ALU.mult, ALU.mult)\
                        .then_inc(ffn["fused"], 1)
                for c in range(C):
                    dve.wait_ge(ffn["down_ps"], b * FT + FT)
                    a = acc[:, bass.ds(b * C + c, 1), :].rearrange("p o n -> p (o n)")
                    nc.vector.scalar_tensor_tensor(a, down_ps(c), 0.5, sd_sb[:, :], ALU.mult, ALU.mult)\
                        .then_inc(ffn["scaled"], 1)
                for c in range(C):
                    a = acc[:, bass.ds(b * C + c, 1), :].rearrange("p o n -> p (o n)")
                    dve.wait_ge(ffn["scaled"], b * C + (C + c + 1))
                    nc.vector.tensor_tensor(a, a, y[:, bass.ds(b * C + c, 1), :].rearrange("p o n -> p (o n)"), ALU.add)\
                        .then_inc(ffn["res"], 1)
                layer_norm(dve, b)

        @block.tensor
        def _(pe):
            mm, tr = nc.tensor.matmul, nc.tensor.transpose
            pe.wait_ge(x_in, 16)
            pe.wait_ge(mask_ready, 3)
            for g in range(NT * KT // 4):
                k, q = g // (NT // 4), g % (NT // 4)
                if g >= 2:
                    pe.wait_ge(xT_lo, g - 1)
                for c in range(4):
                    last = tr(work_ps[:, g % 2, c * P:(c + 1) * P], acc[:, 4 * q + c, k * P:(k + 1) * P], ident[:, :])
                last.then_inc(xT_ps, 1)
            pe.wait_ge(xT_lo, NT * KT // 4)
            pe.wait_ge(setup_lo, 1)
            high, low = setup_weights(setup_hi_sb), setup_weights(setup_lo_sb)
            for b in range(B):
                for i in range(2):
                    if b:
                        pe.wait_ge(first_sb, 2 * b + i - 1)
                    cols = slice(b * T, (b + 1) * T)
                    split_product(proj_ps[:, i, :], high[i], low[i], lambda k: hT_hi[:, k, cols],
                                  lambda k: hT_lo[:, k, cols]).then_inc(first_ps, 1)
            for t in range(NT):
                cols = slice(t * P, (t + 1) * P)
                parts = [(hT_hi, high[2]), (hT_lo, high[2]), (hT_hi, low[2])]
                for k in range(KT):
                    for n, (x_, w) in enumerate(parts):
                        last = mm(work_ps[:, 0, t * H:(t + 1) * H], x_[:, k, cols], w[:, k, :],
                                  start=(k == 0 and n == 0), stop=(k == KT - 1 and n == 2))
            last.then_inc(first_ps, 1)
            pe.wait_ge(first_sb, 2 * B + 1)

            for s in slots(pe, H, B):
                u1, u2, u3, u4 = s.u1, s.u2, s.u3, s.u4
                if s.edge:
                    done = [min(max(s.n - lag, 0), B * H) for lag in range(4)]
                    for sem_, per, left, lag in ((conv_step, 12, 3, 0), (fexp_done, 1, 0, 0), (wN_step, 5, 0, 0),
                                                 (vN_done, 1, 0, 1), (A_done, 4, 0, 1), (UT_done, 8, 0, 1),
                                                 (V_step, 18, 0, 1), (aT_done, 1, 0, 2), (mix_done, 9, 0, 2), (far_done, 3, 0, 2),
                                                 (oN_done, 1, 0, 3), (og_done, 1, 0, 3), (y_done, 2, 0, 3),
                                                 (tg_done, 1, 0, 3)):
                        wait(pe, sem_, per * done[lag] - left)
                if u4:
                    pe.wait_ge(mix_done, u4.count(9, 9))
                    pe.wait_ge(far_done, u4.count(3, 3))
                    pe.wait_ge(vN_done, u4.count(1, 1))
                    wait(pe, y_done, u4.count(2, 0))
                    for t in range(C):
                        for c in range(t + 1):
                            last = mm(work_ps[:, 0, t * P:(t + 1) * P], A2[:, c, t * P:(t + 1) * P],
                                      vN[:, u4.par, c * P:(c + 1) * P], start=(c == 0), stop=(c == t))
                    last.then_inc(o_ps_ready, 1)
                    pe.wait_ge(head_g, 16 * (u4.h + 1))
                    if not s.edge:
                        pe.wait_ge(conv_step, u1.count(12, -6))
                    mm(proj_ps[:, 0, :], wg2_head[:, :], g1T[:, u4.par * T:(u4.par + 1) * T], start=True, stop=True)\
                        .then_inc(gate_ps_ready, 1)
                if u3:
                    pe.wait_ge(a_done, u3.count(4, 4))
                    turn(1, aN).then_inc(aT_ps_ready, 1)
                if u2:
                    pe.wait_ge(silu_done, u2.count(4, 3))
                    if u4:
                        pe.wait_ge(oN_done, u4.count(1, 1))
                    key_query(pe, u2, 0)
                if u1:
                    project(pe, s, 0)
                if u3:
                    pe.wait_ge(aT_done, u3.count(1, 1))
                    mix_products(pe, u3, 0)
                if u2:
                    pe.wait_ge(A_done, u2.count(4, 1))
                    key_query(pe, u2, 1)
                    if u3:
                        pe.wait_ge(aT_done, u3.count(1, 1))
                    key_query(pe, u2, 2)
                if u3:
                    mix_products(pe, u3, 1)
                if u2:
                    pe.wait_ge(A_done, u2.count(4, 2))
                    key_query(pe, u2, 3)
                if u3:
                    mix_products(pe, u3, 2)
                if u2:
                    turn_U(pe, u2, 0)
                if u1:
                    pe.wait_ge(head_f, 16 * (u1.h + 1))
                    wait(pe, conv_step, u1.count(12, 0))
                    nc.tensor.matmul(proj_ps[:, 1, :], wf2_head[:, :], f1T[:, u1.par * T:(u1.par + 1) * T], start=True,
                                     stop=True).then_inc(proj_ps_ready, 1)
                if u2:
                    turn_U(pe, u2, 1)
                for r in range(LEVELS):
                    if u2:
                        level_scores(pe, u2, r)
                        if r + 2 < LEVELS - 1:
                            turn_U(pe, u2, r + 2)
                    if u4 and r in (6, 7):
                        if r == 6:
                            pe.wait_ge(og_done, u4.count(1, 1))
                            pe.wait_ge(wo_scaled, u4.h + 1)
                            if u1:
                                pe.wait_ge(wN_step, u1.count(5, 5))
                        for c in range(2):
                            t0 = (2 * (r - 6) + c) * P
                            last = mm(work_ps[:, r - 6, c * HID:(c + 1) * HID], tg[:, t0:t0 + P], wo_head[:, :], start=True,
                                      stop=True)
                        last.then_inc(y_ps_ready, 1)
                    if u3:
                        mix_products(pe, u3, r + 3)
                    if u2 and r == 2:
                        pe.wait_ge(silu_done, u2.count(4, 4))
                        pe.wait_ge(A_done, u2.count(4, 3))
                        turn(1, conv[:, 2, :]).then_inc(vT_ps_ready, 1)
                    if u1 and r == 1:
                        project(pe, s, 1)
                    if u1 and r == 3:
                        pe.wait_ge(silu_done, u1.count(4, 1))
                        if u2:
                            pe.wait_ge(A_done, u2.count(4, 4))
                        turn(0, wT[:, u1.par, :]).then_inc(wT_ps_ready, 1)
                    if u4 and r == 3:
                        pe.wait_ge(on_done, u4.count(4, 4))
                        if u2:
                            pe.wait_ge(vN_done, u2.count(1, 1))
                        turn(1, oN).then_inc(onT_ps_ready, 1)
                    if u1 and r == 4:
                        project(pe, s, 2)
                if u1:
                    project(pe, s, 3)
                if u2:
                    pe.wait_ge(sT_done, u2.count(1, 1))
                    pe.wait_ge(Alev_done, u2.count(8, 8))
                    if u4:
                        pe.wait_ge(y_done, u4.count(2, 2))
                    else:
                        pe.wait_ge(vN_done, u2.count(1, 1))
                    for c in range(C):
                        mm(work_ps[:, 1, c * P:(c + 1) * P], V[:, c * P:(c + 1) * P], ident[:, :], is_transpose=True,
                           start=True, stop=False)
                        last = mm(work_ps[:, 1, c * P:(c + 1) * P], A_diag[:, c, :],
                                  wN[:, u2.par % 2, c * P:(c + 1) * P], start=False, stop=True)
                    last.then_inc(s_ps_ready, 1)

            for b in range(B):
                pe.wait_ge(ffn["norm"], b * C + C)
                if b:
                    pe.wait_ge(ffn["yT_lo"], b * KT)
                for k in range(KT):
                    for c in range(C):
                        last = tr(work_ps[:, k, c * P:(c + 1) * P], y[:, b * C + c, k * P:(k + 1) * P], ident[:, :])
                    last.then_inc(ffn["yT_ps"], 1)
            pe.wait_ge(ffn["cast"], 3)
            pe.wait_ge(ffn["yT_lo"], B * KT)

            def down(b, f):
                pe.wait_ge(ffn["fused_lo"], b * FT + (f + 1))
                if f == 0:
                    pe.wait_ge(ffn["scaled"], b * C + C)
                for c in range(C):
                    for part in (fused_hi, fused_lo):
                        last = mm(down_ps(c), part[:, f % 4, c * P:(c + 1) * P], wd_r[:, f, :],
                                  start=(f == 0 and part is fused_hi), stop=(f == FT - 1 and part is fused_lo))
                last.then_inc(ffn["down_ps"], 1)

            with pe.Fori(0, B) as b:
                for f in range(FT):
                    if f >= 2:
                        pe.wait_ge(ffn["fused"], b * FT + (f - 1))
                    for w, dst in ((wg_r, ffn_gate_ps(f)), (wu_r, ffn_up_ps(f))):
                        for k in range(KT):
                            for part in (yT_hi, yT_lo):
                                last = mm(dst, w[:, k, f * P:(f + 1) * P], part[:, k, bass.ts(b, T)],
                                          start=(k == 0 and part is yT_hi), stop=(k == KT - 1 and part is yT_lo))
                        last.then_inc(ffn["up_ps"], 1)
                    if f >= 2:
                        down(b, f - 2)
                down(b, FT - 2)
                down(b, FT - 1)

_INS = ["hidden_states", "Wq", "Wk", "Wv", "Ww", "cq", "ck", "cv", "Wf1", "Wf2", "Wb", "Wg1", "Wg2", "bg2", "norm_w",
        "Wo"]
_FFN = ["w_gate", "w_up", "w_down", "s_gate", "s_up", "s_down"]


def kernel(**inputs):
    import numpy as np
    import concourse.bacc as bacc
    from concourse.bass_utils import run_bass_kernel_spmd

    nc = bacc.Bacc("TRN2", target_bir_lowering=False, num_devices=1)
    arrays, args = {}, []
    for name in ["L0_attn_" + n for n in _INS] + ["L0_ffn_" + n for n in _FFN]:
        a = np.ascontiguousarray(inputs[name])
        if a.dtype == np.int8:
            a = a.view(np.int32)
        arrays["in_" + name] = a
        args.append(nc.dram_tensor("in_" + name, a.shape, mybir.dt.from_np(a.dtype), kind="ExternalInput").ap())
    shape = inputs["L0_attn_hidden_states"].shape
    out = nc.dram_tensor("out_x", shape, F32, kind="ExternalOutput").ap()
    build(nc, *args, out)
    r = run_bass_kernel_spmd(nc, [arrays], core_ids=[0])
    return r.results[0]["out_x"]
```

```python
from contextlib import ExitStack

import concourse.bass as bass
from concourse import mybir

F32 = mybir.dt.float32
F32R = mybir.dt.float32r
I8 = mybir.dt.int8
I32 = mybir.dt.int32
U32 = mybir.dt.uint32
ALU = mybir.AluOpType
ACT = mybir.ActivationFunctionType
AX_X = mybir.AxisListType.X

P = 128
LEVELS = 9
IN_CHUNK = 7
NORM_EPS = 1e-6
RMS_EPS = 1e-5
LN_EPS = 1e-5


class Unit:

    def __init__(self, head, off):
        self.head, self.off = head, off
        self.par = off % 4
        self.h = off // 4 if head is None else head + off // 4

    def count(self, per, k):
        if self.head is None:
            return per * self.off + k
        return self.head * (4 * per) + (per * self.off + k)


class Slot:

    def __init__(self, head, off, units):
        def unit(lag):
            if head is None and not 0 <= off - lag < units:
                return None
            return Unit(head, off - lag)

        self.u1, self.u2, self.u3, self.u4 = (unit(lag) for lag in range(4))
        self.edge = head is None
        self.n = off
        self.j = off % 4


def slots(eng, heads, seqs):
    units = heads * seqs
    for n in range(seqs):
        yield Slot(None, n, units)
    with eng.Fori(1, heads) as h:
        for j in range(seqs):
            yield Slot(h, j, units)
    for n in range(units, units + 3):
        yield Slot(None, n, units)


def wait(eng, sem, value):
    if not isinstance(value, int) or value > 0:
        eng.wait_ge(sem, value)


def build(nc, x, Wq, Wk, Wv, Ww, cq, ck, cv, Wf1, Wf2, Wb, Wg1, Wg2, bg2, norm_w, Wo,
          w_gate, w_up, w_down, s_gate, s_up, s_down, out):
    B, T, HID = x.shape
    KW = cq.shape[1]
    H = Wb.shape[1]
    D = norm_w.shape[0]
    INTER = s_gate.shape[0]
    KT = HID // P
    C = T // P
    NT = B * T // P
    FT = INTER // P
    SCALE = float(D) ** -0.5
    SETUP = 2 * KT * P + KT * H
    assert D == P and B == 4 and C == 4 and T == 2 << (LEVELS - 1) and KT == 2 and KW == 4

    with ExitStack() as ctx:
        def sb(name, shape, dt=F32):
            return stacks[-1].enter_context(nc.sbuf_tensor(name, shape, dt))

        def sem(name):
            return ctx.enter_context(nc.semaphore(name))

        proj_ps = ctx.enter_context(nc.psum_tensor("proj_ps", [P, 2, T], F32))
        tr_ps = ctx.enter_context(nc.psum_tensor("tr_ps", [P, T], F32))
        out_ps = ctx.enter_context(nc.psum_tensor("out_ps", [P, T], F32))
        mix_ps = ctx.enter_context(nc.psum_tensor("mix_ps", [P, 2, T], F32))
        work_ps = ctx.enter_context(nc.psum_tensor("work_ps", [P, 2, T], F32))

        stacks = [ctx]

        acc = sb("acc", [P, NT, HID])
        ident = sb("ident", [P, P])
        masks = sb("masks", [P, IN_CHUNK, P // 2])
        consts = sb("consts", [P, 4, C])

        stacks.append(ExitStack())
        setup_raw = sb("setup_raw", [P, SETUP])
        setup_hi_sb = sb("setup_hi_sb", [P, SETUP], F32R)
        setup_lo_sb = sb("setup_lo_sb", [P, SETUP], F32R)
        stacks.pop().close()

        stacks.append(ExitStack())
        U = sb("U", [P, 2, LEVELS - 1, T])
        hT_hi = sb("hT_hi", [P, KT, B * T], F32R)
        hT_lo = sb("hT_lo", [P, KT, B * T], F32R)
        f1T = sb("f1T", [P, B * T])
        g1T = sb("g1T", [P, B * T])
        beta = sb("beta", [P, NT, H])
        coefs = sb("coefs", [P, 3, H, KW])
        bg2_sb = sb("bg2_sb", [P, H])
        w_raw = sb("w_raw", [P, 4, KT, P])
        w_hi = sb("w_hi", [P, 4, KT, P], F32R)
        w_lo = sb("w_lo", [P, 4, KT, P], F32R)
        wo_raw = sb("wo_raw", [P, HID])
        wo_hi = sb("wo_hi", [P, HID], F32R)
        wo_lo = sb("wo_lo", [P, HID], F32R)
        wf2_head = sb("wf2_head", [P, P])
        wg2_head = sb("wg2_head", [P, P])
        coef = sb("coef", [P, 3, KW])
        coef_v = sb("coef_v", [P, KW])
        gbias = sb("gbias", [P, 1])
        wT = sb("wT", [P, 2, T])
        vN = sb("vN", [P, 2, T])
        gT = sb("gT", [P, 2, T])
        tot = sb("tot", [P, 2, T])
        qk = sb("qk", [P, 2, T])
        qk_hi = sb("qk_hi", [P, 2, T], F32R)
        qk_lo = sb("qk_lo", [P, 2, T], F32R)
        wN = sb("wN", [P, 2, T])
        fac = sb("fac", [P, 4, C])
        ssq = sb("ssq", [P, 2, C])
        conv = sb("conv", [P, 3, T])
        th = sb("th", [P, 2, T])
        fexp = sb("fexp", [P, T])
        A = sb("A", [P, C, T])
        A_lev = sb("A_lev", [P, IN_CHUNK, C, P // 2])
        A_diag = sb("A_diag", [P, C, P])
        UT = sb("UT", [P, 2, T])
        V = sb("V", [P, T])
        mx = sb("mx", [P, 2, C])
        aN = sb("aN", [P, T])
        aT = sb("aT", [P, T])
        Z = sb("Z", [P, 4, C])
        own = sb("own", [P, C])
        W = sb("W", [P, T])
        A2 = sb("A2", [P, C, T])
        oN = sb("oN", [P, T])
        ssqo = sb("ssqo", [P, 2, C])
        rms = sb("rms", [P, 2, C])
        tg = sb("tg", [P, T])
        tg_hi = sb("tg_hi", [P, T], F32R)
        tg_lo = sb("tg_lo", [P, T], F32R)

        heads_output = (aN[:, :], fexp[:, :])

        def setup_weights(buf):
            two = buf[:, 0:2 * KT * P].rearrange("p (i k n) -> p i k n", i=2, k=KT)
            return two[:, 0], two[:, 1], buf[:, 2 * KT * P:SETUP].rearrange("p (k n) -> p k n", k=KT)

        stacks.pop().close()
        stacks.append(ctx)
        q8 = sb("q8", [P, 3, KT * INTER // 4], I32)
        wg_r = sb("wg_r", [P, KT, INTER], F32R)
        wu_r = sb("wu_r", [P, KT, INTER], F32R)
        wd_r = sb("wd_r", [P, FT, HID], F32R)
        sg_sb = sb("sg_sb", [P, FT])
        su_sb = sb("su_sb", [P, FT])
        sgu = sb("sgu", [P, FT])
        sd_sb = sb("sd_sb", [P, HID])
        y = sb("y", [P, NT, HID])
        yT_hi = sb("yT_hi", [P, KT, B * T], F32R)
        yT_lo = sb("yT_lo", [P, KT, B * T], F32R)
        gate_th = sb("gate_th", [P, 2, T])
        gate_mid = sb("gate_mid", [P, 2, T])
        fused = sb("fused", [P, 4, T])
        fused_hi = sb("fused_hi", [P, 4, T], F32R)
        fused_lo = sb("fused_lo", [P, 4, T], F32R)
        tick = sb("tick", [P, 1])
        bn = sb("bn", [P, NT, 6])
        mv = sb("mv", [P, NT, 2])
        rs = sb("rs", [P, NT])

        names = ("x_in w_in small_in head_w head_f head_g head_q head_k head_v head_o const_ready mask_ready xT_ps xT_hi xT_lo "
                 "setup_hi setup_lo first_ps first_sb beta_step norm_set wo_scaled wo_cut wo_left high_done low_done coef_set coef_v_set gbias_set "
                 "proj_ps_ready gate_ps_ready wT_ps_ready vT_ps_ready A_ps_ready UT_ps_ready out_ps_ready s_ps_ready "
                 "aT_ps_ready mix_ps_ready o_ps_ready onT_ps_ready y_ps_ready "
                 "conv_step silu_done qk_done qk_cut qk_left og_cut og_left decay_step U_step V_step max_step own_ready own_done mix_done far_done vN_done og_done y_done acc_done "
                 "tap_done tanh_done plus_done fexp_done wN_step A_done UT_done a_done aT_done oN_done osq_done on_done tg_done "
                 "fac_step Alev_done sT_done W_step rms_step").split()
        S = {n: sem(n) for n in names}
        (x_in, w_in, small_in, head_w, head_f, head_g, head_q, head_k, head_v, head_o, const_ready, mask_ready, xT_ps,
         xT_hi, xT_lo, setup_hi, setup_lo, first_ps, first_sb, beta_step, norm_set, wo_scaled, wo_cut, wo_left, high_done, low_done,
         coef_set, coef_v_set, gbias_set,
         proj_ps_ready, gate_ps_ready, wT_ps_ready, vT_ps_ready, A_ps_ready, UT_ps_ready, out_ps_ready, s_ps_ready,
         aT_ps_ready, mix_ps_ready, o_ps_ready, onT_ps_ready, y_ps_ready,
         conv_step, silu_done, qk_done, qk_cut, qk_left, og_cut, og_left, decay_step, U_step, V_step, max_step, own_ready, own_done, mix_done, far_done, vN_done, og_done, y_done, acc_done,
         tap_done, tanh_done, plus_done, fexp_done, wN_step, A_done, UT_done, a_done, aT_done, oN_done, osq_done, on_done, tg_done,
         fac_step, Alev_done, sT_done, W_step, rms_step) = (S[n] for n in names)
        ffn = {n: sem("ffn_" + n) for n in (
            "q_in scale_in cast scales stats var_eps rstd norm yT_ps yT_hi yT_lo up_ps tanh mid fused fused_hi fused_lo "
            "down_ps scaled res stats2 var_eps2 rstd2 done store").split()}

        def pairs(ap, lev):
            return ap.rearrange("p (n e l) -> p n e l", e=2, l=1 << lev)

        def block_tot(par, lev, odd):
            if lev == 0:
                t = gT[:, par % 2, :]
                n = T
            else:
                n = T >> lev
                t = tot[:, par % 2, T - 2 * n:T - n]
            t = t.rearrange("p (n e) -> p n e", e=2)[:, :, odd:odd + 1]
            return t.to_broadcast([P, n // 2, 1 << lev])

        def chunk_sel(buf, lev):
            flat = buf[:, :, :].rearrange("p c t -> p (c t)")
            n = P >> (lev + 1)
            cols = [flat[:, c * (T + P):c * (T + P) + P] for c in range(C)]
            one = cols[0].rearrange("p (n e l) -> p n e l", e=2, l=1 << lev)[:, :, 1, :]
            lead, rest = one.ap[0], list(one.ap[1:])
            return bass.AP(one.tensor, one.offset, [list(lead), [T + P, C]] + [list(r) for r in rest])

        def diag_blocks(buf, c0, nc_):
            flat = buf[:, :, :].rearrange("p c t -> p (c t)")[:, c0 * (T + P):c0 * (T + P) + P]
            return bass.AP(flat.tensor, flat.offset, [list(flat.ap[0]), [T + P, nc_], [1, P]])

        def unused(buf):
            return buf[:, 2:4, 0:2 * P]

        def unused_chunk(buf, c):
            return unused(buf)[:, c // 2, (c % 2) * P:(c % 2 + 1) * P]

        def mask_sel(lev, dt=F32):
            m = masks[:, lev, :].bitcast(dt) if dt != F32 else masks[:, lev, :]
            one = m.rearrange("p (n l) -> p n l", l=1 << lev)
            return bass.AP(one.tensor, one.offset, [list(one.ap[0]), [0, C]] + [list(r) for r in one.ap[1:]])

        def mix_cols(half, lev):
            return mix_ps[:, half, 0:T // 2].rearrange("p (c n l) -> p c n l", c=C, l=1 << lev)

        def Ulev(u, lev):
            return wT[:, u.par % 2, :] if lev == 0 else U[:, u.par % 2, lev - 1, :]


        def grow_W(pool, u3, lev):
            w = pairs(W[:, :], lev)[:, :, 1, :]
            pool.wait_ge(W_step, u3.count(9, 1 + lev))
            pool.wait_ge(mix_ps_ready, u3.count(10, 1 + lev))
            nc.gpsimd.tensor_tensor(w, w, block_tot(u3.par, lev, 0), ALU.mult).then_inc(W_step, 1)

        def ffn_gate_ps(f):
            return proj_ps[:, f % 2, :]

        def ffn_up_ps(f):
            return mix_ps[:, f % 2, :]

        CONV_BANK = (0, 0, 1, 1)
        CONV_BUF = (0, 1, 0, 2)
        PROJ_AT = (1, 3, 4, 5)
        COEF_OF = (0, 1, 2, 0)

        def filt(i, k):
            return coef_v[:, k:k + 1] if i == 3 else coef[:, COEF_OF[i], k:k + 1]

        def tap(act, u, i):
            if i == 0:
                act.wait_ge(coef_set, u.h + 1)
                wait(act, qk_done, u.count(2, 0))
            if i == 1:
                wait(act, qk_done, u.count(2, -1))
            if i == 2:
                act.wait_ge(silu_done, u.count(2, 1))
            if i == 3:
                act.wait_ge(coef_v_set, u.h + 1)
                wait(act, vT_ps_ready, u.count(1, 0))
            act.wait_ge(proj_ps_ready, u.count(5, PROJ_AT[i]))
            nc.scalar.activation(conv[:, CONV_BUF[i], :], proj_ps[:, CONV_BANK[i], :], ACT.Copy,
                                 scale=filt(i, KW - 1)).then_inc(tap_done, 1)

        def tanh(act, u, i):
            if i == 3:
                act.wait_ge(qk_done, u.count(2, 1))
            if i == 0:
                wait(act, qk_done, u.count(2, 0))
            act.wait_ge(conv_step, u.count(12, 3 * i + 3))
            nc.scalar.activation(th[:, i % 2, :], conv[:, CONV_BUF[i], :], ACT.Tanh, scale=0.5).then_inc(tanh_done, 1)
            if i in (1, 2):
                act.wait_ge(tanh_done, u.count(4, i + 1))
                nc.scalar.activation(th[:, i % 2, :], th[:, i % 2, :], ACT.Copy, bias=1.0).then_inc(plus_done, 1)

        def exp_scores(act, u3):
            act.wait_ge(max_step, u3.count(2, 2))
            wait(act, acc_done, u3.count(2, -3))
            for c in range(C):
                nc.scalar.activation(aN[:, c * P:(c + 1) * P], work_ps[:, 1, c * P:(c + 1) * P], ACT.Exp,
                                     bias=mx[:, 1, c:c + 1], scale=SCALE / 4,
                                     accum_out=Z[:, u3.par, c:c + 1]).then_inc(a_done, 1)

        A_BANK = (0, 0, 1, 0)

        def evac_A(act, u2, c):
            act.wait_ge(A_ps_ready, u2.count(4, c + 1))
            nc.scalar.activation(A[:, c, c * P:T], work_ps[:, A_BANK[c], c * P:T], ACT.Copy,
                                 scale=fac[:, u2.par, c:c + 1]).then_inc(A_done, 1)

        def evac_UT(act, u2, i):
            act.wait_ge(UT_ps_ready, u2.count(8, i + 1))
            wait(act, out_ps_ready, u2.count(9, i - 1))
            dst, src = UT[:, i % 2, :], tr_ps[:, :]
            if i == 0:
                dst, src = dst[:, 0:T // 2], src[:, 0:T // 2]
            if i == 1:
                dst, src = (x_.rearrange("p (n e t) -> p n e t", e=2, t=P)[:, :, 0, :] for x_ in (dst, src))
            nc.scalar.activation(dst, src, ACT.Copy).then_inc(UT_done, 1)

        def down_ps(c):
            return (work_ps[:, 0, 0:HID], work_ps[:, 1, 0:HID], tr_ps[:, 0:HID], out_ps[:, 0:HID])[c]

        def attention_stats(dve, b):
            for t in range(b * C, (b + 1) * C):
                nc.vector.bn_stats(bn[:, t, :], acc[:, t, :]).then_inc(ffn["stats"], 1)
            dve.wait_ge(ffn["stats"], 2 * b * C + C)
            nc.vector.memset(tick[:, :], 0.0)
            for t in range(b * C, (b + 1) * C):
                nc.vector.bn_aggr(mv[:, t, :], bn[:, t, :]).then_inc(ffn["stats"], 1)
            dve.wait_ge(ffn["stats"], 2 * (b + 1) * C)
            nc.vector.tensor_scalar(rs[:, b * C:(b + 1) * C].unsqueeze(2), mv[:, b * C:(b + 1) * C, 1:2], LN_EPS, None,
                                    ALU.add).then_inc(ffn["var_eps"], 1)

        def attention_norm(dve, b):
            dve.wait_ge(ffn["rstd"], b + 1)
            for t in range(b * C, (b + 1) * C):
                nc.vector.tensor_scalar(y[:, t, :], acc[:, t, :], mv[:, t, 0:1], rs[:, t:t + 1], ALU.subtract, ALU.mult)\
                    .then_inc(ffn["norm"], 1)

        def lows(dve, b):
            for k in range(KT):
                dve.wait_ge(ffn["yT_hi"], b * KT + k + 1)
                cols = slice(b * T, (b + 1) * T)
                nc.vector.tensor_tensor(yT_lo[:, k, cols], work_ps[:, k, :], yT_hi[:, k, cols].bitcast(F32), ALU.subtract)\
                    .then_inc(ffn["yT_lo"], 1)

        def layer_norm(dve, b):
            def tile(c):
                return acc[:, bass.ds(b * C + c, 1), :].rearrange("p o n -> p (o n)")
            dve.wait_ge(ffn["res"], b * C + C)
            nc.vector.memset(tick[:, :], 0.0)
            for c in range(C):
                nc.vector.bn_stats(bn[:, c, :], tile(c)).then_inc(ffn["stats2"], 1)
            dve.wait_ge(ffn["stats2"], b * 2 * C + C)
            nc.vector.memset(tick[:, :], 0.0)
            for c in range(C):
                nc.vector.bn_aggr(mv[:, c, :], bn[:, c, :]).then_inc(ffn["stats2"], 1)
            dve.wait_ge(ffn["stats2"], b * 2 * C + 2 * C)
            nc.vector.tensor_scalar(rs[:, 0:C].unsqueeze(2), mv[:, 0:C, 1:2], LN_EPS, None, ALU.add)\
                .then_inc(ffn["var_eps2"], 1)
            dve.wait_ge(ffn["rstd2"], b * 1 + 1)
            for c in range(C):
                nc.vector.tensor_scalar(tile(c), tile(c), mv[:, c, 0:1], rs[:, c:c + 1], ALU.subtract, ALU.mult)\
                    .then_inc(ffn["done"], 1)

        V_TAPS = (4, 6, 7)

        def grow_U(dve, u, lev):
            src, dst = pairs(Ulev(u, lev), lev), pairs(Ulev(u, lev + 1), lev)
            wait(dve, mix_ps_ready, u.count(10, -10))
            if lev == 0:
                dve.wait_ge(silu_done, u.count(2, 1))
                dve.wait_ge(decay_step, u.count(12, 5))
            else:
                dve.wait_ge(U_step, u.count(16, 2 * lev))
                dve.wait_ge(decay_step, u.count(12, 5 + lev))
            n = T >> (lev + 1) if lev < IN_CHUNK else 1
            nc.vector.tensor_tensor(dst[:, 0:n, 0, :], src[:, 0:n, 0, :], block_tot(u.par, lev, 1)[:, 0:n], ALU.mult)\
                .then_inc(U_step, 1)
            nc.vector.tensor_copy(dst[:, 0:n, 1, :], src[:, 0:n, 1, :]).then_inc(U_step, 1)

        def conv_tap(dve, u, i, k):
            back = k + 1
            dve.wait_ge(tap_done, u.count(4, i + 1)) if k == 0 else dve.wait_ge(conv_step, u.count(12, 3 * i + k))
            y_ = conv[:, CONV_BUF[i], back:T]
            nc.vector.scalar_tensor_tensor(y_, proj_ps[:, CONV_BANK[i], 0:T - back], filt(i, KW - 1 - back), y_,
                                           ALU.mult, ALU.add).then_inc(conv_step, 1)

        def silu(dve, u, i):
            dst = wT[:, u.par % 2, :] if i == 0 else conv[:, 2, :]
            dve.wait_ge(tanh_done, u.count(4, i + 1))
            if i == 0:
                wait(dve, mix_ps_ready, u.count(10, 1 - 20))
            nc.vector.scalar_tensor_tensor(dst, th[:, i % 2, :], 1.0, conv[:, CONV_BUF[i], :], ALU.add, ALU.mult)\
                .then_inc(silu_done, 1)

        def cut_qk(act, u, i):
            act.wait_ge(qk_done, u.count(2, i))
            wait(act, A_ps_ready, u.count(4, 0))
            nc.scalar.activation(qk_hi[:, i - 1, :], qk[:, i - 1, :], ACT.Copy).then_inc(qk_cut, 1)

        def left_qk(pool, u, i, cols):
            pool.wait_ge(qk_cut, u.count(2, i))
            wait(pool, A_ps_ready, u.count(4, 0))
            nc.gpsimd.tensor_tensor(qk_lo[:, i - 1, cols], qk[:, i - 1, cols], qk_hi[:, i - 1, cols].bitcast(F32),
                                    ALU.subtract).then_inc(qk_left, 1)

        def silu_qk(pool, u, i):
            pool.wait_ge(plus_done, u.count(2, i))
            nc.gpsimd.tensor_tensor(qk[:, i - 1, :], th[:, i % 2, :], conv[:, CONV_BUF[i], :], ALU.mult)\
                .then_inc(qk_done, 1)

        def gates(dve, u1, i):
            if i == 0:
                dve.wait_ge(fexp_done, u1.count(1, 1))
                nc.vector.tensor_scalar(fexp[:, :], fexp[:, :], 1.0, None, ALU.add).then_inc(decay_step, 1)
                return
            dve.wait_ge(decay_step, u1.count(12, 1))
            if i == 1:
                wait(dve, W_step, u1.count(9, 2 - 18))
            cols = slice((i - 1) * P, i * P)
            nc.vector.reciprocal(gT[:, u1.par % 2, cols], fexp[:, cols]).then_inc(decay_step, 1)

        def gate_products(dve, u2, lev):
            dve.wait_ge(decay_step, u2.count(12, 4 + lev))
            if lev == 1:
                wait(dve, W_step, u2.count(9, 9 - 18))
            n = T >> lev
            src = gT[:, u2.par % 2, :] if lev == 1 else tot[:, u2.par % 2, T - 4 * n:T - 2 * n]
            src = src.rearrange("p (n e) -> p n e", e=2)
            nc.vector.tensor_tensor(tot[:, u2.par % 2, T - 2 * n:T - n], src[:, :, 0], src[:, :, 1], ALU.mult)\
                .then_inc(decay_step, 1)

        def values(dve, u2):
            dve.wait_ge(vT_ps_ready, u2.count(1, 1))
            wait(dve, o_ps_ready, u2.count(1, 1 - 2))
            dve.wait_ge(fac_step, u2.count(3, 3))
            fb = fac[:, u2.par, :].unsqueeze(2).to_broadcast([P, C, P])
            nc.vector.tensor_tensor(vN[:, u2.par % 2, :].rearrange("p (c d) -> p c d", c=C),
                                    work_ps[:, 1, :].rearrange("p (c d) -> p c d", c=C), fb, ALU.mult)\
                .then_inc(vN_done, 1)

        def add_heads_output(pool, u4, i):
            pool.wait_ge(y_done, u4.count(2, i + 1))
            a = acc[:, u4.par * C + 2 * i:u4.par * C + 2 * i + 2, :]
            nc.gpsimd.tensor_tensor(a, a, heads_output[i].rearrange("p (c n) -> p c n", c=2), ALU.add)\
                .then_inc(acc_done, 1)

        def descend(dve, u2, r):
            lev = LEVELS - 1 - r
            new = out_ps[:, 0:T // 2]
            if r == 0:
                wait(dve, s_ps_ready, u2.count(1, 0))
                nc.vector.memset(V[:, 0:T // 2], 0.0).then_inc(V_step, 1)
                dve.wait_ge(out_ps_ready, u2.count(9, 1))
                nc.vector.tensor_copy(V[:, T // 2:T], new).then_inc(V_step, 1)
                return
            v = pairs(V[:, :], lev)[:, :, 1, :]
            dve.wait_ge(V_step, u2.count(18, 2 * r))
            nc.vector.tensor_tensor(v, v, block_tot(u2.par, lev, 0), ALU.mult).then_inc(V_step, 1)
            dve.wait_ge(V_step, u2.count(18, 2 * r + 1))
            dve.wait_ge(out_ps_ready, u2.count(9, r + 1))
            nc.vector.tensor_tensor(v, v, new.rearrange("p (n l) -> p n l", l=1 << lev), ALU.add).then_inc(V_step, 1)

        def own_products(pool, u3):
            pool.wait_ge(a_done, u3.count(4, 4))
            nc.gpsimd.tensor_tensor(unused(A), aN[:, :].rearrange("p (a n) -> p a n", a=2),
                                    wN[:, u3.par % 2, :].rearrange("p (a n) -> p a n", a=2), ALU.mult)\
                .then_inc(own_ready, 1)

        def own_sums(act, u3):
            act.wait_ge(own_ready, u3.count(1, 1))
            wait(act, mix_done, u3.count(8, 0))
            for c in range(C):
                at = unused_chunk(A, c)
                nc.scalar.activation(at, at, ACT.Copy, accum_out=own[:, c:c + 1]).then_inc(own_done, 1)

        def scores_end(dve, u2, odd):
            dve.wait_ge(V_step, u2.count(18, 16 + 2 * odd))
            v = pairs(V[:, :], 0)[:, :, odd, :]
            nc.vector.tensor_tensor(v, v, pairs(gT[:, u2.par % 2, :], 0)[:, :, odd, :], ALU.mult).then_inc(sT_done, 1)

        def own_mixable(dve, s):
            if not s.u2:
                wait(dve, mix_done, s.u3.count(8, IN_CHUNK))
            dve.wait_ge(own_done, s.u3.count(4, 4))

        def mix_own(dve):
            idb = ident[:, :].bitcast(U32).unsqueeze(1).to_broadcast([P, C, P])
            nc.vector.copy_predicated(diag_blocks(A2, 0, C), idb, own[:, :].unsqueeze(2).to_broadcast([P, C, P]))\
                .then_inc(mix_done, 1)

        def mixable(dve, s, lev):
            if lev == 0:
                wait(dve, o_ps_ready, s.u3.count(1, 0))
            if not s.u2 or lev == 0:
                wait(dve, mix_done, s.u3.count(8, lev))
            dve.wait_ge(mix_ps_ready, s.u3.count(10, lev + 1))

        def mix(dve, lev):
            nc.vector.copy_predicated(chunk_sel(A2, lev), mask_sel(lev, U32), mix_cols(lev % 2, lev)).then_inc(mix_done, 1)

        def mix_far(act, u3, i):
            half = i % 2
            act.wait_ge(mix_ps_ready, u3.count(10, i + 1))
            if i == IN_CHUNK:
                for p_ in range(2):
                    ins = nc.scalar.activation(A2[:, 2 * p_, (2 * p_ + 1) * P:(2 * p_ + 2) * P],
                                               mix_ps[:, half, p_ * P:(p_ + 1) * P], ACT.Copy)
            else:
                ins = nc.scalar.activation(A2[:, i - 8, T // 2:T], mix_ps[:, half, 0:T // 2], ACT.Copy)
            ins.then_inc(far_done, 1)

        def split_product(dst, wh, wl, xh, xl):
            parts = [(wh, xh), (wh, xl), (wl, xh)]
            for k in range(KT):
                for n, (w, x_) in enumerate(parts):
                    last = nc.tensor.matmul(dst, w[:, k, :], x_(k),
                                            start=(k == 0 and n == 0), stop=(k == KT - 1 and n == 2))
            return last

        def project(u, i):
            cols = slice(u.par * T, (u.par + 1) * T)
            split_product(proj_ps[:, CONV_BANK[i], :], w_hi[:, i], w_lo[:, i],
                          lambda k: hT_hi[:, k, cols], lambda k: hT_lo[:, k, cols]).then_inc(proj_ps_ready, 1)

        def even_chunks(lev):
            return (0, 1) if lev == LEVELS - 1 else (0, 2) if lev == IN_CHUNK else range(C)

        def turn_U(pe, u2, i):
            lev = LEVELS - 1 - i
            pe.wait_ge(U_step, u2.count(16, 2 * lev))
            wait(pe, UT_done, u2.count(8, i))
            for c in even_chunks(lev):
                last = nc.tensor.transpose(tr_ps[:, c * P:(c + 1) * P], Ulev(u2, lev)[:, c * P:(c + 1) * P],
                                           ident[:, :])
            last.then_inc(UT_ps_ready, 1)

        def level_scores(pe, u2, r):
            lev = LEVELS - 1 - r
            dst = out_ps[:, 0:T // 2]
            wait(pe, V_step, u2.count(18, 2 * r))
            if lev:
                pe.wait_ge(UT_done, u2.count(8, r + 1))
            else:
                pe.wait_ge(wN_step, u2.count(5, 5))
            ut = UT[:, r % 2, :] if lev else wN[:, u2.par % 2, :]
            if lev == 8:
                for c in range(2):
                    last = nc.tensor.matmul(dst, ut[:, c * P:(c + 1) * P], A[:, c, T // 2:T], start=(c == 0), stop=(c == 1))
            elif lev == 7:
                for c in (0, 2):
                    last = nc.tensor.matmul(dst[:, c * P // 2:(c + 2) * P // 2], ut[:, c * P:(c + 1) * P],
                                            A[:, c, (c + 1) * P:(c + 2) * P], start=True, stop=True)
            else:
                pe.wait_ge(Alev_done, u2.count(8, 1 + (IN_CHUNK - 1 - lev)))
                for c in range(C):
                    last = nc.tensor.matmul(dst[:, c * P // 2:(c + 1) * P // 2], ut[:, c * P:(c + 1) * P],
                                            A_lev[:, lev, c, :], start=True, stop=True)
            last.then_inc(out_ps_ready, 1)

        def mix_products(pe, u3, i):
            half = i % 2
            if i < 2:
                wait(pe, far_done, u3.count(3, i - 1))
            elif i == LEVELS:
                pe.wait_ge(far_done, u3.count(3, 1))
            else:
                pe.wait_ge(mix_done, u3.count(8, i - 1))
            lev = min(i, LEVELS - 1)
            pe.wait_ge(W_step, u3.count(9, 1 + lev))
            ul = Ulev(u3, lev)
            if lev < IN_CHUNK:
                for c in range(C):
                    t_sel = pairs(W[:, c * P:(c + 1) * P], lev)[:, :, 1, :]
                    last = nc.tensor.matmul(mix_ps[:, half, c * P // 2:(c + 1) * P // 2], ul[:, c * P:(c + 1) * P],
                                            t_sel, start=True, stop=True)
            elif lev == IN_CHUNK:
                for c in (0, 2):
                    last = nc.tensor.matmul(mix_ps[:, half, c * P // 2:(c + 2) * P // 2], ul[:, c * P:(c + 1) * P],
                                            W[:, (c + 1) * P:(c + 2) * P], start=True, stop=True)
            else:
                c = i - 8
                last = nc.tensor.matmul(mix_ps[:, half, 0:T // 2], ul[:, c * P:(c + 1) * P], W[:, T // 2:T],
                                        start=True, stop=True)
            last.then_inc(mix_ps_ready, 1)

        def key_query(pe, u2, c):
            dst, s_, t_ = work_ps[:, A_BANK[c], c * P:T], slice(c * P, (c + 1) * P), slice(c * P, T)
            parts = [(qk_hi, qk_hi), (qk_hi, qk_lo), (qk_lo, qk_hi)] if T - c * P >= 2 * P else [(qk, qk)]
            for n, (k, q) in enumerate(parts):
                last = nc.tensor.matmul(dst, k[:, 1, s_], q[:, 0, t_], start=(n == 0), stop=(n == len(parts) - 1))
            last.then_inc(A_ps_ready, 1)

        def turn(bank, src):
            for c in range(C):
                last = nc.tensor.transpose(work_ps[:, bank, c * P:(c + 1) * P], src[:, c * P:(c + 1) * P], ident[:, :])
            return last

        block = ctx.enter_context(nc.Block())

        @block.sync
        def _(sp):
            nc.sync.dma_start(acc[:, :, :], x.rearrange("b (c p) n -> p (b c) n", p=P)).then_inc(x_in, 16)
            wf1_raw, wg1_raw, wb_raw = setup_weights(setup_raw)
            nc.sync.dma_start(wf1_raw, Wf1.rearrange("(k p) n -> p k n", p=P)).then_inc(w_in, 16)
            nc.sync.dma_start(wg1_raw, Wg1.rearrange("(k p) n -> p k n", p=P)).then_inc(w_in, 16)
            nc.sync.dma_start(wb_raw, Wb.rearrange("(k p) n -> p k n", p=P)).then_inc(w_in, 16)
            for i, c in enumerate((cv, cq, ck)):
                nc.sync.dma_start(coefs[:, i], c.rearrange("(h p) w -> p h w", p=P)).then_inc(small_in, 16)
            with nc.allow_non_contiguous_dma(reason="a few hundred words, once"):
                nc.sync.dma_start(bg2_sb[:, :], bg2.rearrange("(h p) -> p h", p=P)).then_inc(small_in, 16)
                nc.sync.dma_start(consts[:, 3, 0:1], norm_w.rearrange("(p o) -> p o", o=1)).then_inc(small_in, 16)

            def head_cols(w, h):
                return w[:, bass.ts(h, P)].rearrange("(k p) n -> p k n", p=P)

            def load_head(h, first):
                before = None if first else Unit(h, -1)
                for i, (w, landed) in enumerate(((Ww, head_w), (None, head_f), (Wq, head_q), (Wk, head_k),
                                                 (Wv, head_v))):
                    if before is not None:
                        sp.wait_ge(proj_ps_ready, before.count(5, i + 1))
                    if w is None:
                        nc.sync.dma_start(wf2_head[:, :], Wf2[:, bass.ts(h, P)]).then_inc(landed, 16)
                    else:
                        slot = i if i == 0 else i - 1
                        nc.sync.dma_start(w_raw[:, slot], head_cols(w, h)).then_inc(landed, 16)

            def load_gate(h, first):
                if not first:
                    sp.wait_ge(gate_ps_ready, Unit(h, 0).count(1, 0))
                nc.sync.dma_start(wg2_head[:, :], Wg2[:, bass.ts(h, P)]).then_inc(head_g, 16)

            def load_out(h, first):
                if not first:
                    sp.wait_ge(wo_left, h)
                nc.sync.dma_start(wo_raw[:, :], Wo[bass.ts(h, P), :]).then_inc(head_o, 16)

            load_head(0, True)
            load_gate(0, True)
            load_out(0, True)
            with sp.Fori(1, H) as h:
                load_head(h, False)
                load_gate(h, False)
                load_out(h, False)

            sp.wait_ge(acc_done, 2 * B * H)
            for i, (w, tiles) in enumerate(((w_gate, KT), (w_up, KT), (w_down, FT))):
                nc.sync.dma_start(q8[:, i, :].rearrange("p (k n) -> p k n", k=tiles), w.rearrange("(k p) n -> p k n", p=P))\
                    .then_inc(ffn["q_in"], 16)
            with nc.allow_non_contiguous_dma(reason="a few hundred words, once"):
                nc.sync.dma_start(sg_sb[:, :], s_gate.rearrange("(f p) -> p f", p=P)).then_inc(ffn["scale_in"], 16)
                nc.sync.dma_start(su_sb[:, :], s_up.rearrange("(f p) -> p f", p=P)).then_inc(ffn["scale_in"], 16)
            nc.sync.dma_start(sd_sb[:, :], s_down.rearrange("(o n) -> o n", o=1).to_broadcast([P, HID])).then_inc(ffn["scale_in"], 16)

            out_v = out.rearrange("b (c p) n -> p (b c) n", p=P)
            with sp.Fori(0, B) as b:
                sp.wait_ge(ffn["done"], b * C + C)
                nc.sync.dma_start(out_v[:, bass.ts(b, C), :], acc[:, bass.ts(b, C), :]).then_inc(ffn["store"], 16)
            sp.wait_ge(ffn["store"], 16 * B)

        @block.gpsimd
        def _(pool):
            nc.gpsimd.memset(ident[:, :], 0.0).then_inc(mask_ready, 1)
            nc.gpsimd.memset(masks[:, :, :], 1.0).then_inc(mask_ready, 1)
            nc.gpsimd.memset(A2[:, :, :], 0.0).then_inc(const_ready, 1)
            nc.gpsimd.memset(consts[:, 0, :], 4.0 * NORM_EPS).then_inc(const_ready, 1)
            nc.gpsimd.memset(consts[:, 1, :], -0.5).then_inc(const_ready, 1)
            nc.gpsimd.memset(consts[:, 2, :], 4.0 * D * RMS_EPS).then_inc(const_ready, 1)
            pool.wait_ge(mask_ready, 2)
            nc.gpsimd.affine_select(out=ident[:, :], in_=ident[:, :], compare_op=ALU.not_equal, fill=1.0, base=0,
                                    pattern=[[-1, P]], channel_multiplier=1).then_inc(mask_ready, 1)
            for lev in range(IN_CHUNK):
                L = 1 << lev
                m = masks[:, lev, :].rearrange("p (n l) -> p n l", l=L)
                nc.gpsimd.affine_select(out=m, in_=m, compare_op=ALU.is_ge, fill=0.0, base=0,
                                        pattern=[[-2 * L, P // 2 // L], [0, L]], channel_multiplier=1)\
                    .then_inc(mask_ready, 1)
                pool.wait_ge(mask_ready, 4 + 2 * lev)
                nc.gpsimd.affine_select(out=m, in_=m, compare_op=ALU.is_ge, fill=0.0, base=L - 1,
                                        pattern=[[2 * L, P // 2 // L], [0, L]], channel_multiplier=-1)\
                    .then_inc(mask_ready, 1)
            pool.wait_ge(mask_ready, 3 + 2 * IN_CHUNK)
            pool.wait_ge(const_ready, 4)

            for s in slots(pool, H, B):
                u1, u2, u3, u4 = s.u1, s.u2, s.u3, s.u4
                if u1 and s.j == 0:
                    pool.wait_ge(high_done, 2 * u1.h + 1)
                    nc.gpsimd.tensor_tensor(w_lo[:, 0:3], w_raw[:, 0:3], w_hi[:, 0:3].bitcast(F32), ALU.subtract)\
                        .then_inc(low_done, 1)
                if u2:
                    left_qk(pool, u2, 2, slice(0, P))
                    left_qk(pool, u2, 2, slice(P, T))
                if u3:
                    pool.wait_ge(aT_done, u3.count(1, 1))
                    pool.wait_ge(decay_step, u3.count(12, 12))
                    wait(pool, mix_ps_ready, u3.count(10, 0))
                    nc.gpsimd.tensor_tensor(W[:, :], aT[:, :], gT[:, u3.par % 2, :], ALU.mult).then_inc(W_step, 1)
                    own_products(pool, u3)
                if u2:
                    wait(pool, out_ps_ready, u2.count(9, 0))
                    pool.wait_ge(A_done, u2.count(4, 4))
                for i in range(IN_CHUNK):
                    lev = IN_CHUNK - 1 - i
                    if u2:
                        dst = A_lev[:, lev].rearrange("p c (n l) -> p c n l", l=1 << lev)
                        nc.gpsimd.tensor_tensor(dst, chunk_sel(A, lev), mask_sel(lev), ALU.mult)\
                            .then_inc(Alev_done, 1)
                    if u4 and i == IN_CHUNK - 1:
                        if u4.par == 0:
                            pool.wait_ge(wo_cut, u4.h + 1)
                            nc.gpsimd.tensor_tensor(wo_lo[:, :], wo_raw[:, :], wo_hi[:, :].bitcast(F32), ALU.subtract).then_inc(wo_left, 1)
                        pool.wait_ge(og_cut, u4.count(1, 1))
                        nc.gpsimd.tensor_tensor(tg_lo[:, :], tg[:, :], tg_hi[:, :].bitcast(F32), ALU.subtract)\
                            .then_inc(og_left, 1)
                    if u3:
                        grow_W(pool, u3, i)
                    if u4 and i == 1:
                        r = rms[:, u4.par % 2, :]
                        z = Z[:, u4.par, :]
                        wait(pool, on_done, u4.count(4, -4))
                        pool.wait_ge(a_done, u4.count(4, 4))
                        nc.gpsimd.tensor_tensor(r, z, z, ALU.mult).then_inc(rms_step, 1)
                        pool.wait_ge(rms_step, u4.count(4, 1))
                        nc.gpsimd.tensor_tensor(r, r, consts[:, 2, :], ALU.mult).then_inc(rms_step, 1)
                        pool.wait_ge(rms_step, u4.count(4, 2))
                        pool.wait_ge(osq_done, u4.count(4, 4))
                        nc.gpsimd.tensor_tensor(r, r, ssqo[:, u4.par % 2, :], ALU.add).then_inc(rms_step, 1)
                        pool.wait_ge(rms_step, u4.count(4, 3))
                        nc.gpsimd.tensor_tensor(r, r, consts[:, 1, :], ALU.pow).then_inc(rms_step, 1)
                if u1 and s.j == 0:
                    pool.wait_ge(high_done, 2 * u1.h + 2)
                    nc.gpsimd.tensor_tensor(w_lo[:, 3], w_raw[:, 3], w_hi[:, 3].bitcast(F32), ALU.subtract)\
                        .then_inc(low_done, 1)
                if u1:
                    f = fac[:, u1.par, :]
                    pool.wait_ge(wN_step, u1.count(5, 4))
                    nc.gpsimd.tensor_tensor(f, ssq[:, u1.par % 2, :], consts[:, 0, :], ALU.add).then_inc(fac_step, 1)
                    pool.wait_ge(fac_step, u1.count(3, 1))
                    nc.gpsimd.tensor_tensor(f, f, consts[:, 1, :], ALU.pow).then_inc(fac_step, 1)
                if u3:
                    grow_W(pool, u3, IN_CHUNK)
                if u1:
                    silu_qk(pool, u1, 1)
                if u2:
                    wait(pool, s_ps_ready, u2.count(1, 0))
                    idb = ident[:, :].unsqueeze(1).to_broadcast([P, C, P])
                    nc.gpsimd.tensor_tensor(A_diag[:, :, :], diag_blocks(A, 0, C), idb, ALU.mult).then_inc(Alev_done, 1)
                if u4:
                    add_heads_output(pool, u4, 0)
                if u1:
                    left_qk(pool, u1, 1, slice(0, T))
                    pool.wait_ge(fac_step, u1.count(3, 2))
                    if s.n == 0 and s.edge:
                        pool.wait_ge(beta_step, 1 + NT)
                    bt = beta[:, u1.par * C:(u1.par + 1) * C, bass.ds(u1.h, 1)].rearrange("p c o -> p (c o)")
                    nc.gpsimd.tensor_tensor(f, f, bt, ALU.mult).then_inc(fac_step, 1)
                    silu_qk(pool, u1, 2)
                if u4:
                    add_heads_output(pool, u4, 1)
            for b in range(B):
                pool.wait_ge(ffn["var_eps"], b + 1)
                r = rs[:, b * C:(b + 1) * C]
                nc.gpsimd.tensor_tensor(r, r, consts[:, 1, :], ALU.pow).then_inc(ffn["rstd"], 1)
            with pool.Fori(0, B) as b:
                for f in range(FT):
                    pool.wait_ge(ffn["fused_hi"], b * FT + (f + 1))
                    nc.gpsimd.tensor_tensor(fused_lo[:, f % 4, :], fused[:, f % 4, :], fused_hi[:, f % 4, :].bitcast(F32),
                                            ALU.subtract).then_inc(ffn["fused_lo"], 1)
                pool.wait_ge(ffn["var_eps2"], b * 1 + 1)
                nc.gpsimd.tensor_tensor(rs[:, 0:C], rs[:, 0:C], consts[:, 1, :], ALU.pow).then_inc(ffn["rstd2"], 1)

        @block.scalar
        def _(act):
            for g in range(NT * KT // 4):
                act.wait_ge(xT_ps, g + 1)
                k, t0 = g // (NT // 4), (g % (NT // 4)) * T
                nc.scalar.activation(hT_hi[:, k, t0:t0 + T], work_ps[:, g % 2, :], ACT.Copy).then_inc(xT_hi, 1)
            act.wait_ge(w_in, 48)
            nc.scalar.activation(setup_hi_sb[:, :], setup_raw[:, :], ACT.Copy).then_inc(setup_hi, 1)
            for b in range(B):
                for i, dst in enumerate((f1T, g1T)):
                    act.wait_ge(first_ps, 2 * b + i + 1)
                    nc.scalar.activation(dst[:, b * T:(b + 1) * T], proj_ps[:, i, :], ACT.Copy).then_inc(first_sb, 1)
            act.wait_ge(first_ps, 2 * B + 1)
            nc.scalar.activation(beta[:, :, :].rearrange("p t h -> p (t h)"), work_ps[:, 0, 0:NT * H], ACT.Exp,
                                 scale=-1.0).then_inc(first_sb, 1)
            act.wait_ge(small_in, 16 * 5)
            nc.scalar.activation(bg2_sb[:, :], bg2_sb[:, :], ACT.Copy, scale=0.5).then_inc(gbias_set, 1)

            for s in slots(act, H, B):
                u1, u2, u3, u4 = s.u1, s.u2, s.u3, s.u4
                if u1 and s.j == 0:
                    for landed in (head_w, head_q, head_k):
                        act.wait_ge(landed, 16 * (u1.h + 1))
                    nc.scalar.activation(w_hi[:, 0:3], w_raw[:, 0:3], ACT.Copy).then_inc(high_done, 1)
                if u4:
                    if u4.par == 0:
                        nc.scalar.activation(gbias[:, :], bg2_sb[:, bass.ds(u4.h, 1)], ACT.Copy)\
                            .then_inc(gbias_set, 1)
                    act.wait_ge(gbias_set, 2 + u4.h)
                    act.wait_ge(gate_ps_ready, u4.count(1, 1))
                    wait(act, y_ps_ready, u4.count(2, 0))
                    nc.scalar.activation(tg[:, :], proj_ps[:, 0, :], ACT.Tanh, bias=gbias[:, 0:1], scale=0.5)\
                        .then_inc(tg_done, 1)
                if u3:
                    exp_scores(act, u3)
                if u2:
                    cut_qk(act, u2, 2)
                if u4:
                    act.wait_ge(o_ps_ready, u4.count(1, 1))
                    wait(act, onT_ps_ready, u4.count(1, 0))
                    nc.scalar.activation(oN[:, :], work_ps[:, 0, :], ACT.Copy).then_inc(oN_done, 1)
                if u2:
                    tap(act, u2, 3)
                if u3:
                    act.wait_ge(aT_ps_ready, u3.count(1, 1))
                    wait(act, W_step, u3.count(9, -8))
                    nc.scalar.activation(aT[:, :], work_ps[:, 1, :], ACT.Copy).then_inc(aT_done, 1)
                if u2:
                    wait(act, out_ps_ready, u2.count(9, 0))
                    wait(act, Alev_done, u2.count(8, 0))
                    act.wait_ge(fac_step, u2.count(3, 3))
                    evac_A(act, u2, 0)
                if u1:
                    tap(act, u1, 0)
                if u2:
                    evac_A(act, u2, 1)
                    evac_A(act, u2, 2)
                    evac_UT(act, u2, 0)
                    evac_A(act, u2, 3)
                    tanh(act, u2, 3)
                if u1:
                    act.wait_ge(proj_ps_ready, u1.count(5, 2))
                    wait(act, decay_step, u1.count(12, -7))
                    wait(act, acc_done, u1.count(2, -6))
                    nc.scalar.activation(fexp[:, :], proj_ps[:, 1, :], ACT.Exp, scale=-1.0).then_inc(fexp_done, 1)
                if u2:
                    evac_UT(act, u2, 1)
                for r in range(LEVELS):
                    if u4 and r == 5:
                        act.wait_ge(og_done, u4.count(1, 1))
                        wait(act, y_ps_ready, u4.count(2, 0))
                        nc.scalar.activation(tg_hi[:, :], tg[:, :], ACT.Copy).then_inc(og_cut, 1)
                    if u1 and r == 2:
                        tap(act, u1, 1)
                    if u1 and r == 4:
                        act.wait_ge(wT_ps_ready, u1.count(1, 1))
                        if u3:
                            act.wait_ge(own_done, u3.count(4, 4))
                        for c in range(C):
                            nc.scalar.activation(unused_chunk(A, c), work_ps[:, 0, c * P:(c + 1) * P], ACT.Square,
                                                 accum_out=ssq[:, u1.par % 2, c:c + 1]).then_inc(wN_step, 1)
                        nc.scalar.activation(wN[:, u1.par % 2, :], work_ps[:, 0, :], ACT.Copy).then_inc(wN_step, 1)
                    if u2 and r + 2 < LEVELS - 1:
                        evac_UT(act, u2, r + 2)
                    if u4 and r == 0:
                        act.wait_ge(oN_done, u4.count(1, 1))
                        for c in range(C):
                            nc.scalar.activation(unused_chunk(A2, c), oN[:, c * P:(c + 1) * P], ACT.Square,
                                                 accum_out=ssqo[:, u4.par % 2, c:c + 1]).then_inc(osq_done, 1)
                    if u1 and r == 1:
                        tanh(act, u1, 0)
                    if u3 and r == 3:
                        own_sums(act, u3)
                    if u4 and r == 2:
                        act.wait_ge(rms_step, u4.count(4, 4))
                        for c in range(C):
                            nc.scalar.activation(oN[:, c * P:(c + 1) * P], oN[:, c * P:(c + 1) * P], ACT.Copy,
                                                 scale=rms[:, u4.par % 2, c:c + 1]).then_inc(on_done, 1)
                    if u1 and s.j == 0 and r == 3:
                        act.wait_ge(head_v, 16 * (u1.h + 1))
                        nc.scalar.activation(w_hi[:, 3], w_raw[:, 3], ACT.Copy).then_inc(high_done, 1)
                    if u4 and u4.par == 0 and r == 3:
                        act.wait_ge(norm_set, 1)
                        act.wait_ge(head_o, 16 * (u4.h + 1))
                        wait(act, y_ps_ready, u4.count(2, 0))
                        nc.scalar.activation(wo_raw[:, :], wo_raw[:, :], ACT.Copy, scale=consts[:, 3, 0:1])\
                            .then_inc(wo_scaled, 1)
                        act.wait_ge(wo_scaled, u4.h + 1)
                        nc.scalar.activation(wo_hi[:, :], wo_raw[:, :], ACT.Copy).then_inc(wo_cut, 1)
                    if u1 and r == 4:
                        tanh(act, u1, 1)
                    if u1 and r == 5:
                        tap(act, u1, 2)
                    if u3 and r >= 7:
                        mix_far(act, u3, r)
                    if u4 and r == 8:
                        if u1:
                            act.wait_ge(decay_step, u1.count(12, 5))
                        for i in range(2):
                            act.wait_ge(y_ps_ready, u4.count(2, i + 1))
                            nc.scalar.activation(heads_output[i], work_ps[:, i, :], ACT.Copy).then_inc(y_done, 1)
                if u3:
                    mix_far(act, u3, LEVELS)
                if u1:
                    cut_qk(act, u1, 1)
                    tanh(act, u1, 2)
            act.wait_ge(ffn["q_in"], 48)
            for i, dst in enumerate((wg_r, wu_r, wd_r)):
                nc.scalar.activation(dst.rearrange("p k n -> p (k n)"), q8[:, i, :].bitcast(I8),
                                     ACT.Copy).then_inc(ffn["cast"], 1)
            for b in range(B):
                for k in range(KT):
                    act.wait_ge(ffn["yT_ps"], b * KT + (k + 1))
                    nc.scalar.activation(yT_hi[:, k, b * T:(b + 1) * T], work_ps[:, k, :], ACT.Copy)\
                        .then_inc(ffn["yT_hi"], 1)
            act.wait_ge(ffn["scales"], 2)

            def high(b, f):
                act.wait_ge(ffn["fused"], b * FT + (f + 1))
                if f >= 4:
                    act.wait_ge(ffn["down_ps"], b * FT + (f - 3))
                nc.scalar.activation(fused_hi[:, f % 4, :], fused[:, f % 4, :], ACT.Copy).then_inc(ffn["fused_hi"], 1)

            with act.Fori(0, B) as b:
                for f in range(FT):
                    act.wait_ge(ffn["up_ps"], b * 2 * FT + (2 * f + 1))
                    if f >= 2:
                        act.wait_ge(ffn["mid"], b * FT + (f - 1))
                    nc.scalar.activation(gate_th[:, f % 2, :], ffn_gate_ps(f), ACT.Tanh, scale=sg_sb[:, f:f + 1])\
                        .then_inc(ffn["tanh"], 1)
                    if f:
                        high(b, f - 1)
                high(b, FT - 1)

        @block.vector
        def _(dve):
            for g in range(NT * KT // 4):
                k, t0 = g // (NT // 4), (g % (NT // 4)) * T
                dve.wait_ge(xT_hi, g + 1)
                nc.vector.tensor_tensor(hT_lo[:, k, t0:t0 + T], work_ps[:, g % 2, :],
                                        hT_hi[:, k, t0:t0 + T].bitcast(F32),
                                        ALU.subtract).then_inc(xT_lo, 1)
            dve.wait_ge(setup_hi, 1)
            nc.vector.tensor_tensor(setup_lo_sb[:, :], setup_raw[:, :], setup_hi_sb[:, :].bitcast(F32), ALU.subtract).then_inc(setup_lo, 1)
            dve.wait_ge(small_in, 16 * 5)
            nc.vector.tensor_scalar(consts[:, 3, 0:1], consts[:, 3, 0:1], 0.5 * float(D) ** 0.5, None, ALU.mult)\
                .then_inc(norm_set, 1)
            dve.wait_ge(first_sb, 2 * B + 1)
            bflat = beta[:, :, :].rearrange("p t h -> p (t h)")
            nc.vector.tensor_scalar(bflat, bflat, 1.0, None, ALU.add).then_inc(beta_step, 1)
            dve.wait_ge(beta_step, 1)
            for t in range(NT):
                nc.vector.reciprocal(beta[:, t, :], beta[:, t, :]).then_inc(beta_step, 1)
            dve.wait_ge(mask_ready, 3 + 2 * IN_CHUNK)
            dve.wait_ge(const_ready, 4)

            for s in slots(dve, H, B):
                u1, u2, u3, u4 = s.u1, s.u2, s.u3, s.u4
                if u1 and s.j == 0:
                    wait(dve, conv_step, u1.count(12, -3))
                    wait(dve, tap_done, u1.count(4, -1))
                    nc.vector.tensor_copy(coef[:, :, :], coefs[:, :, bass.ds(u1.h, 1), :].rearrange("p i o w -> p i (o w)"))\
                        .then_inc(coef_set, 1)
                if u3:
                    dve.wait_ge(s_ps_ready, u3.count(1, 1))
                    wait(dve, a_done, u3.count(4, 0))
                    nc.vector.reduce_max(mx[:, 0, :], work_ps[:, 1, :].rearrange("p (c m) -> p c m", c=C), AX_X)\
                        .then_inc(max_step, 1)
                    dve.wait_ge(max_step, u3.count(2, 1))
                    nc.vector.tensor_scalar(mx[:, 1, :], mx[:, 0, :], -SCALE / 4, None, ALU.mult).then_inc(max_step, 1)
                for lev in range(LEVELS - 1):
                    if u2:
                        grow_U(dve, u2, lev)
                        if lev + 2 < LEVELS - 1:
                            gate_products(dve, u2, lev + 2)
                    if u2 and lev in V_TAPS:
                        conv_tap(dve, u2, 3, V_TAPS.index(lev))
                if u1 and s.j == 0:
                    dve.wait_ge(coef_set, u1.h + 1)
                if u1:
                    conv_tap(dve, u1, 0, 0)
                    conv_tap(dve, u1, 0, 1)
                    conv_tap(dve, u1, 0, 2)
                if u1 and s.j == 0:
                    nc.vector.tensor_copy(coef_v[:, :], coefs[:, 0, bass.ds(u1.h, 1), :].rearrange("p o w -> p (o w)"))\
                        .then_inc(coef_v_set, 1)
                for r in range(LEVELS):
                    if u3 and r < IN_CHUNK:
                        mixable(dve, s, r)
                    if u3 and r == LEVELS - 1:
                        own_mixable(dve, s)
                    if u2:
                        descend(dve, u2, r)
                    if u3 and r < IN_CHUNK:
                        mix(dve, r)
                    if u2 and r == 0:
                        silu(dve, u2, 3)
                    if u1 and r == 0:
                        gates(dve, u1, 0)
                        gates(dve, u1, 1)
                    if u1 and r == 1:
                        gates(dve, u1, 2)
                    if u1 and r == 2:
                        silu(dve, u1, 0)
                    if u2 and r == 2:
                        values(dve, u2)
                    if u1 and r == 2:
                        conv_tap(dve, u1, 1, 0)
                    if u1 and r == 3:
                        conv_tap(dve, u1, 1, 1)
                        conv_tap(dve, u1, 1, 2)
                    if u4 and r == 4:
                        dve.wait_ge(tg_done, u4.count(1, 1))
                        dve.wait_ge(onT_ps_ready, u4.count(1, 1))
                        wait(dve, y_ps_ready, u4.count(2, 0))
                        nc.vector.scalar_tensor_tensor(tg[:, :], tg[:, :], 1.0, work_ps[:, 1, :], ALU.add, ALU.mult)\
                            .then_inc(og_done, 1)
                    if u1 and r == 4:
                        gates(dve, u1, 3)
                    if u1 and r == 5:
                        gates(dve, u1, 4)
                    if u1 and r == 6:
                        conv_tap(dve, u1, 2, 0)
                    if u1 and r == 7:
                        conv_tap(dve, u1, 2, 1)
                    if u2 and r >= 7:
                        scores_end(dve, u2, r - 7)
                if u1:
                    conv_tap(dve, u1, 2, 2)
                if u3:
                    mix_own(dve)
                if u1:
                    gate_products(dve, u1, 1)

            dve.wait_ge(acc_done, 2 * B * H)
            dve.wait_ge(ffn["scale_in"], 48)
            nc.vector.tensor_tensor(sgu[:, :], sg_sb[:, :], su_sb[:, :], ALU.mult).then_inc(ffn["scales"], 1)
            nc.vector.tensor_scalar(sg_sb[:, :], sg_sb[:, :], 0.5, None, ALU.mult).then_inc(ffn["scales"], 1)
            nc.vector.memset(tick[:, :], 0.0).then_inc(ffn["scaled"], C)
            for b in range(B + 2):
                if b < B:
                    attention_stats(dve, b)
                if 1 <= b <= B:
                    attention_norm(dve, b - 1)
                if b >= 2:
                    lows(dve, b - 2)
            with dve.Fori(0, B) as b:
                for f in range(FT):
                    dve.wait_ge(ffn["tanh"], b * FT + (f + 1))
                    m = gate_mid[:, f % 2, :]
                    nc.vector.scalar_tensor_tensor(m, gate_th[:, f % 2, :], 1.0, ffn_gate_ps(f), ALU.add, ALU.mult)\
                        .then_inc(ffn["mid"], 1)
                    dve.wait_ge(ffn["mid"], b * FT + (f + 1))
                    dve.wait_ge(ffn["up_ps"], b * 2 * FT + (2 * f + 2))
                    if f >= 4:
                        dve.wait_ge(ffn["fused_lo"], b * FT + (f - 3))
                    nc.vector.scalar_tensor_tensor(fused[:, f % 4, :], m, sgu[:, f:f + 1], ffn_up_ps(f), ALU.mult, ALU.mult)\
                        .then_inc(ffn["fused"], 1)
                for c in range(C):
                    dve.wait_ge(ffn["down_ps"], b * FT + FT)
                    a = acc[:, bass.ds(b * C + c, 1), :].rearrange("p o n -> p (o n)")
                    nc.vector.scalar_tensor_tensor(a, down_ps(c), 0.5, sd_sb[:, :], ALU.mult, ALU.mult)\
                        .then_inc(ffn["scaled"], 1)
                for c in range(C):
                    a = acc[:, bass.ds(b * C + c, 1), :].rearrange("p o n -> p (o n)")
                    dve.wait_ge(ffn["scaled"], b * C + (C + c + 1))
                    nc.vector.tensor_tensor(a, a, y[:, bass.ds(b * C + c, 1), :].rearrange("p o n -> p (o n)"), ALU.add)\
                        .then_inc(ffn["res"], 1)
                layer_norm(dve, b)

        @block.tensor
        def _(pe):
            mm, tr = nc.tensor.matmul, nc.tensor.transpose
            pe.wait_ge(x_in, 16)
            pe.wait_ge(mask_ready, 3)
            for g in range(NT * KT // 4):
                k, q = g // (NT // 4), g % (NT // 4)
                if g >= 2:
                    pe.wait_ge(xT_lo, g - 1)
                for c in range(4):
                    last = tr(work_ps[:, g % 2, c * P:(c + 1) * P], acc[:, 4 * q + c, k * P:(k + 1) * P], ident[:, :])
                last.then_inc(xT_ps, 1)
            pe.wait_ge(xT_lo, NT * KT // 4)
            pe.wait_ge(setup_lo, 1)
            high, low = setup_weights(setup_hi_sb), setup_weights(setup_lo_sb)
            for b in range(B):
                for i in range(2):
                    if b:
                        pe.wait_ge(first_sb, 2 * b + i - 1)
                    cols = slice(b * T, (b + 1) * T)
                    split_product(proj_ps[:, i, :], high[i], low[i], lambda k: hT_hi[:, k, cols],
                                  lambda k: hT_lo[:, k, cols]).then_inc(first_ps, 1)
            for t in range(NT):
                cols = slice(t * P, (t + 1) * P)
                parts = [(hT_hi, high[2]), (hT_lo, high[2]), (hT_hi, low[2])]
                for k in range(KT):
                    for n, (x_, w) in enumerate(parts):
                        last = mm(work_ps[:, 0, t * H:(t + 1) * H], x_[:, k, cols], w[:, k, :],
                                  start=(k == 0 and n == 0), stop=(k == KT - 1 and n == 2))
            last.then_inc(first_ps, 1)
            pe.wait_ge(first_sb, 2 * B + 1)

            for s in slots(pe, H, B):
                u1, u2, u3, u4 = s.u1, s.u2, s.u3, s.u4
                if s.edge:
                    done = [min(max(s.n - lag, 0), B * H) for lag in range(4)]
                    for sem_, per, left, lag in ((conv_step, 12, 3, 0), (fexp_done, 1, 0, 0), (wN_step, 5, 0, 0),
                                                 (vN_done, 1, 0, 1), (A_done, 4, 0, 1), (UT_done, 8, 0, 1),
                                                 (V_step, 18, 0, 1), (aT_done, 1, 0, 2), (mix_done, 8, 0, 2), (far_done, 3, 0, 2),
                                                 (oN_done, 1, 0, 3), (og_done, 1, 0, 3), (y_done, 2, 0, 3),
                                                 (tg_done, 1, 0, 3)):
                        wait(pe, sem_, per * done[lag] - left)
                if u4:
                    pe.wait_ge(mix_done, u4.count(8, 8))
                    pe.wait_ge(far_done, u4.count(3, 3))
                    pe.wait_ge(vN_done, u4.count(1, 1))
                    wait(pe, y_done, u4.count(2, 0))
                    for t in range(C):
                        for c in range(t + 1):
                            last = mm(work_ps[:, 0, t * P:(t + 1) * P], A2[:, c, t * P:(t + 1) * P],
                                      vN[:, u4.par % 2, c * P:(c + 1) * P], start=(c == 0), stop=(c == t))
                    last.then_inc(o_ps_ready, 1)
                if u2:
                    pe.wait_ge(low_done, 2 * u2.h + 2)
                    pe.wait_ge(conv_step, u2.count(12, 9))
                    project(u2, 3)
                if u3:
                    pe.wait_ge(a_done, u3.count(4, 4))
                    turn(1, aN).then_inc(aT_ps_ready, 1)
                if u2:
                    pe.wait_ge(qk_left, u2.count(3, 2))
                    if u4:
                        pe.wait_ge(oN_done, u4.count(1, 1))
                    key_query(pe, u2, 0)
                if u1:
                    pe.wait_ge(low_done, 2 * u1.h + 1)
                    if u4:
                        pe.wait_ge(tg_done, u4.count(1, 1))
                    project(u1, 0)
                if u2:
                    pe.wait_ge(A_done, u2.count(4, 1))
                    pe.wait_ge(qk_left, u2.count(3, 3))
                    key_query(pe, u2, 1)
                    if u3:
                        pe.wait_ge(aT_done, u3.count(1, 1))
                    key_query(pe, u2, 2)
                if u3:
                    mix_products(pe, u3, 0)
                if u2:
                    turn_U(pe, u2, 0)
                if u2:
                    pe.wait_ge(A_done, u2.count(4, 2))
                    key_query(pe, u2, 3)
                if u1:
                    pe.wait_ge(head_f, 16 * (u1.h + 1))
                    wait(pe, conv_step, u1.count(12, 0))
                    nc.tensor.matmul(proj_ps[:, 1, :], wf2_head[:, :], f1T[:, u1.par * T:(u1.par + 1) * T], start=True,
                                     stop=True).then_inc(proj_ps_ready, 1)
                if u2:
                    turn_U(pe, u2, 1)
                for r in range(LEVELS):
                    if u2:
                        level_scores(pe, u2, r)
                        if r + 2 < LEVELS - 1:
                            turn_U(pe, u2, r + 2)
                    if u4 and r in (6, 7):
                        if r == 6:
                            pe.wait_ge(og_left, u4.count(1, 1))
                            pe.wait_ge(wo_left, u4.h + 1)
                            if u1:
                                pe.wait_ge(wN_step, u1.count(5, 5))
                        for c in range(2):
                            t0 = (2 * (r - 6) + c) * P
                            for n, (o, w) in enumerate(((tg_hi, wo_hi), (tg_hi, wo_lo), (tg_lo, wo_hi))):
                                last = mm(work_ps[:, r - 6, c * HID:(c + 1) * HID], o[:, t0:t0 + P], w[:, :],
                                          start=(n == 0), stop=(n == 2))
                        last.then_inc(y_ps_ready, 1)
                    if u3:
                        mix_products(pe, u3, r + 1)
                    if u2 and r == 2:
                        pe.wait_ge(silu_done, u2.count(2, 2))
                        pe.wait_ge(A_done, u2.count(4, 3))
                        turn(1, conv[:, 2, :]).then_inc(vT_ps_ready, 1)
                    if u1 and r == 1:
                        pe.wait_ge(conv_step, u1.count(12, 3))
                        project(u1, 1)
                    if u1 and r == 3:
                        pe.wait_ge(silu_done, u1.count(2, 1))
                        if u2:
                            pe.wait_ge(A_done, u2.count(4, 4))
                        turn(0, wT[:, u1.par % 2, :]).then_inc(wT_ps_ready, 1)
                    if u4 and r == 3:
                        pe.wait_ge(on_done, u4.count(4, 4))
                        if u2:
                            pe.wait_ge(vN_done, u2.count(1, 1))
                        turn(1, oN).then_inc(onT_ps_ready, 1)
                    if u1 and r == 4:
                        pe.wait_ge(fexp_done, u1.count(1, 1))
                        project(u1, 2)
                if u3:
                    pe.wait_ge(head_g, 16 * (u3.h + 1))
                    if u1:
                        pe.wait_ge(conv_step, u1.count(12, 6))
                    elif u4:
                        pe.wait_ge(tg_done, u4.count(1, 1))
                    mm(proj_ps[:, 0, :], wg2_head[:, :], g1T[:, u3.par * T:(u3.par + 1) * T], start=True, stop=True)\
                        .then_inc(gate_ps_ready, 1)
                if u2:
                    pe.wait_ge(sT_done, u2.count(2, 2))
                    pe.wait_ge(Alev_done, u2.count(8, 8))
                    if u4:
                        pe.wait_ge(y_done, u4.count(2, 2))
                    else:
                        pe.wait_ge(vN_done, u2.count(1, 1))
                    for c in range(C):
                        mm(work_ps[:, 1, c * P:(c + 1) * P], V[:, c * P:(c + 1) * P], ident[:, :], is_transpose=True,
                           start=True, stop=False)
                        last = mm(work_ps[:, 1, c * P:(c + 1) * P], A_diag[:, c, :],
                                  wN[:, u2.par % 2, c * P:(c + 1) * P], start=False, stop=True)
                    last.then_inc(s_ps_ready, 1)

            for b in range(B):
                pe.wait_ge(ffn["norm"], b * C + C)
                if b:
                    pe.wait_ge(ffn["yT_lo"], b * KT)
                for k in range(KT):
                    for c in range(C):
                        last = tr(work_ps[:, k, c * P:(c + 1) * P], y[:, b * C + c, k * P:(k + 1) * P], ident[:, :])
                    last.then_inc(ffn["yT_ps"], 1)
            pe.wait_ge(ffn["cast"], 3)
            pe.wait_ge(ffn["yT_lo"], B * KT)

            def down(b, f):
                pe.wait_ge(ffn["fused_lo"], b * FT + (f + 1))
                if f == 0:
                    pe.wait_ge(ffn["scaled"], b * C + C)
                for c in range(C):
                    for part in (fused_hi, fused_lo):
                        last = mm(down_ps(c), part[:, f % 4, c * P:(c + 1) * P], wd_r[:, f, :],
                                  start=(f == 0 and part is fused_hi), stop=(f == FT - 1 and part is fused_lo))
                last.then_inc(ffn["down_ps"], 1)

            with pe.Fori(0, B) as b:
                for f in range(FT):
                    if f >= 2:
                        pe.wait_ge(ffn["fused"], b * FT + (f - 1))
                    for w, dst in ((wg_r, ffn_gate_ps(f)), (wu_r, ffn_up_ps(f))):
                        for k in range(KT):
                            for part in (yT_hi, yT_lo):
                                last = mm(dst, w[:, k, f * P:(f + 1) * P], part[:, k, bass.ts(b, T)],
                                          start=(k == 0 and part is yT_hi), stop=(k == KT - 1 and part is yT_lo))
                        last.then_inc(ffn["up_ps"], 1)
                    if f >= 2:
                        down(b, f - 2)
                down(b, FT - 2)
                down(b, FT - 1)

_INS = ["hidden_states", "Wq", "Wk", "Wv", "Ww", "cq", "ck", "cv", "Wf1", "Wf2", "Wb", "Wg1", "Wg2", "bg2", "norm_w",
        "Wo"]
_FFN = ["w_gate", "w_up", "w_down", "s_gate", "s_up", "s_down"]


def kernel(**inputs):
    import numpy as np
    import concourse.bacc as bacc
    from concourse.bass_utils import run_bass_kernel_spmd

    nc = bacc.Bacc("TRN2", target_bir_lowering=False, num_devices=1)
    arrays, args = {}, []
    for name in ["L0_attn_" + n for n in _INS] + ["L0_ffn_" + n for n in _FFN]:
        a = np.ascontiguousarray(inputs[name])
        if a.dtype == np.int8:
            a = a.view(np.int32)
        arrays["in_" + name] = a
        args.append(nc.dram_tensor("in_" + name, a.shape, mybir.dt.from_np(a.dtype), kind="ExternalInput").ap())
    shape = inputs["L0_attn_hidden_states"].shape
    out = nc.dram_tensor("out_x", shape, F32, kind="ExternalOutput").ap()
    build(nc, *args, out)
    r = run_bass_kernel_spmd(nc, [arrays], core_ids=[0])
    return r.results[0]["out_x"]
```
